# Optimizing a Trainium2 kernel written in Bass

```python
import numpy as np
import jax
import jax.numpy as jnp

def _softmax(x, axis=-1):
    return jax.nn.softmax(x, axis=axis)

def _gelu(x):
    return jax.nn.gelu(x, approximate=True)

def _silu(x):
    return jax.nn.silu(x)

def _sigmoid(x):
    return jax.nn.sigmoid(x)

def _layernorm(x, axis=-1, eps=1e-05):
    m = jnp.mean(x, axis=axis, keepdims=True)
    v = jnp.var(x, axis=axis, keepdims=True)
    return (x - m) / jnp.sqrt(v + eps)

def _scatter_add(tgt, idx, src, axis=0):
    return tgt.at[idx].add(src)

def _segment_sum(src, seg, n):
    return jax.ops.segment_sum(src, seg, n)
kernel_name = 'mk_lm_tower_d2_tok_ids256_r4_13b78b'

def setup_inputs(seed: int=0):
    np.random.seed(seed)
    _w = jnp.asarray

    def _rec_inputs():
        import jax
        import jax.numpy as jnp
        _rk = jax.random.key(seed)
        x = jax.random.randint(jax.random.fold_in(_rk, 1), (16, 512), 0, 4360, jnp.int32)
        return x
    x = _rec_inputs()

    def _L0_tok_setup():
        import jax, jax.numpy as jnp
        import numpy as np
        VOCAB = 4360
        PROJ = 64
        PAD_IDX = 0
        key = jax.random.key(seed)
        k1, k2 = jax.random.split(key)
        x = jax.random.randint(k1, (64, 512), 0, VOCAB, dtype=jnp.int64)
        W = jax.random.normal(k2, (PROJ, VOCAB), dtype=jnp.float32) * 0.02
        return {'x': x, 'W': W}
    _L0_tok_all = _L0_tok_setup()
    _L0_tok_in = {k: v for k, v in _L0_tok_all.items() if k in ('W',)}
    del _L0_tok_all

    def _L0_attn_setup():
        import jax, jax.numpy as jnp
        import numpy as np
        import math
        DIM = 64
        key = jax.random.key(seed)
        kx, kq, kk, kv = jax.random.split(key, 4)
        B, N, D = (2, 2048, DIM)
        x = jax.random.normal(kx, (B, N, D), dtype=jnp.float32)
        s = 1.0 / math.sqrt(D)
        Wq = jax.random.uniform(kq, (D, D), dtype=jnp.float32, minval=-s, maxval=s)
        Wk = jax.random.uniform(kk, (D, D), dtype=jnp.float32, minval=-s, maxval=s)
        Wv = jax.random.uniform(kv, (D, D), dtype=jnp.float32, minval=-s, maxval=s)
        return {'x': x, 'Wq': Wq, 'Wk': Wk, 'Wv': Wv}
    _L0_attn_all = _L0_attn_setup()
    _L0_attn_in = {k: v for k, v in _L0_attn_all.items() if k in ('Wq', 'Wk', 'Wv')}
    del _L0_attn_all

    def _L0_ffn_setup():
        import math
        import jax, jax.numpy as jnp
        import numpy as np
        CAPACITY_FACTOR = 1.25
        TOP_K = 2
        LN_EPS = 1e-05

        def _layer_norm(x, gamma, beta):
            mu = jnp.mean(x, axis=-1, keepdims=True)
            var = jnp.var(x, axis=-1, keepdims=True)
            return (x - mu) * jax.lax.rsqrt(var + LN_EPS) * gamma + beta
        key = jax.random.key(seed)
        ks = jax.random.split(key, 4)
        B, S, D, F, E = (8, 1024, 64, 128, 8)
        x = jax.random.normal(ks[0], (B, S, D), dtype=jnp.float32)
        Wr = jax.random.normal(ks[1], (D, E), dtype=jnp.float32) / np.sqrt(D)
        br = jnp.zeros((E,), jnp.float32)
        W1 = jax.random.normal(ks[2], (E, D, F), dtype=jnp.float32) / np.sqrt(D)
        b1 = jnp.zeros((E, F), jnp.float32)
        W2 = jax.random.normal(ks[3], (E, F, D), dtype=jnp.float32) / np.sqrt(F)
        b2 = jnp.zeros((E, D), jnp.float32)
        gamma = jnp.ones((D,), jnp.float32)
        beta = jnp.zeros((D,), jnp.float32)
        return {'x': x, 'Wr': Wr, 'br': br, 'W1': W1, 'b1': b1, 'W2': W2, 'b2': b2, 'gamma': gamma, 'beta': beta}
    _L0_ffn_all = _L0_ffn_setup()
    _L0_ffn_in = {k: v for k, v in _L0_ffn_all.items() if k in ('Wr', 'br', 'W1', 'b1', 'W2', 'b2', 'gamma', 'beta')}
    del _L0_ffn_all

    def _L1_attn_setup():
        import jax, jax.numpy as jnp
        import numpy as np
        B, N, DIM = (4, 512, 64)
        H, HD, M = (8, 32, 4)
        SPARSE_TOPK = 32
        key = jax.random.key(seed)
        ks = jax.random.split(key, 6)
        x = jax.random.normal(ks[0], (B, N, DIM), dtype=jnp.float32)
        w_qkv = jax.random.normal(ks[1], (DIM, 3 * H * HD), dtype=jnp.float32) * 0.02
        b_qkv = jnp.zeros((3 * H * HD,), dtype=jnp.float32)
        w_proj = jax.random.normal(ks[2], (H * HD, DIM), dtype=jnp.float32) * 0.02
        b_proj = jnp.zeros((DIM,), dtype=jnp.float32)
        scale = jnp.ones((1, H, 1, 1), dtype=jnp.float32)
        mem_k = jax.random.normal(ks[3], (H, M, HD), dtype=jnp.float32)
        mem_v = jax.random.normal(ks[4], (H, M, HD), dtype=jnp.float32)
        return {'x': x, 'w_qkv': w_qkv, 'b_qkv': b_qkv, 'w_proj': w_proj, 'b_proj': b_proj, 'scale': scale, 'mem_k': mem_k, 'mem_v': mem_v}
    _L1_attn_all = _L1_attn_setup()
    _L1_attn_in = {k: v for k, v in _L1_attn_all.items() if k in ('w_qkv', 'b_qkv', 'w_proj', 'b_proj', 'scale', 'mem_k', 'mem_v')}
    del _L1_attn_all

    def _L1_ffn_setup():
        import jax, jax.numpy as jnp
        import numpy as np
        B, T, IN_DIM = (64, 64, 64)
        HID, OUT_DIM = (128, 64)
        N_LAYERS, N_EXPERTS, N_SHARED = (2, 16, 1)
        key = jax.random.key(seed)
        ks = jax.random.split(key, 10)
        s = 0.02
        x = jax.random.normal(ks[0], (B, T, IN_DIM), dtype=jnp.float32)
        route_id = jax.random.randint(ks[1], (B,), 0, N_EXPERTS)
        Wi = jax.random.normal(ks[2], (HID, IN_DIM), dtype=jnp.float32) * s
        bi = jnp.zeros((HID,), dtype=jnp.float32)
        Wr = jax.random.normal(ks[3], (N_LAYERS, N_EXPERTS, HID, HID), dtype=jnp.float32) * s
        br = jax.random.normal(ks[4], (N_LAYERS, N_EXPERTS, HID), dtype=jnp.float32) * s
        Ws = jax.random.normal(ks[5], (N_LAYERS, N_SHARED, HID, HID), dtype=jnp.float32) * s
        bs = jax.random.normal(ks[6], (N_LAYERS, N_SHARED, HID), dtype=jnp.float32) * s
        Wo = jax.random.normal(ks[7], (OUT_DIM, HID), dtype=jnp.float32) * s
        bo = jnp.zeros((OUT_DIM,), dtype=jnp.float32)
        return {'x': x, 'route_id': route_id, 'Wi': Wi, 'bi': bi, 'Wr': Wr, 'br': br, 'Ws': Ws, 'bs': bs, 'Wo': Wo, 'bo': bo}
    _L1_ffn_all = _L1_ffn_setup()
    _L1_ffn_in = {k: v for k, v in _L1_ffn_all.items() if k in ('route_id', 'Wi', 'bi', 'Wr', 'br', 'Ws', 'bs', 'Wo', 'bo')}
    del _L1_ffn_all
    return {'x': x, 'L0_tok_W': _L0_tok_in['W'], 'L0_attn_Wq': _L0_attn_in['Wq'], 'L0_attn_Wk': _L0_attn_in['Wk'], 'L0_attn_Wv': _L0_attn_in['Wv'], 'L0_ffn_Wr': _L0_ffn_in['Wr'], 'L0_ffn_br': _L0_ffn_in['br'], 'L0_ffn_W1': _L0_ffn_in['W1'], 'L0_ffn_b1': _L0_ffn_in['b1'], 'L0_ffn_W2': _L0_ffn_in['W2'], 'L0_ffn_b2': _L0_ffn_in['b2'], 'L0_ffn_gamma': _L0_ffn_in['gamma'], 'L0_ffn_beta': _L0_ffn_in['beta'], 'L1_attn_w_qkv': _L1_attn_in['w_qkv'], 'L1_attn_b_qkv': _L1_attn_in['b_qkv'], 'L1_attn_w_proj': _L1_attn_in['w_proj'], 'L1_attn_b_proj': _L1_attn_in['b_proj'], 'L1_attn_scale': _L1_attn_in['scale'], 'L1_attn_mem_k': _L1_attn_in['mem_k'], 'L1_attn_mem_v': _L1_attn_in['mem_v'], 'L1_ffn_route_id': _L1_ffn_in['route_id'], 'L1_ffn_Wi': _L1_ffn_in['Wi'], 'L1_ffn_bi': _L1_ffn_in['bi'], 'L1_ffn_Wr': _L1_ffn_in['Wr'], 'L1_ffn_br': _L1_ffn_in['br'], 'L1_ffn_Ws': _L1_ffn_in['Ws'], 'L1_ffn_bs': _L1_ffn_in['bs'], 'L1_ffn_Wo': _L1_ffn_in['Wo'], 'L1_ffn_bo': _L1_ffn_in['bo']}

def reference(x, L0_tok_W, L0_attn_Wq, L0_attn_Wk, L0_attn_Wv, L0_ffn_Wr, L0_ffn_br, L0_ffn_W1, L0_ffn_b1, L0_ffn_W2, L0_ffn_b2, L0_ffn_gamma, L0_ffn_beta, L1_attn_w_qkv, L1_attn_b_qkv, L1_attn_w_proj, L1_attn_b_proj, L1_attn_scale, L1_attn_mem_k, L1_attn_mem_v, L1_ffn_route_id, L1_ffn_Wi, L1_ffn_bi, L1_ffn_Wr, L1_ffn_br, L1_ffn_Ws, L1_ffn_bs, L1_ffn_Wo, L1_ffn_bo):
    import jax
    import jax.numpy as jnp

    def _L0_tok_ref(x, W):
        import jax, jax.numpy as jnp
        import numpy as np
        VOCAB = 4360
        PROJ = 64
        PAD_IDX = 0
        out = jnp.take(W.T, x, axis=0)
        mask = (x != PAD_IDX)[..., None]
        return jnp.where(mask, out, jnp.zeros((), dtype=out.dtype))

    def _L0_attn_ref(x, Wq, Wk, Wv):
        import jax, jax.numpy as jnp
        import numpy as np
        import math
        DIM = 64
        Q = jnp.einsum('bnd,ed->bne', x, Wq)
        K = jnp.einsum('bnd,ed->bne', x, Wk)
        V = jnp.einsum('bnd,ed->bne', x, Wv)
        D = x.shape[-1]
        scores = jnp.einsum('bqd,bkd->bqk', Q, K) / jnp.sqrt(jnp.float32(D))
        attn = jax.nn.softmax(scores, axis=1)
        out = jnp.einsum('bqk,bkd->bqd', attn, V)
        return out

    def _L0_ffn_ref(x, Wr, br, W1, b1, W2, b2, gamma, beta):
        import math
        import jax, jax.numpy as jnp
        import numpy as np
        CAPACITY_FACTOR = 1.25
        TOP_K = 2
        LN_EPS = 1e-05

        def _layer_norm(x, gamma, beta):
            mu = jnp.mean(x, axis=-1, keepdims=True)
            var = jnp.var(x, axis=-1, keepdims=True)
            return (x - mu) * jax.lax.rsqrt(var + LN_EPS) * gamma + beta
        B, S, D = x.shape
        E = Wr.shape[1]
        N = B * S
        K = TOP_K
        logits = jnp.mean(x, axis=1) @ Wr + br
        routing_weights = jax.nn.softmax(logits, axis=-1)
        capacity = float(math.ceil(N * CAPACITY_FACTOR / E))
        expected_loads = routing_weights.sum(axis=0) * (N / B)
        scale = jnp.where(expected_loads > capacity, capacity / expected_loads, 1.0)
        routing_weights = jax.nn.softmax(routing_weights * scale, axis=-1)
        rw_tok = jnp.broadcast_to(routing_weights[:, None, :], (B, S, E)).reshape(N, E)
        top_w, top_i = jax.lax.top_k(rw_tok, K)
        top_w = jax.nn.softmax(top_w, axis=-1)
        xf = x.reshape(N, D)
        h = jax.nn.gelu(jnp.einsum('nd,edf->enf', xf, W1) + b1[:, None, :], approximate=False)
        y = jnp.einsum('enf,efd->end', h, W2) + b2[:, None, :]
        w_dense = jnp.zeros((N, E), x.dtype).at[jnp.arange(N)[:, None], top_i].add(top_w)
        out = jnp.einsum('ne,end->nd', w_dense, y).reshape(B, S, D)
        out = _layer_norm(out + x, gamma, beta)
        return out

    def _L1_attn_ref(x, w_qkv, b_qkv, w_proj, b_proj, scale, mem_k, mem_v):
        import jax, jax.numpy as jnp
        import numpy as np
        B, N, DIM = (4, 512, 64)
        H, HD, M = (8, 32, 4)
        SPARSE_TOPK = 32
        b, n, dim = x.shape
        h, m, hd = mem_k.shape
        qkv = (x @ w_qkv + b_qkv).reshape(b, n, 3, h, hd).transpose(2, 0, 3, 1, 4)
        q, k, v = (qkv[0], qkv[1], qkv[2])
        k = jnp.concatenate([k, jnp.broadcast_to(mem_k, (b, h, m, hd))], axis=2)
        v = jnp.concatenate([v, jnp.broadcast_to(mem_v, (b, h, m, hd))], axis=2)
        s = n + m
        scores = jnp.einsum('bhnd,bhsd->bhns', q, k) * hd ** (-0.5) * scale
        neg = -jnp.finfo(scores.dtype).max
        diag = jnp.arange(n)[:, None] == jnp.arange(s)[None, :]
        scores = jnp.where(diag, neg, scores)
        top = jax.lax.top_k(scores, SPARSE_TOPK)[0]
        vk = top[..., -1:]
        scores = jnp.where(scores < vk, neg, scores)
        attn = jax.nn.softmax(scores, axis=-1)
        out = jnp.einsum('bhns,bhsd->bhnd', attn, v)
        out = out.transpose(0, 2, 1, 3).reshape(b, n, h * hd)
        return out @ w_proj + b_proj

    def _L1_ffn_ref(x, route_id, Wi, bi, Wr, br, Ws, bs, Wo, bo):
        import jax, jax.numpy as jnp
        import numpy as np
        B, T, IN_DIM = (64, 64, 64)
        HID, OUT_DIM = (128, 64)
        N_LAYERS, N_EXPERTS, N_SHARED = (2, 16, 1)
        flat = x.reshape(-1, x.shape[-1])
        n_tok = flat.shape[0]
        route = jnp.repeat(route_id, n_tok // route_id.shape[0])
        h = jax.nn.relu(flat @ Wi.T + bi)
        n_layers, n_experts = (Wr.shape[0], Wr.shape[1])
        for l in range(n_layers):
            shared = (jnp.einsum('nd,shd->snh', h, Ws[l]) + bs[l][:, None, :]).mean(axis=0)
            routed = jnp.zeros_like(h)
            for e in range(n_experts):
                ye = h @ Wr[l, e].T + br[l, e]
                routed = routed + jnp.where((route == e)[:, None], ye, 0.0)
            h = jax.nn.relu(shared + routed + h)
        out = h @ Wo.T + bo
        return out.reshape(*x.shape[:-1], out.shape[-1])
    h = _L0_tok_ref(x, L0_tok_W)
    h = h + _L0_attn_ref(_layernorm(h, axis=-1), L0_attn_Wq, L0_attn_Wk, L0_attn_Wv)
    h = h + _L0_ffn_ref(_layernorm(h, axis=-1), L0_ffn_Wr, L0_ffn_br, L0_ffn_W1, L0_ffn_b1, L0_ffn_W2, L0_ffn_b2, L0_ffn_gamma, L0_ffn_beta)
    h = h + _L1_attn_ref(_layernorm(h, axis=-1), L1_attn_w_qkv, L1_attn_b_qkv, L1_attn_w_proj, L1_attn_b_proj, L1_attn_scale, L1_attn_mem_k, L1_attn_mem_v)
    h = h + _L1_ffn_ref(_layernorm(h, axis=-1), L1_ffn_route_id, L1_ffn_Wi, L1_ffn_bi, L1_ffn_Wr, L1_ffn_br, L1_ffn_Ws, L1_ffn_bs, L1_ffn_Wo, L1_ffn_bo)
    return h

_drawn_inputs = setup_inputs


def setup_inputs(seed=0):
    import zlib

    import numpy as np

    out = dict(_drawn_inputs(seed))
    spreads = {'L0_ffn_br': (0.0, 0.1),
     'L0_ffn_b1': (0.0, 0.1),
     'L0_ffn_b2': (0.0, 0.1),
     'L0_ffn_gamma': (1.0, 0.2),
     'L0_ffn_beta': (0.0, 0.1),
     'L1_attn_b_qkv': (0.0, 0.281),
     'L1_attn_b_proj': (0.0, 0.1),
     'L1_attn_scale': (1.0, 0.6),
     'L1_ffn_bi': (0.0, 0.646),
     'L1_ffn_bo': (0.0, 0.1)}
    factors = {'L1_attn_mem_k': 5.549,
     'L1_attn_mem_v': 4.496,
     'L1_ffn_Wi': 3.11,
     'L1_ffn_Wr': 7.974,
     'L1_ffn_br': 8.0,
     'L1_ffn_Ws': 6.979,
     'L1_ffn_bs': 8.0}
    for name, (base, spread) in spreads.items():
        noise = np.random.default_rng([zlib.crc32(name.encode()), seed]).standard_normal(out[name].shape)
        drawn = base * np.exp(spread * noise) if base else spread * noise
        out[name] = jnp.asarray(drawn.astype(out[name].dtype))
    for name, factor in factors.items():
        out[name] = (out[name] * factor).astype(out[name].dtype)
    return out
```

```python
from contextlib import ExitStack, contextmanager

import concourse.bass as bass
from concourse import mybir

F32 = mybir.dt.float32
I32 = mybir.dt.int32
U32 = mybir.dt.uint32
ALU = mybir.AluOpType
ACT = mybir.ActivationFunctionType
AX = mybir.AxisListType

P = 128
B, S, D = 16, 512, 64
T = S // P
NT = B * T
EPS = 1e-5
E0, F0 = 8, 128
CAPACITY = 1280.0
H, HD, M = 8, 32, 4
SK = S + M
TOPK = 32
R, HID = 16, 128
HV = HD + 1
OW = T * HV
NH = B * H
FILL = -(2.0 ** 64)
STEEP = 2.0 ** 62
REMOVED = -3.0e38
PAIRS = B // 2


def spread(ap, width):
    return ap.unsqueeze(2).to_broadcast([ap.shape[0], ap.shape[1], width])


def tower(nc, a, out):
    ctx = ExitStack()
    with ctx:
        def sb(name, shape, dt=F32):
            return ctx.enter_context(nc.sbuf_tensor(name, shape, dt))

        t = {}
        t["hidden"] = sb("hidden", [P, NT, D])
        t["normed"] = sb("normed", [P, NT, D])
        t["normedT"] = sb("normedT", [D, B * S])
        t["heads"] = sb("heads", [P, NH * OW])
        t["ident"] = sb("ident", [P, P])
        t["ones_row"] = sb("ones_row", [1, P])
        t["minus_half"] = sb("minus_half", [P, T])
        t["token_ids"] = sb("token_ids", [P, NT], I32)
        t["mix_qk"] = sb("mix_qk", [D, D])
        t["wv0T"] = sb("wv0T", [D, D])
        t["token_sums"] = sb("token_sums", [D, B])
        t["w_route"] = sb("w_route", [D, E0])
        t["b_route"] = sb("b_route", [1, E0])
        t["gate_cols"] = sb("gate_cols", [P, 2 * B])
        t["expert_row"] = sb("expert_row", [1, 2 * B], U32)
        t["gamma"] = sb("gamma", [P, D])
        t["beta"] = sb("beta", [P, D])
        t["w_heads"] = sb("w_heads", [D + 1, H, 3 * HD])
        t["mem_kT"] = sb("mem_kT", [HD, H, M])
        t["mem_v"] = sb("mem_v", [M, H, HD])
        t["w_proj"] = sb("w_proj", [P, 2, D])
        t["b_proj"] = sb("b_proj", [1, D])
        t["w_inT"] = sb("w_inT", [D, HID])
        t["b_in"] = sb("b_in", [HID, 1])
        t["w_shared"] = sb("w_shared", [HID, 2, HID])
        t["b_shared"] = sb("b_shared", [HID, 2])
        t["w_outT"] = sb("w_outT", [HID, D])
        t["b_out"] = sb("b_out", [1, D])
        t["route_row"] = sb("route_row", [1, B * T], I32)

        setup(nc, a, t)
        attention0(nc, a, t)
        router(nc, t)
        experts(nc, a, t)
        attention1(nc, t)
        routed_ffn(nc, a, t, out)


@contextmanager
def phase(nc):
    taken = []

    def take(semaphore):
        taken.append(semaphore)
        return semaphore

    with ExitStack() as ctx:
        yield ctx, take
    nc.clear_and_free_semaphores(taken)
    nc.all_engine_barrier()


def setup(nc, a, t):
    with phase(nc) as (ctx, take):
        wq = ctx.enter_context(nc.sbuf_tensor("wq", [D, D], F32))
        wk = ctx.enter_context(nc.sbuf_tensor("wk", [D, D], F32))
        q_scale = ctx.enter_context(nc.sbuf_tensor("q_scale", [D + 1, H], F32))
        ps_mix = ctx.enter_context(nc.psum_tensor("ps_mix", [D, D], F32))
        sem = lambda name: take(nc.alloc_semaphore(name))
        loaded, cleared, made = sem("loaded"), sem("cleared"), sem("made")
        mixed, scaled, copied = sem("mixed"), sem("scaled"), sem("copied")
        block = ctx.enter_context(nc.Block())
        loads = [
            (t["token_ids"][:, :], a["token_ids"]),
            (wq[:, :], a["L0_attn_Wq"]),
            (wk[:, :], a["L0_attn_Wk"]),
            (q_scale[:, :], a["L1_attn_scale"].partition_broadcast(D + 1)),
            (t["wv0T"][:, :], a["wv0T"]),
            (t["w_route"][:, :], a["L0_ffn_Wr"]),
            (t["b_route"][:, :], a["L0_ffn_br"]),
            (t["gamma"][:, :], a["L0_ffn_gamma"].partition_broadcast(P)),
            (t["beta"][:, :], a["L0_ffn_beta"].partition_broadcast(P)),
            (t["w_heads"][0:D, :, :], a["w_heads"]),
            (t["w_heads"][D:D + 1, :, :], a["b_heads"]),
            (t["mem_kT"][:, :, :], a["mem_kT"]),
            (t["mem_v"][:, :, :], a["mem_v"]),
            (t["w_proj"][:, :, :], a["w_proj"]),
            (t["b_proj"][:, :], a["L1_attn_b_proj"]),
            (t["w_inT"][:, :], a["w_inT"]),
            (t["b_in"][:, :], a["b_in"]),
            (t["w_shared"][:, :, :], a["w_shared"]),
            (t["b_shared"][:, :], a["b_shared"]),
            (t["w_outT"][:, :], a["w_outT"]),
            (t["b_out"][:, :], a["L1_ffn_bo"]),
            (t["route_row"][:, :], a["L1_ffn_route_id"]),
        ]

        @block.sync
        def _(sp):
            for dst, src in loads:
                sp.dma_start(dst, src).then_inc(loaded, 16)
            sp.wait_ge(loaded, 16 * len(loads))

        @block.gpsimd
        def _(pool):
            nc.gpsimd.memset(t["ident"][:, :], 0.0).then_inc(cleared, 1)
            nc.gpsimd.memset(t["ones_row"][:, :], 1.0)
            nc.gpsimd.memset(t["minus_half"][:, :], -0.5)
            pool.wait_ge(cleared, 1)
            nc.gpsimd.affine_select(out=t["ident"][:, :], in_=t["ident"][:, :], compare_op=ALU.not_equal,
                                    fill=1.0, base=0, pattern=[[-1, P]], channel_multiplier=1).then_inc(made, 1)
            pool.wait_ge(made, 1)

        @block.tensor
        def _(pe):
            pe.wait_ge(loaded, 16 * len(loads))
            nc.tensor.matmul(ps_mix[:, :], wq[:, :], wk[:, :], start=True, stop=True).then_inc(mixed, 1)

        @block.scalar
        def _(act):
            act.wait_ge(mixed, 1)
            nc.scalar.activation(t["mix_qk"][:, :], ps_mix[:, :], ACT.Copy, scale=D ** -0.5).then_inc(copied, 1)
            act.wait_ge(copied, 1)

        @block.vector
        def _(dve):
            dve.wait_ge(loaded, 16 * len(loads))
            nc.vector.tensor_scalar(q_scale[:, :], q_scale[:, :], HD ** -0.5, None, ALU.mult).then_inc(scaled, 1)
            dve.wait_ge(scaled, 1)
            wq_part = t["w_heads"][:, :, 0:HD]
            nc.vector.tensor_tensor(wq_part, wq_part, spread(q_scale[:, :], HD), ALU.mult).then_inc(scaled, 1)
            dve.wait_ge(made, 1)
            for l in range(2):
                nc.vector.tensor_tensor(t["w_shared"][:, l, :], t["w_shared"][:, l, :], t["ident"][:, :],
                                        ALU.add).then_inc(scaled, 1)
            dve.wait_ge(scaled, 4)


def attention0(nc, a, t):
    with phase(nc) as (ctx, take):
        def sb(name, shape, dt=F32):
            return [ctx.enter_context(nc.sbuf_tensor(f"a_{name}{u}", shape, dt)) for u in range(2)]

        def ps(name, shape):
            return [ctx.enter_context(nc.psum_tensor(f"a_{name}{u}", shape, F32)) for u in range(2)]

        def sem(name):
            return [take(nc.alloc_semaphore(f"a_{name}{u}")) for u in range(2)]

        ids = sb("ids", [P, T], I32)
        gathered_rows = sb("gathered_rows", [P, T, D])
        not_pad = sb("not_pad", [P, T])
        h = sb("h", [P, T, D])
        stats, mean_var = sb("stats", [P, T, 6]), sb("mean_var", [P, T, 2])
        var_eps, rstd = sb("var_eps", [P, T]), sb("rstd", [P, T])
        xn, x2 = sb("xn", [P, T, D]), sb("x2", [P, T, D])
        xT, mixT = sb("xT", [D, S]), sb("mixT", [D, S])
        neg_max, weight_sum, inv_sum = sb("neg_max", [P, T]), sb("weight_sum", [P, T]), sb("inv_sum", [P, T])
        weights = [t["heads"][:, u * T * S:(u + 1) * T * S].rearrange("p (k q) -> p k q", k=T) for u in range(2)]
        values = sb("values", [P, T, D])
        ps_x = ps("ps_x", [D, S])
        ps_vo = ps("ps_vo", [P, S])
        ps_sc = [ps(f"ps_sc{u}_", [P, S]) for u in range(2)]

        ids_ready, gathered, rows_used = sem("ids_ready"), sem("gathered"), sem("rows_used")
        var1, rstd1, xn_ready = sem("var1"), sem("rstd1"), sem("xn_ready")
        xT_ps, xT_sb, mix_ps, mix_sb = sem("xT_ps"), sem("xT_sb"), sem("mix_ps"), sem("mix_sb")
        v_ps, score_ps, max_ready, exp_ready = sem("v_ps"), sem("score_ps"), sem("max_ready"), sem("exp_ready")
        v_ready, o_ps, h_added, h_saved = sem("v_ready"), sem("o_ps"), sem("h_added"), sem("h_saved")
        var2, rstd2, x2_ready, x2_saved = sem("var2"), sem("rstd2"), sem("x2_ready"), sem("x2_saved")
        x2T_ps, x2T_saved = sem("x2T_ps"), sem("x2T_saved")
        chain = take(nc.alloc_semaphore("a_chain"))
        gate = {e: take(nc.alloc_semaphore(f"a_gate_{e}")) for e in ("pool", "act", "dve", "pe")}
        block = ctx.enter_context(nc.Block())

        @block.gpsimd
        def _(pool):
            for u in range(2):
                pool.sem_inc(h_saved[u], 1)
                pool.sem_inc(x2_saved[u], 1)
            with pool.Fori(0, PAIRS) as i:
                for u in range(2):
                    pool.wait_ge(rows_used[u], i + 1)
                    pool.sem_inc(gate["pool"], 1)
                    nc.gpsimd.tensor_copy(ids[u][:, :], t["token_ids"][:, bass.ds(i * (2 * T) + u * T, T)]) \
                        .then_inc(ids_ready[u], 1)
                    pool.wait_ge(ids_ready[u], i + 1)
                    pool.sem_inc(gate["pool"], 1)
                    for j in range(T):
                        nc.gpsimd.indirect_dma_start(
                            out=gathered_rows[u][:, j, :], out_offset=None, in_=a["table"],
                            in_offset=bass.IndirectOffsetOnAxis(ap=ids[u][:, j:j + 1].bitcast(U32), axis=0),
                        ).then_inc(gathered[u], 16)
                for u in range(2):
                    pool.wait_ge(var1[u], i + 1)
                    nc.gpsimd.tensor_tensor(rstd[u][:, :], var_eps[u][:, :], t["minus_half"][:, :], ALU.pow) \
                        .then_inc(rstd1[u], 1)
                for u in range(2):
                    pool.wait_ge(h_added[u], i + 2)
                    pool.sem_inc(gate["pool"], 1)
                    nc.gpsimd.tensor_copy(t["hidden"][:, bass.ds(i * (2 * T) + u * T, T), :], h[u][:, :, :]) \
                        .then_inc(h_saved[u], 1)
                    pool.wait_ge(var2[u], i + 1)
                    nc.gpsimd.tensor_tensor(rstd[u][:, :], var_eps[u][:, :], t["minus_half"][:, :], ALU.pow) \
                        .then_inc(rstd2[u], 1)
                for u in range(2):
                    pool.wait_ge(x2_ready[u], i + 1)
                    pool.sem_inc(gate["pool"], 1)
                    nc.gpsimd.tensor_copy(t["normed"][:, bass.ds(i * (2 * T) + u * T, T), :], x2[u][:, :, :]) \
                        .then_inc(x2_saved[u], 1)

        @block.vector
        def _(dve):
            count = [0]

            def link(ins):
                count[0] += 1
                ins.then_inc(chain, 1)
                dve.wait_ge(chain, count[0])

            def variance(u):
                for j in range(T):
                    last = nc.vector.bn_stats(stats[u][:, j, :], h[u][:, j, :])
                link(last)
                for j in range(T):
                    last = nc.vector.bn_aggr(mean_var[u][:, j, :], stats[u][:, j, :])
                link(last)

            def normalise(dst, u):
                for j in range(T):
                    last = nc.vector.tensor_scalar(dst[u][:, j, :], h[u][:, j, :], mean_var[u][:, j, 0:1],
                                                   rstd[u][:, j:j + 1], ALU.subtract, ALU.mult)
                return last

            for u in range(2):
                dve.sem_inc(rows_used[u], 1)
                dve.sem_inc(h_added[u], 1)
            with dve.Fori(0, PAIRS) as i:
                count[0] = 0
                for u in range(2):
                    dve.wait_ge(gathered[u], i * (16 * T) + 16 * T)
                    dve.sem_inc(gate["dve"], 1)
                    link(nc.vector.tensor_scalar(not_pad[u][:, :], ids[u][:, :], 0.0, None, ALU.not_equal))
                    dve.wait_ge(h_saved[u], i + 1)
                    nc.vector.tensor_tensor(h[u][:, :, :], gathered_rows[u][:, :, :], spread(not_pad[u][:, :], D),
                                            ALU.mult).then_inc(rows_used[u], 1)
                    dve.wait_ge(rows_used[u], i + 2)
                    dve.sem_inc(gate["dve"], 1)
                    variance(u)
                    nc.vector.tensor_scalar(var_eps[u][:, :], mean_var[u][:, :, 1], EPS, None, ALU.add) \
                        .then_inc(var1[u], 1)
                for u in range(2):
                    dve.wait_ge(rstd1[u], i + 1)
                    normalise(xn, u).then_inc(xn_ready[u], 1)
                for k in range(T):
                    for u in range(2):
                        dve.wait_ge(score_ps[u], i * T + k + 1)
                        nc.vector.tensor_reduce(neg_max[u][:, k:k + 1], ps_sc[u][k % 2][:, :], AX.X, ALU.max,
                                                negate=True).then_inc(max_ready[u], 1)
                for u in range(2):
                    dve.wait_ge(exp_ready[u], i * T + T)
                    link(nc.vector.reciprocal(inv_sum[u][:, :], weight_sum[u][:, :]))
                    dve.wait_ge(v_ps[u], i + 1)
                    nc.vector.tensor_tensor(values[u][:, :, :],
                                            ps_vo[u][:, 0:T * D].rearrange("p (k d) -> p k d", k=T),
                                            spread(inv_sum[u][:, :], D), ALU.mult).then_inc(v_ready[u], 1)
                for u in range(2):
                    dve.wait_ge(o_ps[u], i + 1)
                    nc.vector.tensor_tensor(h[u][:, :, :], h[u][:, :, :],
                                            ps_vo[u][:, 0:T * D].rearrange("p (k d) -> p k d", k=T),
                                            ALU.add).then_inc(h_added[u], 1)
                    dve.wait_ge(h_added[u], i + 2)
                    dve.sem_inc(gate["dve"], 1)
                    variance(u)
                    nc.vector.tensor_scalar(var_eps[u][:, :], mean_var[u][:, :, 1], EPS, None, ALU.add) \
                        .then_inc(var2[u], 1)
                for u in range(2):
                    dve.wait_ge(rstd2[u], i + 1)
                    dve.sem_inc(gate["dve"], 1)
                    dve.wait_ge(x2_saved[u], i + 1)
                    normalise(x2, u).then_inc(x2_ready[u], 1)
                dve.sem_clear(chain)

        @block.tensor
        def _(pe):
            def to_features(u, x):
                for j in range(T):
                    last = nc.tensor.transpose(ps_x[u][:, j * P:(j + 1) * P], x[u][:, j, :], t["ident"][:, :])
                return last

            with pe.Fori(0, PAIRS) as i:
                for u in range(2):
                    pe.wait_ge(xn_ready[u], i + 1)
                    pe.wait_ge(x2T_saved[u], i + 1)
                    pe.sem_inc(gate["pe"], 1)
                    to_features(u, xn).then_inc(xT_ps[u], 1)
                for u in range(2):
                    pe.wait_ge(xT_sb[u], i + 1)
                    pe.sem_inc(gate["pe"], 1)
                    nc.tensor.matmul(ps_x[u][:, :], t["mix_qk"][:, :], xT[u][:, :], start=True, stop=True) \
                        .then_inc(mix_ps[u], 1)
                    pe.wait_ge(h_added[u], i + 1)
                    for k in range(T):
                        last = nc.tensor.matmul(ps_vo[u][:, k * D:(k + 1) * D], xT[u][:, k * P:(k + 1) * P],
                                                t["wv0T"][:, :], start=True, stop=True)
                    last.then_inc(v_ps[u], 1)
                for k in range(T):
                    for u in range(2):
                        if k == 0:
                            pe.wait_ge(mix_sb[u], i + 1)
                        if k >= 2:
                            pe.wait_ge(exp_ready[u], i * T + k - 1)
                        nc.tensor.matmul(ps_sc[u][k % 2][:, :], xT[u][:, k * P:(k + 1) * P], mixT[u][:, :],
                                         start=True, stop=True).then_inc(score_ps[u], 1)
                for u in range(2):
                    pe.wait_ge(v_ready[u], i + 1)
                    for j in range(T):
                        for k in range(T):
                            last = nc.tensor.matmul(ps_vo[u][:, j * D:(j + 1) * D],
                                                    weights[u][:, k, j * P:(j + 1) * P], values[u][:, k, :],
                                                    start=(k == 0), stop=(k == T - 1))
                    last.then_inc(o_ps[u], 1)
                for u in range(2):
                    pe.wait_ge(x2_ready[u], i + 1)
                    pe.sem_inc(gate["pe"], 1)
                    to_features(u, x2).then_inc(x2T_ps[u], 1)

        @block.scalar
        def _(act):
            for u in range(2):
                act.sem_inc(x2T_saved[u], 1)
            with act.Fori(0, PAIRS) as i:
                for u in range(2):
                    act.wait_ge(xT_ps[u], i + 1)
                    nc.scalar.activation(xT[u][:, :], ps_x[u][:, :], ACT.Copy).then_inc(xT_sb[u], 1)
                for u in range(2):
                    act.wait_ge(mix_ps[u], i + 1)
                    nc.scalar.activation(mixT[u][:, :], ps_x[u][:, :], ACT.Copy).then_inc(mix_sb[u], 1)
                for k in range(T):
                    for u in range(2):
                        act.wait_ge(max_ready[u], i * T + k + 1)
                        nc.scalar.activation(weights[u][:, k, :], ps_sc[u][k % 2][:, :], ACT.Exp,
                                             bias=neg_max[u][:, k:k + 1], accum_out=weight_sum[u][:, k:k + 1]) \
                            .then_inc(exp_ready[u], 1)
                for u in range(2):
                    act.wait_ge(x2T_ps[u], i + 1)
                    act.sem_inc(gate["act"], 1)
                    nc.scalar.activation(t["normedT"][:, bass.ds(i * (2 * S) + u * S, S)], ps_x[u][:, :], ACT.Copy,
                                         accum_out=t["token_sums"][:, bass.ds(i * 2 + u, 1)]) \
                        .then_inc(x2T_saved[u], 1)


def router(nc, t):
    with phase(nc) as (ctx, take):
        def sb(name, shape, dt=F32):
            return ctx.enter_context(nc.sbuf_tensor("r_" + name, shape, dt))

        means = sb("means", [D, B])
        load_rows = sb("load_rows", [B, B])
        top, neg_top, total, inv = sb("top", [B, 1]), sb("neg_top", [B, 1]), sb("total", [B, 1]), sb("inv", [B, 1])
        probs, shrink = sb("probs", [B, E0]), sb("shrink", [B, E0])
        best, best_at = sb("best", [B, 8]), sb("best_at", [B, 8], U32)
        pair = sb("pair", [B, 2])
        gate_row = sb("gate_row", [1, 2 * B])
        ps_logits = ctx.enter_context(nc.psum_tensor("r_logits", [B, E0], F32))
        ps_loads = ctx.enter_context(nc.psum_tensor("r_loads", [B, E0], F32))
        ps_gates = ctx.enter_context(nc.psum_tensor("r_gates", [P, 2 * B], F32))
        sem = lambda name: take(nc.alloc_semaphore("r_" + name))
        means_ready, logits_ps, steps, exps = sem("means_ready"), sem("logits_ps"), sem("steps"), sem("exps")
        probs_ready, loads_ps, pair_ready, rows_in = sem("probs_ready"), sem("loads_ps"), sem("pair_ready"), sem("rows_in")
        max_ready, gates_ps = sem("max_ready"), sem("gates_ps")
        block = ctx.enter_context(nc.Block())

        @block.tensor
        def _(pe):
            pe.wait_ge(means_ready, 1)
            nc.tensor.matmul(ps_logits[:, :], means[:, :], t["w_route"][:, :], start=True, stop=False)
            nc.tensor.matmul(ps_logits[:, :], t["ones_row"][:, 0:B], t["b_route"][:, :], start=False, stop=True) \
                .then_inc(logits_ps, 1)
            pe.wait_ge(probs_ready, 1)
            nc.tensor.matmul(ps_loads[:, :], load_rows[:, :], probs[:, :], start=True, stop=True).then_inc(loads_ps, 1)
            pe.wait_ge(rows_in, 32)
            nc.tensor.matmul(ps_gates[:, :], t["ones_row"][:, :], gate_row[:, :], start=True, stop=True) \
                .then_inc(gates_ps, 1)

        @block.scalar
        def _(act):
            act.wait_ge(max_ready, 1)
            nc.scalar.activation(probs[:, :], ps_logits[:, :], ACT.Exp, bias=neg_top[:, :], accum_out=total[:, :]) \
                .then_inc(exps, 1)
            act.wait_ge(max_ready, 2)
            nc.scalar.activation(probs[:, :], shrink[:, :], ACT.Exp, bias=neg_top[:, :], accum_out=total[:, :]) \
                .then_inc(exps, 1)
            act.wait_ge(max_ready, 3)
            nc.scalar.activation(pair[:, :], best[:, 0:2], ACT.Exp, bias=neg_top[:, :], accum_out=total[:, :]) \
                .then_inc(exps, 1)
            act.wait_ge(gates_ps, 1)
            nc.scalar.activation(t["gate_cols"][:, :], ps_gates[:, :], ACT.Copy).then_inc(exps, 1)
            act.wait_ge(exps, 4)

        @block.vector
        def _(dve):
            count = [0]

            def link(ins):
                count[0] += 1
                ins.then_inc(steps, 1)
                dve.wait_ge(steps, count[0])

            nc.vector.memset(load_rows[:, :], float(S))
            nc.vector.tensor_scalar(means[:, :], t["token_sums"][:, :], 1.0 / S, None, ALU.mult).then_inc(means_ready, 1)
            dve.wait_ge(logits_ps, 1)
            nc.vector.tensor_reduce(neg_top[:, :], ps_logits[:, :], AX.X, ALU.max, negate=True).then_inc(max_ready, 1)
            dve.wait_ge(exps, 1)
            link(nc.vector.reciprocal(inv[:, :], total[:, :]))
            nc.vector.tensor_scalar(probs[:, :], probs[:, :], inv[:, :], None, ALU.mult).then_inc(probs_ready, 1)
            dve.wait_ge(probs_ready, 1)
            dve.wait_ge(loads_ps, 1)
            link(nc.vector.reciprocal(shrink[:, :], ps_loads[:, :]))
            link(nc.vector.tensor_scalar(shrink[:, :], shrink[:, :], CAPACITY, 1.0, ALU.mult, ALU.min))
            link(nc.vector.tensor_tensor(shrink[:, :], shrink[:, :], probs[:, :], ALU.mult))
            nc.vector.tensor_reduce(neg_top[:, :], shrink[:, :], AX.X, ALU.max, negate=True).then_inc(max_ready, 1)
            dve.wait_ge(exps, 2)
            link(nc.vector.reciprocal(inv[:, :], total[:, :]))
            link(nc.vector.tensor_scalar(probs[:, :], probs[:, :], inv[:, :], None, ALU.mult))
            link(nc.vector.max(best[:, :], probs[:, :]))
            link(nc.vector.max_index(best_at[:, :], best[:, :], probs[:, :]))
            nc.vector.tensor_scalar(neg_top[:, :], best[:, 0:1], -1.0, None, ALU.mult).then_inc(max_ready, 1)
            dve.wait_ge(exps, 3)
            link(nc.vector.reciprocal(inv[:, :], total[:, :]))
            nc.vector.tensor_scalar(pair[:, :], pair[:, :], inv[:, :], None, ALU.mult).then_inc(pair_ready, 1)

        @block.sync
        def _(sp):
            sp.wait_ge(pair_ready, 1)
            sp.dma_start(gate_row[:, :].rearrange("a (b k) -> a b k", k=2), pair[:, :]).then_inc(rows_in, 16)
            sp.dma_start(t["expert_row"][:, :].rearrange("a (b k) -> a b k", k=2), best_at[:, 0:2]).then_inc(rows_in, 16)
            sp.wait_ge(rows_in, 32)


def experts(nc, a, t):
    with phase(nc) as (ctx, take):
        def sb(name, shape, dt=F32):
            return [ctx.enter_context(nc.sbuf_tensor(f"e_{name}{u}", shape, dt)) for u in range(2)]

        def ps(name, shape):
            return [ctx.enter_context(nc.psum_tensor(f"e_{name}{u}", shape, F32)) for u in range(2)]

        def sem(name):
            return [take(nc.alloc_semaphore(f"e_{name}{u}")) for u in range(2)]

        w1, w2, b2 = sb("w1", [D, 2, F0]), sb("w2", [F0, 2, D + 1]), sb("b2", [1, 2, D])
        w2g, b2g = sb("w2g", [F0, 2, D]), sb("b2g", [1, 2, D])
        act_h = sb("act_h", [F0, 2, S])
        r, y, h, x3 = sb("r", [P, T, D]), sb("y", [P, T, D]), sb("h", [P, T, D]), sb("x3", [P, T, D])
        stats, mean_var = sb("stats", [P, T, 6]), sb("mean_var", [P, T, 2])
        var_eps, rstd = sb("var_eps", [P, T]), sb("rstd", [P, T])
        ps_h = [ps(f"ps_h{u}_", [F0, S]) for u in range(2)]
        ps_y = ps("ps_y", [P, S])
        ps_x = ps("ps_x", [D, S])
        w_loaded, w2_gated, h_ps, gelu_ready = sem("w_loaded"), sem("w2_gated"), sem("h_ps"), sem("gelu_ready")
        y_ps, var1, rstd1, y_normed, y_step = sem("y_ps"), sem("var1"), sem("rstd1"), sem("y_normed"), sem("y_step")
        h_ready, var2, rstd2, x3_ready = sem("h_ready"), sem("var2"), sem("rstd2"), sem("x3_ready")
        x3T_ps, x3T_saved = sem("x3T_ps"), sem("x3T_saved")
        chain = take(nc.alloc_semaphore("e_chain"))
        gate = {e: take(nc.alloc_semaphore(f"e_gate_{e}")) for e in ("pool", "act", "dve", "pe")}
        block = ctx.enter_context(nc.Block())

        @block.sync
        def _(sp):
            with sp.Fori(0, PAIRS) as i:
                for u in range(2):
                    sp.wait_ge(y_ps[u], i + 1)
                    for k in range(2):
                        e = sp.value_load(t["expert_row"][0:1, bass.ds(i * 4 + 2 * u + k, 1)], min_val=0, max_val=E0 - 1)
                        sp.dma_start(w1[u][:, k, :], a["L0_ffn_W1"][bass.ds(e, 1), :, :].rearrange("e d f -> (e d) f")) \
                            .then_inc(w_loaded[u], 16)
                        sp.dma_start(w2[u][:, k, :], a["w2_b1"][bass.ds(e, 1), :, :].rearrange("e f d -> (e f) d")) \
                            .then_inc(w_loaded[u], 16)
                        sp.dma_start(b2[u][:, k, :], a["L0_ffn_b2"][bass.ds(e, 1), :]).then_inc(w_loaded[u], 16)

        @block.tensor
        def _(pe):
            for u in range(2):
                pe.sem_inc(y_ps[u], 1)
            with pe.Fori(0, PAIRS) as i:
                for u in range(2):
                    pe.wait_ge(w_loaded[u], i * 96 + 96)
                    pe.sem_inc(gate["pe"], 1)
                    for k in range(2):
                        nc.tensor.matmul(ps_h[u][k][:, :], w1[u][:, k, :], t["normedT"][:, bass.ds(i * (2 * S) + u * S, S)],
                                         start=True, stop=True).then_inc(h_ps[u], 1)
                for u in range(2):
                    pe.wait_ge(w2_gated[u], i + 1)
                    pe.wait_ge(gelu_ready[u], i * 2 + 2)
                    for j in range(T):
                        for k in range(2):
                            nc.tensor.matmul(ps_y[u][:, j * D:(j + 1) * D], act_h[u][:, k, j * P:(j + 1) * P],
                                             w2g[u][:, k, :], start=(k == 0), stop=False)
                        for k in range(2):
                            last = nc.tensor.matmul(ps_y[u][:, j * D:(j + 1) * D], t["ones_row"][:, :],
                                                    b2g[u][:, k, :], start=False, stop=(k == 1))
                    last.then_inc(y_ps[u], 1)
                for u in range(2):
                    pe.wait_ge(x3_ready[u], i + 1)
                    pe.wait_ge(x3T_saved[u], i + 1)
                    pe.sem_inc(gate["pe"], 1)
                    for j in range(T):
                        last = nc.tensor.transpose(ps_x[u][:, j * P:(j + 1) * P], x3[u][:, j, :], t["ident"][:, :])
                    last.then_inc(x3T_ps[u], 1)

        @block.scalar
        def _(act):
            for u in range(2):
                act.sem_inc(x3T_saved[u], 1)
            with act.Fori(0, PAIRS) as i:
                for u in range(2):
                    for k in range(2):
                        act.wait_ge(h_ps[u], i * 2 + k + 1)
                        nc.scalar.activation(act_h[u][:, k, :], ps_h[u][k][:, :], ACT.Gelu, bias=w2[u][:, k, D:D + 1]) \
                            .then_inc(gelu_ready[u], 1)
                for u in range(2):
                    act.wait_ge(x3T_ps[u], i + 1)
                    act.sem_inc(gate["act"], 1)
                    nc.scalar.activation(t["normedT"][:, bass.ds(i * (2 * S) + u * S, S)], ps_x[u][:, :], ACT.Copy) \
                        .then_inc(x3T_saved[u], 1)

        @block.vector
        def _(dve):
            count = [0]

            def link(ins):
                count[0] += 1
                ins.then_inc(chain, 1)
                dve.wait_ge(chain, count[0])

            def variance(u, x):
                for j in range(T):
                    last = nc.vector.bn_stats(stats[u][:, j, :], x[u][:, j, :])
                link(last)
                for j in range(T):
                    last = nc.vector.bn_aggr(mean_var[u][:, j, :], stats[u][:, j, :])
                link(last)
                return nc.vector.tensor_scalar(var_eps[u][:, :], mean_var[u][:, :, 1], EPS, None, ALU.add)

            def normalise(dst, x, u):
                for j in range(T):
                    last = nc.vector.tensor_scalar(dst[u][:, j, :], x[u][:, j, :], mean_var[u][:, j, 0:1],
                                                   rstd[u][:, j:j + 1], ALU.subtract, ALU.mult)
                return last

            with dve.Fori(0, PAIRS) as i:
                count[0] = 0
                for u in range(2):
                    gates = t["gate_cols"][:, bass.ds(i * 4 + 2 * u, 2)]
                    dve.wait_ge(w_loaded[u], i * 96 + 96)
                    dve.sem_inc(gate["dve"], 1)
                    nc.vector.tensor_tensor(w2g[u][:, :, :], w2[u][:, :, 0:D], spread(gates, D), ALU.mult)
                    nc.vector.tensor_tensor(b2g[u][:, :, :], b2[u][:, :, :],
                                            spread(t["gate_cols"][0:1, bass.ds(i * 4 + 2 * u, 2)], D),
                                            ALU.mult).then_inc(w2_gated[u], 1)
                for u in range(2):
                    dve.wait_ge(y_ps[u], i + 2)
                    dve.sem_inc(gate["dve"], 1)
                    link(nc.vector.tensor_tensor(r[u][:, :, :], ps_y[u][:, 0:T * D].rearrange("p (j d) -> p j d", j=T),
                                                 t["normed"][:, bass.ds(i * (2 * T) + u * T, T), :], ALU.add))
                    variance(u, r).then_inc(var1[u], 1)
                for u in range(2):
                    dve.wait_ge(rstd1[u], i + 1)
                    normalise(y, r, u).then_inc(y_normed[u], 1)
                for u in range(2):
                    dve.wait_ge(h_ready[u], i + 1)
                    variance(u, h).then_inc(var2[u], 1)
                for u in range(2):
                    dve.wait_ge(rstd2[u], i + 1)
                    normalise(x3, h, u).then_inc(x3_ready[u], 1)
                dve.sem_clear(chain)

        @block.gpsimd
        def _(pool):
            with pool.Fori(0, PAIRS) as i:
                for u in range(2):
                    pool.wait_ge(var1[u], i + 1)
                    nc.gpsimd.tensor_tensor(rstd[u][:, :], var_eps[u][:, :], t["minus_half"][:, :], ALU.pow) \
                        .then_inc(rstd1[u], 1)
                for u in range(2):
                    hidden = t["hidden"][:, bass.ds(i * (2 * T) + u * T, T), :]
                    pool.wait_ge(y_normed[u], i + 1)
                    for j in range(T):
                        last = nc.gpsimd.tensor_tensor(y[u][:, j, :], y[u][:, j, :], t["gamma"][:, :], ALU.mult)
                    last.then_inc(y_step[u], 1)
                    pool.wait_ge(y_step[u], i * 2 + 1)
                    for j in range(T):
                        last = nc.gpsimd.tensor_tensor(y[u][:, j, :], y[u][:, j, :], t["beta"][:, :], ALU.add)
                    last.then_inc(y_step[u], 1)
                    pool.wait_ge(y_step[u], i * 2 + 2)
                    pool.sem_inc(gate["pool"], 1)
                    nc.gpsimd.tensor_tensor(h[u][:, :, :], y[u][:, :, :], hidden, ALU.add).then_inc(h_ready[u], 1)
                for u in range(2):
                    pool.wait_ge(var2[u], i + 1)
                    nc.gpsimd.tensor_tensor(rstd[u][:, :], var_eps[u][:, :], t["minus_half"][:, :], ALU.pow) \
                        .then_inc(rstd2[u], 1)
                    pool.wait_ge(h_ready[u], i + 1)
                    pool.sem_inc(gate["pool"], 1)
                    nc.gpsimd.tensor_copy(t["hidden"][:, bass.ds(i * (2 * T) + u * T, T), :], h[u][:, :, :])


def attention1(nc, t):
    with phase(nc) as (ctx, take):
        def sb(name, shape, dt=F32):
            return ctx.enter_context(nc.sbuf_tensor("c_" + name, shape, dt))

        def sb2(name, shape, dt=F32):
            return [sb(f"{name}{u}", shape, dt) for u in range(2)]

        def ps(name, width):
            return ctx.enter_context(nc.psum_tensor("c_" + name, [P, width], F32))

        def sem(name):
            return take(nc.alloc_semaphore("c_" + name))

        w_head = sb2("w_head", [D + 1, 3 * HD])
        x_in = sb2("x_in", [D + 1, S])
        qT, kT = sb2("qT", [HD, S]), sb2("kT", [HD, SK])
        vals = sb2("vals", [P, T + 1, HV])
        scores = sb2("scores", [P, T, SK])
        left = sb2("left", [P, SK])
        largest = sb("largest", [P, T, TOPK])
        shift = sb("shift", [P, T, 2])
        factors = sb("factors", [P, 2])
        masked = sb2("masked", [P, SK])
        expT = sb2("expT", [P, T + 1, P])
        ps_s = [ps(f"ps_s{k}", S) for k in range(2)]
        ps_t = [ps(f"ps_t{k}", 2 * S) for k in range(2)]
        ps_qk = ps("ps_qk", S)
        ps_ov = ps("ps_ov", S)
        V_AT, M_AT = OW, OW + T * HD

        made = sem("made")
        staged = [sem(f"staged{u}") for u in range(2)]
        mem_staged = [sem(f"mem_staged{u}") for u in range(2)]
        qk_ps, qk_copied, v_ps, v_copied = sem("qk_ps"), sem("qk_copied"), sem("v_ps"), sem("v_copied")
        s_ps, s_copied, s_ready, found = sem("s_ps"), sem("s_copied"), sem("s_ready"), sem("found")
        shifts, dropped, subtracted, exps = sem("shifts"), sem("dropped"), sem("subtracted"), sem("exps")
        expT_ps, expT_copied, pv_done = sem("expT_ps"), sem("expT_copied"), sem("pv_done")
        chain = sem("chain")
        gate = {e: sem(f"gate_{e}") for e in ("pool", "act", "dve")}
        head_step = NH - 2
        block = ctx.enter_context(nc.Block())
        STAGED = 16 * 3
        CREDIT = 2 * T

        @block.sync
        def _(sp):
            sp.wait_ge(made, 1)
            def stage(u, sequence, head):
                sp.dma_start(w_head[u][:, :], t["w_heads"][:, bass.ds(head, 1), :].rearrange("p h c -> p (h c)")) \
                    .then_inc(staged[u], 16)
                sp.dma_start(x_in[u][0:D, :], t["normedT"][:, bass.ds(sequence * S, S)]).then_inc(staged[u], 16)
                sp.dma_start(kT[u][:, S:SK], t["mem_kT"][:, bass.ds(head, 1), :].rearrange("p h c -> p (h c)")) \
                    .then_inc(staged[u], 16)

            with sp.Fori(0, B) as b:
                with sp.Fori(0, H // 2) as g:
                    for u in range(2):
                        sp.wait_ge(s_copied, (b * H + g * 2) * T + (u + 1) * T)
                        stage(u, b, g * 2 + u)
                        sp.wait_ge(pv_done, (b * H + g * 2) * T + (u + 1) * T)
                        sp.dma_start(vals[u][0:M, T, 0:HD],
                                     t["mem_v"][:, bass.ds(g * 2 + u, 1), :].rearrange("p h c -> p (h c)")) \
                            .then_inc(mem_staged[u], 16)

        @block.tensor
        def _(pe):
            def project(n, u, turns):
                pe.wait_ge(staged[u], turns * STAGED)
                nc.tensor.matmul(ps_qk[0:2 * HD, :], w_head[u][:, 0:2 * HD], x_in[u][:, :], start=True, stop=True) \
                    .then_inc(qk_ps, 1)

            def project_values(n, u):
                for j in range(T):
                    nc.tensor.matmul(ps_ov[:, V_AT + j * HD:V_AT + (j + 1) * HD], x_in[u][:, j * P:(j + 1) * P],
                                     w_head[u][:, 2 * HD:3 * HD], start=True, stop=True)
                pe.wait_ge(qk_copied, n + 1)
                for j in range(T):
                    last = nc.tensor.matmul(ps_ov[:, M_AT + j * M:M_AT + (j + 1) * M], qT[u][:, j * P:(j + 1) * P],
                                            kT[u][:, S:SK], start=True, stop=True)
                last.then_inc(v_ps, 1)

            def score(n, u, j, first):
                if not (first and j < 2):
                    pe.wait_ge(s_copied, n * T + j - 1 + CREDIT)
                nc.tensor.matmul(ps_s[j % 2][:, :], qT[u][:, j * P:(j + 1) * P], kT[u][:, 0:S], start=True, stop=True) \
                    .then_inc(s_ps, 1)

            def turn_over(n, u, j):
                pe.wait_ge(exps, n * T + j + 1)
                for c in range(T):
                    nc.tensor.transpose(ps_t[j % 2][:, c * P:(c + 1) * P], masked[j % 2][:, c * P:(c + 1) * P],
                                        t["ident"][:, :])
                nc.tensor.transpose(ps_t[j % 2][0:M, S:S + P], masked[j % 2][:, S:SK], t["ident"][:, :]) \
                    .then_inc(expT_ps, 1)

            def apply(n, u, j, turns=None):
                pe.wait_ge(expT_copied, n * T + j + 1)
                if j == 0:
                    pe.wait_ge(v_copied, n + 2)
                    pe.wait_ge(mem_staged[u], turns * 16)
                for c in range(T + 1):
                    last = nc.tensor.matmul(ps_ov[:, j * HV:(j + 1) * HV], expT[j % 2][:, c, :], vals[u][:, c, :],
                                            start=(c == 0), stop=(c == T))
                last.then_inc(pv_done, 1)

            def head(n, u, turns, turns_next, first=False, last=False):
                for j in range(T):
                    if j == 0 and not last:
                        project(n + 1, 1 - u, turns_next)
                    if j and not last:
                        score(n + 1, 1 - u, j, False)
                    if not (first and j == 0):
                        apply(n if j else n - 1, u if j else 1 - u, (j - 1) % T, turns)
                    if j == 0 and not last:
                        project_values(n + 1, 1 - u)
                        score(n + 1, 1 - u, j, False)
                    turn_over(n, u, j)

            pe.wait_ge(made, 1)
            pe.sem_inc(pv_done, CREDIT)
            project(0, 0, 1)
            project_values(0, 0)
            for j in range(T):
                score(0, 0, j, True)
            head(0, 0, 1, 1, first=True)
            with pe.Fori(0, head_step // 2) as i:
                head(i * 2 + 1, 1, i + 1, i + 2)
                head(i * 2 + 2, 0, i + 2, i + 2)
            head(NH - 1, 1, NH // 2, None, last=True)
            apply(NH - 1, 1, T - 1)

        @block.scalar
        def _(act):
            def copy_qk(n, u):
                act.wait_ge(qk_ps, n + 1)
                nc.scalar.activation(qT[u][:, :], ps_qk[0:HD, :], ACT.Copy)
                nc.scalar.activation(kT[u][:, 0:S], ps_qk[HD:2 * HD, :], ACT.Copy).then_inc(qk_copied, 1)

            def copy_values(n, u, outputs_of=None):
                act.wait_ge(v_ps, n + 1)
                if outputs_of is not None:
                    act.sem_inc(gate["act"], 1)
                    nc.scalar.activation(t["heads"][:, bass.ds(outputs_of * OW, OW)], ps_ov[:, 0:OW], ACT.Copy)
                nc.scalar.activation(vals[u][:, 0:T, 0:HD],
                                     ps_ov[:, V_AT:V_AT + T * HD].rearrange("p (j c) -> p j c", j=T), ACT.Copy)
                nc.scalar.activation(scores[u][:, :, S:SK],
                                     ps_ov[:, M_AT:M_AT + T * M].rearrange("p (j c) -> p j c", j=T), ACT.Copy) \
                    .then_inc(v_copied, 1)

            def copy_scores(n, u, j):
                act.wait_ge(s_ps, n * T + j + 1)
                nc.scalar.activation(scores[u][:, j, 0:S], ps_s[j % 2][:, :], ACT.Copy).then_inc(s_copied, 1)

            def drop(n, u, j):
                act.wait_ge(shifts, n * T + j + 1)
                nc.scalar.activation(masked[j % 2][:, :], scores[u][:, j, :], ACT.Relu, scale=-STEEP,
                                     bias=shift[:, j, 1:2]).then_inc(dropped, 1)

            def exponent(n, j):
                act.wait_ge(subtracted, n * T + j + 1)
                nc.scalar.activation(masked[j % 2][:, :], masked[j % 2][:, :], ACT.Exp, bias=shift[:, j, 0:1]) \
                    .then_inc(exps, 1)

            def copy_expT(n, j):
                act.wait_ge(expT_ps, n * T + j + 1)
                nc.scalar.activation(expT[j % 2][:, :, :], ps_t[j % 2][:, 0:(T + 1) * P].rearrange("p (c q) -> p c q", c=T + 1),
                                     ACT.Copy).then_inc(expT_copied, 1)

            def head(n, u, first=False, last=False):
                for j in range(T):
                    drop(n, u, j)
                    if j == 0 and not last:
                        copy_qk(n + 1, 1 - u)
                    if not (first and j == 0):
                        copy_expT(n if j else n - 1, (j - 1) % T)
                    if not last and j:
                        copy_scores(n + 1, 1 - u, j)
                    exponent(n, j)
                    if j == 0 and not last:
                        copy_values(n + 1, 1 - u, None if first else n - 1)
                        copy_scores(n + 1, 1 - u, 0)
                    if j == 0 and last:
                        act.wait_ge(pv_done, NH * T - T + CREDIT)
                        nc.scalar.activation(t["heads"][:, (NH - 2) * OW:(NH - 1) * OW], ps_ov[:, 0:OW], ACT.Copy) \
                            .then_inc(v_copied, 1)

            act.wait_ge(made, 1)
            act.sem_inc(s_copied, CREDIT)
            copy_qk(0, 0)
            copy_values(0, 0)
            for j in range(T):
                copy_scores(0, 0, j)
            head(0, 0, first=True)
            with act.Fori(0, head_step // 2) as i:
                head(i * 2 + 1, 1)
                head(i * 2 + 2, 0)
            head(NH - 1, 1, last=True)
            copy_expT(NH - 1, T - 1)
            act.wait_ge(pv_done, NH * T + CREDIT)
            nc.scalar.activation(t["heads"][:, (NH - 1) * OW:NH * OW], ps_ov[:, 0:OW], ACT.Copy).then_inc(v_copied, 1)
            act.wait_ge(v_copied, NH + 2)

        @block.gpsimd
        def _(pool):
            def exclude_self(n, u, j):
                own = scores[u][:, j, j * P:(j + 1) * P]
                if j == 0:
                    pool.wait_ge(v_copied, n + 1)
                    pool.sem_inc(gate["pool"], 1)
                pool.wait_ge(s_copied, n * T + j + 1 + CREDIT)
                pool.sem_inc(gate["pool"], 1)
                nc.gpsimd.affine_select(out=own, in_=own, compare_op=ALU.not_equal, fill=FILL, base=0,
                                        pattern=[[-1, P]], channel_multiplier=1).then_inc(s_ready, 1)

            def head(n, u, last=False):
                for j in range(T):
                    pool.wait_ge(found, n * T + j + 1)
                    nc.gpsimd.tensor_tensor(shift[:, j, :], largest[:, j, 0:TOPK:TOPK - 1], factors[:, :], ALU.mult) \
                        .then_inc(shifts, 1)
                    pool.wait_ge(dropped, n * T + j + 1)
                    nc.gpsimd.tensor_tensor(masked[j % 2][:, :], scores[u][:, j, :], masked[j % 2][:, :], ALU.subtract) \
                        .then_inc(subtracted, 1)
                    if not last:
                        exclude_self(n + 1, 1 - u, j)

            nc.gpsimd.memset(factors[:, 0:1], -1.0)
            nc.gpsimd.memset(factors[:, 1:2], STEEP).then_inc(gate["pool"], 1)
            pool.wait_ge(gate["pool"], 1)
            for j in range(T):
                exclude_self(0, 0, j)
            head(0, 0)
            with pool.Fori(0, head_step // 2) as i:
                head(i * 2 + 1, 1)
                head(i * 2 + 2, 0)
            head(NH - 1, 1, last=True)

        @block.vector
        def _(dve):
            count = [0]

            def link(ins):
                count[0] += 1
                ins.then_inc(chain, 1)
                dve.wait_ge(chain, count[0])

            def find(n, u, j):
                dve.wait_ge(s_ready, n * T + j + 1)
                dve.sem_inc(gate["dve"], 1)
                source = scores[u][:, j, :]
                for c in range(0, TOPK, 8):
                    eight = largest[:, j, c:c + 8]
                    if c + 8 == TOPK:
                        nc.vector.max(eight, source).then_inc(found, 1)
                        break
                    link(nc.vector.max(eight, source))
                    link(nc.vector.match_replace(left[j % 2][:, :], eight, source, REMOVED))
                    source = left[j % 2][:, :]

            def head(n, u):
                for j in range(T):
                    find(n, u, j)

            for u in range(2):
                nc.vector.memset(x_in[u][D:D + 1, :], 1.0)
                nc.vector.memset(vals[u][:, :, :], 0.0)
                nc.vector.memset(ps_t[u][:, S:S + P], 0.0)
            nc.vector.memset(ps_ov[:, 0:OW], 0.0)
            link(nc.vector.memset(ps_qk[:, :], 0.0))
            for u in range(2):
                last = nc.vector.memset(vals[u][:, 0:T, HD:HV], 1.0)
                last = nc.vector.memset(vals[u][0:M, T, HD:HV], 1.0)
            last.then_inc(made, 1)
            dve.wait_ge(made, 1)
            head(0, 0)
            dve.sem_clear(chain)
            with dve.Fori(0, head_step // 2) as i:
                count[0] = 0
                head(i * 2 + 1, 1)
                head(i * 2 + 2, 0)
                dve.sem_clear(chain)
            count[0] = 0
            head(NH - 1, 1)


def routed_ffn(nc, a, t, out):
    with phase(nc) as (ctx, take):
        def sb(name, shape, dt=F32):
            return [ctx.enter_context(nc.sbuf_tensor(f"d_{name}{u}", shape, dt)) for u in range(2)]

        def ps(name, shape):
            return [ctx.enter_context(nc.psum_tensor(f"d_{name}{u}", shape, F32)) for u in range(2)]

        def sem(name):
            return [take(nc.alloc_semaphore(f"d_{name}{u}")) for u in range(2)]

        w_routed = sb("w_routed", [P, T, 2, HID + 1])
        bias = sb("bias", [P, T, 2])
        inv = sb("inv", [P, H, T])
        attended = sb("attended", [P, T, H * HD])
        attendedT = sb("attendedT", [P, 2, S])
        h, xn, result = sb("h", [P, T, D]), sb("xn", [P, T, D]), sb("result", [P, T, D])
        stats, mean_var = sb("stats", [P, T, 6]), sb("mean_var", [P, T, 2])
        var_eps, rstd = sb("var_eps", [P, T]), sb("rstd", [P, T])
        xT = sb("xT", [D, S])
        g = [sb(f"g{l}_", [HID, S]) for l in range(3)]
        ps_a = ps("ps_a", [P, 2 * S])
        ps_g, ps_y = ps("ps_g", [P, S]), ps("ps_y", [P, S])
        w_loaded, bias_ready, attended_ready, aT_ps, aT_sb = (sem("w_loaded"), sem("bias_ready"),
                                                              sem("attended_ready"), sem("aT_ps"), sem("aT_sb"))
        y_ps, var, rstd_ready, xn_ready, xT_ps, xT_sb = (sem("y_ps"), sem("var"), sem("rstd_ready"), sem("xn_ready"),
                                                         sem("xT_ps"), sem("xT_sb"))
        g_ps, g_sb, out_ps, result_ready, stored = sem("g_ps"), sem("g_sb"), sem("out_ps"), sem("result_ready"), sem("stored")
        chain = take(nc.alloc_semaphore("d_chain"))
        gate = {e: take(nc.alloc_semaphore(f"d_gate_{e}")) for e in ("dve", "pe")}
        block = ctx.enter_context(nc.Block())

        @block.sync
        def _(sp):
            for u in range(2):
                sp.sem_inc(stored[u], 16)
            with sp.Fori(0, PAIRS) as i:
                for u in range(2):
                    sp.wait_ge(out_ps[u], i + 1)
                    for j in range(T):
                        route = sp.value_load(t["route_row"][0:1, bass.ds(i * (2 * T) + u * T + j, 1)],
                                              min_val=0, max_val=R - 1)
                        sp.dma_start(w_routed[u][:, j, :, :].rearrange("p l c -> p (l c)"),
                                     a["w_routed"][bass.ds(route, 1), :, :].rearrange("r p c -> (r p) c")) \
                            .then_inc(w_loaded[u], 16)
                for u in range(2):
                    sp.wait_ge(result_ready[u], i + 2)
                    sp.dma_start(out[bass.ds(i * 2 + u, 1), :, :].rearrange("b (j p) d -> p (b j) d", p=P),
                                 result[u][:, :, :]).then_inc(stored[u], 16)
            for u in range(2):
                sp.wait_ge(stored[u], 16 * (PAIRS + 1))

        @block.gpsimd
        def _(pool):
            with pool.Fori(0, PAIRS) as i:
                for u in range(2):
                    pool.wait_ge(w_loaded[u], i * (16 * T) + 16 * T)
                    for j in range(T):
                        last = nc.gpsimd.tensor_tensor(bias[u][:, j, :], w_routed[u][:, j, :, HID], t["b_shared"][:, :],
                                                       ALU.add)
                    last.then_inc(bias_ready[u], 1)
                for u in range(2):
                    pool.wait_ge(var[u], i + 1)
                    nc.gpsimd.tensor_tensor(rstd[u][:, :], var_eps[u][:, :], t["minus_half"][:, :], ALU.pow) \
                        .then_inc(rstd_ready[u], 1)

        @block.vector
        def _(dve):
            count = [0]

            def link(ins):
                count[0] += 1
                ins.then_inc(chain, 1)
                dve.wait_ge(chain, count[0])

            for u in range(2):
                dve.sem_inc(result_ready[u], 1)
            with dve.Fori(0, PAIRS) as i:
                count[0] = 0
                for u in range(2):
                    ours = t["heads"][:, bass.ds(i * (2 * H * OW) + u * H * OW, H * OW)] \
                        .rearrange("p (h j c) -> p h j c", h=H, j=T)
                    link(nc.vector.reciprocal(inv[u][:, :, :], ours[:, :, :, HD]))
                    for j in range(T):
                        last = nc.vector.tensor_tensor(
                            attended[u][:, j, :].rearrange("p (h c) -> p h c", h=H), ours[:, :, j, 0:HD],
                            spread(inv[u][:, :, j], HD), ALU.mult)
                    last.then_inc(attended_ready[u], 1)
                for u in range(2):
                    dve.wait_ge(y_ps[u], i + 1)
                    dve.sem_inc(gate["dve"], 1)
                    link(nc.vector.tensor_tensor(h[u][:, :, :], ps_y[u][:, 0:T * D].rearrange("p (j d) -> p j d", j=T),
                                                 t["hidden"][:, bass.ds(i * (2 * T) + u * T, T), :], ALU.add))
                    for j in range(T):
                        last = nc.vector.bn_stats(stats[u][:, j, :], h[u][:, j, :])
                    link(last)
                    for j in range(T):
                        last = nc.vector.bn_aggr(mean_var[u][:, j, :], stats[u][:, j, :])
                    link(last)
                    nc.vector.tensor_scalar(var_eps[u][:, :], mean_var[u][:, :, 1], EPS, None, ALU.add).then_inc(var[u], 1)
                for u in range(2):
                    dve.wait_ge(rstd_ready[u], i + 1)
                    for j in range(T):
                        last = nc.vector.tensor_scalar(xn[u][:, j, :], h[u][:, j, :], mean_var[u][:, j, 0:1],
                                                       rstd[u][:, j:j + 1], ALU.subtract, ALU.mult)
                    last.then_inc(xn_ready[u], 1)
                for u in range(2):
                    dve.wait_ge(out_ps[u], i + 2)
                    dve.sem_inc(gate["dve"], 1)
                    dve.wait_ge(stored[u], i * 16 + 16)
                    nc.vector.tensor_tensor(result[u][:, :, :], h[u][:, :, :],
                                            ps_y[u][:, 0:T * D].rearrange("p (j d) -> p j d", j=T), ALU.add) \
                        .then_inc(result_ready[u], 1)
                dve.sem_clear(chain)

        @block.tensor
        def _(pe):
            def rows(u, lhs, rhs, b_row):
                for j in range(T):
                    for c, (l, r) in enumerate(zip(lhs, rhs)):
                        nc.tensor.matmul(ps_y[u][:, j * D:(j + 1) * D], l[:, j * P:(j + 1) * P], r, start=(c == 0),
                                         stop=False)
                    last = nc.tensor.matmul(ps_y[u][:, j * D:(j + 1) * D], t["ones_row"][:, :], b_row, start=False,
                                            stop=True)
                return last

            for u in range(2):
                pe.sem_inc(out_ps[u], 1)
            with pe.Fori(0, PAIRS) as i:
                for u in range(2):
                    pe.wait_ge(attended_ready[u], i + 1)
                    for c in range(2):
                        for j in range(T):
                            last = nc.tensor.transpose(ps_a[u][:, c * S + j * P:c * S + (j + 1) * P],
                                                       attended[u][:, j, c * P:(c + 1) * P], t["ident"][:, :])
                    last.then_inc(aT_ps[u], 1)
                for u in range(2):
                    pe.wait_ge(aT_sb[u], i + 1)
                    pe.wait_ge(result_ready[u], i + 1)
                    rows(u, [attendedT[u][:, c, :] for c in range(2)], [t["w_proj"][:, c, :] for c in range(2)],
                         t["b_proj"][:, :]).then_inc(y_ps[u], 1)
                for u in range(2):
                    pe.wait_ge(xn_ready[u], i + 1)
                    pe.sem_inc(gate["pe"], 1)
                    for j in range(T):
                        last = nc.tensor.transpose(ps_a[u][0:D, j * P:(j + 1) * P], xn[u][:, j, :], t["ident"][:, :])
                    last.then_inc(xT_ps[u], 1)
                for u in range(2):
                    pe.wait_ge(xT_sb[u], i + 1)
                    nc.tensor.matmul(ps_g[u][:, :], t["w_inT"][:, :], xT[u][:, :], start=True, stop=True) \
                        .then_inc(g_ps[u], 1)
                for l in range(2):
                    for u in range(2):
                        pe.wait_ge(g_sb[u], i * 3 + l + 1)
                        pe.wait_ge(w_loaded[u], i * (16 * T) + 16 * T)
                        nc.tensor.matmul(ps_g[u][:, :], t["w_shared"][:, l, :], g[l][u][:, :], start=True, stop=False)
                        for j in range(T):
                            last = nc.tensor.matmul(ps_g[u][:, j * P:(j + 1) * P], w_routed[u][:, j, l, 0:HID],
                                                    g[l][u][:, j * P:(j + 1) * P], start=False, stop=(j == T - 1))
                        last.then_inc(g_ps[u], 1)
                for u in range(2):
                    pe.wait_ge(g_sb[u], i * 3 + 3)
                    rows(u, [g[2][u][:, :]], [t["w_outT"][:, :]], t["b_out"][:, :]).then_inc(out_ps[u], 1)

        @block.scalar
        def _(act):
            with act.Fori(0, PAIRS) as i:
                for u in range(2):
                    act.wait_ge(aT_ps[u], i + 1)
                    nc.scalar.activation(attendedT[u][:, :, :], ps_a[u][:, :].rearrange("p (c q) -> p c q", c=2),
                                         ACT.Copy).then_inc(aT_sb[u], 1)
                for u in range(2):
                    act.wait_ge(xT_ps[u], i + 1)
                    nc.scalar.activation(xT[u][:, :], ps_a[u][0:D, 0:S], ACT.Copy).then_inc(xT_sb[u], 1)
                for u in range(2):
                    act.wait_ge(g_ps[u], i * 3 + 1)
                    nc.scalar.activation(g[0][u][:, :], ps_g[u][:, :], ACT.Relu, bias=t["b_in"][:, :]).then_inc(g_sb[u], 1)
                for l in range(2):
                    for u in range(2):
                        act.wait_ge(g_ps[u], i * 3 + l + 2)
                        act.wait_ge(bias_ready[u], i + 1)
                        for j in range(T):
                            last = nc.scalar.activation(g[l + 1][u][:, j * P:(j + 1) * P], ps_g[u][:, j * P:(j + 1) * P],
                                                        ACT.Relu, bias=bias[u][:, j, l:l + 1])
                        last.then_inc(g_sb[u], 1)


def kernel(**inputs):
    import numpy as np
    import concourse.bacc as bacc
    from concourse.bass_utils import run_bass_kernel_spmd as run

    v = {name: np.asarray(x) for name, x in inputs.items()}
    row = lambda x: x.reshape(1, -1)
    heads = lambda x, n: x.reshape(n, 3, H, HD).transpose(0, 2, 1, 3).reshape(n, H, 3 * HD)
    w_routed = np.concatenate([v["L1_ffn_Wr"].transpose(1, 3, 0, 2), v["L1_ffn_br"].transpose(1, 2, 0)[..., None]], axis=3)
    arrays = {
        "token_ids": v["x"].reshape(NT, P).T,
        "table": v["L0_tok_W"].T,
        "L0_attn_Wq": v["L0_attn_Wq"],
        "L0_attn_Wk": v["L0_attn_Wk"],
        "wv0T": v["L0_attn_Wv"].T,
        "L0_ffn_Wr": v["L0_ffn_Wr"],
        "L0_ffn_br": row(v["L0_ffn_br"]),
        "L0_ffn_W1": v["L0_ffn_W1"],
        "w2_b1": np.concatenate([v["L0_ffn_W2"], v["L0_ffn_b1"][..., None]], axis=2),
        "L0_ffn_b2": v["L0_ffn_b2"],
        "L0_ffn_gamma": v["L0_ffn_gamma"],
        "L0_ffn_beta": v["L0_ffn_beta"],
        "w_heads": heads(v["L1_attn_w_qkv"], D),
        "b_heads": heads(row(v["L1_attn_b_qkv"]), 1),
        "L1_attn_scale": v["L1_attn_scale"].reshape(-1),
        "mem_kT": v["L1_attn_mem_k"].transpose(2, 0, 1),
        "mem_v": v["L1_attn_mem_v"].transpose(1, 0, 2),
        "w_proj": v["L1_attn_w_proj"].reshape(2, P, D).transpose(1, 0, 2),
        "L1_attn_b_proj": row(v["L1_attn_b_proj"]),
        "w_inT": v["L1_ffn_Wi"].T,
        "b_in": v["L1_ffn_bi"].reshape(-1, 1),
        "w_routed": w_routed.reshape(R, HID, 2 * (HID + 1)),
        "w_shared": v["L1_ffn_Ws"].reshape(2, HID, HID).transpose(2, 0, 1),
        "b_shared": v["L1_ffn_bs"].reshape(2, HID).T,
        "w_outT": v["L1_ffn_Wo"].T,
        "L1_ffn_bo": row(v["L1_ffn_bo"]),
        "L1_ffn_route_id": row(v["L1_ffn_route_id"]),
    }
    nc = bacc.Bacc("TRN2", target_bir_lowering=False, num_devices=1)
    feed, aps = {}, {}
    for name, x in arrays.items():
        feed["in_" + name] = np.ascontiguousarray(x)
        aps[name] = nc.dram_tensor("in_" + name, x.shape, mybir.dt.from_np(x.dtype), kind="ExternalInput").ap()
    out = nc.dram_tensor("out", (B, S, D), F32, kind="ExternalOutput").ap()
    tower(nc, aps, out)
    return run(nc, [feed], core_ids=[0]).results[0]["out"]
```

```python
from contextlib import ExitStack, contextmanager

import concourse.bass as bass
from concourse import mybir

F32 = mybir.dt.float32
I32 = mybir.dt.int32
U32 = mybir.dt.uint32
ALU = mybir.AluOpType
ACT = mybir.ActivationFunctionType
AX = mybir.AxisListType

P = 128
B, S, D = 16, 512, 64
T = S // P
NT = B * T
EPS = 1e-5
E0, F0 = 8, 128
CAPACITY = 1280.0
H, HD, M = 8, 32, 4
SK = S + M
TOPK = 32
R, HID = 16, 128
HV = HD + 1
VM = HD + M
OW = T * HV
NH = B * H
FILL = -(2.0 ** 64)
STEEP = 2.0 ** 62
REMOVED = -3.0e38
PAIRS = B // 2


def spread(ap, width):
    return ap.unsqueeze(2).to_broadcast([ap.shape[0], ap.shape[1], width])


def tower(nc, a, out):
    ctx = ExitStack()
    with ctx:
        def sb(name, shape, dt=F32):
            return ctx.enter_context(nc.sbuf_tensor(name, shape, dt))

        t = {}
        t["hidden"] = sb("hidden", [P, NT, D])
        t["normed"] = sb("normed", [P, NT, D])
        t["normedT"] = sb("normedT", [D, B * S])
        t["heads"] = sb("heads", [P, NH * OW])
        t["ident"] = sb("ident", [P, P])
        t["ones_row"] = sb("ones_row", [1, P])
        t["minus_half"] = sb("minus_half", [P, T])
        t["token_ids"] = sb("token_ids", [P, NT], I32)
        t["mix_qk"] = sb("mix_qk", [D, D])
        t["wv0T"] = sb("wv0T", [D, D])
        t["token_sums"] = sb("token_sums", [D, B])
        t["w_route"] = sb("w_route", [D, E0])
        t["b_route"] = sb("b_route", [1, E0])
        t["gate_cols"] = sb("gate_cols", [P, 2 * B])
        t["expert_row"] = sb("expert_row", [1, 2 * B], U32)
        t["gamma"] = sb("gamma", [P, D])
        t["beta"] = sb("beta", [P, D])
        t["w_qk"] = sb("w_qk", [D + 1, H, 2 * HD])
        t["w_vm"] = sb("w_vm", [D + 1, H, VM])
        t["mem_v"] = sb("mem_v", [M, H, HD])
        t["w_proj"] = sb("w_proj", [P, 2, D])
        t["b_proj"] = sb("b_proj", [1, D])
        t["w_inT"] = sb("w_inT", [D, HID])
        t["b_in"] = sb("b_in", [HID, 1])
        t["w_shared"] = sb("w_shared", [HID, 2, HID])
        t["b_shared"] = sb("b_shared", [HID, 2])
        t["w_outT"] = sb("w_outT", [HID, D])
        t["b_out"] = sb("b_out", [1, D])
        t["route_row"] = sb("route_row", [1, B * T], I32)

        setup(nc, a, t)
        attention0(nc, a, t)
        router(nc, t)
        experts(nc, a, t)
        attention1(nc, t)
        routed_ffn(nc, a, t, out)


@contextmanager
def phase(nc):
    taken = []

    def take(semaphore):
        taken.append(semaphore)
        return semaphore

    with ExitStack() as ctx:
        yield ctx, take
    nc.clear_and_free_semaphores(taken)
    nc.all_engine_barrier()


def setup(nc, a, t):
    with phase(nc) as (ctx, take):
        wq = ctx.enter_context(nc.sbuf_tensor("wq", [D, D], F32))
        wk = ctx.enter_context(nc.sbuf_tensor("wk", [D, D], F32))
        q_scale = ctx.enter_context(nc.sbuf_tensor("q_scale", [D + 1, H], F32))
        mem_scale = ctx.enter_context(nc.sbuf_tensor("mem_scale", [HD, H], F32))
        mem_kT = ctx.enter_context(nc.sbuf_tensor("mem_kT", [HD, H, M], F32))
        w_qT = ctx.enter_context(nc.sbuf_tensor("w_qT", [HD, H, D + 1], F32))
        ps_mem = ctx.enter_context(nc.psum_tensor("ps_mem", [D + 1, H, M], F32))
        ps_mix = ctx.enter_context(nc.psum_tensor("ps_mix", [D, D], F32))
        sem = lambda name: take(nc.alloc_semaphore(name))
        loaded, cleared, made = sem("loaded"), sem("cleared"), sem("made")
        mixed, scaled, copied = sem("mixed"), sem("scaled"), sem("copied")
        block = ctx.enter_context(nc.Block())
        loads = [
            (t["token_ids"][:, :], a["token_ids"]),
            (wq[:, :], a["L0_attn_Wq"]),
            (wk[:, :], a["L0_attn_Wk"]),
            (q_scale[:, :], a["L1_attn_scale"].partition_broadcast(D + 1)),
            (t["wv0T"][:, :], a["wv0T"]),
            (t["w_route"][:, :], a["L0_ffn_Wr"]),
            (t["b_route"][:, :], a["L0_ffn_br"]),
            (t["gamma"][:, :], a["L0_ffn_gamma"].partition_broadcast(P)),
            (t["beta"][:, :], a["L0_ffn_beta"].partition_broadcast(P)),
            (mem_scale[:, :], a["L1_attn_scale"].partition_broadcast(HD)),
            (t["w_qk"][:, :, :], a["w_qk"]),
            (t["w_vm"][:, :, 0:HD], a["w_v"]),
            (w_qT[:, :, :], a["w_qT"]),
            (mem_kT[:, :, :], a["mem_kT"]),
            (t["mem_v"][:, :, :], a["mem_v"]),
            (t["w_proj"][:, :, :], a["w_proj"]),
            (t["b_proj"][:, :], a["L1_attn_b_proj"]),
            (t["w_inT"][:, :], a["w_inT"]),
            (t["b_in"][:, :], a["b_in"]),
            (t["w_shared"][:, :, :], a["w_shared"]),
            (t["b_shared"][:, :], a["b_shared"]),
            (t["w_outT"][:, :], a["w_outT"]),
            (t["b_out"][:, :], a["L1_ffn_bo"]),
            (t["route_row"][:, :], a["L1_ffn_route_id"]),
        ]

        @block.sync
        def _(sp):
            for dst, src in loads:
                sp.dma_start(dst, src).then_inc(loaded, 16)
            sp.wait_ge(loaded, 16 * len(loads))

        @block.gpsimd
        def _(pool):
            nc.gpsimd.memset(t["ident"][:, :], 0.0).then_inc(cleared, 1)
            nc.gpsimd.memset(t["ones_row"][:, :], 1.0)
            nc.gpsimd.memset(t["minus_half"][:, :], -0.5)
            pool.wait_ge(cleared, 1)
            nc.gpsimd.affine_select(out=t["ident"][:, :], in_=t["ident"][:, :], compare_op=ALU.not_equal,
                                    fill=1.0, base=0, pattern=[[-1, P]], channel_multiplier=1).then_inc(made, 1)
            pool.wait_ge(made, 1)

        @block.tensor
        def _(pe):
            pe.wait_ge(loaded, 16 * len(loads))
            nc.tensor.matmul(ps_mix[:, :], wq[:, :], wk[:, :], start=True, stop=True).then_inc(mixed, 1)
            pe.wait_ge(scaled, 4)
            for head in range(H):
                last = nc.tensor.matmul(ps_mem[:, head, :], w_qT[:, head, :], mem_kT[:, head, :], start=True, stop=True)
            last.then_inc(mixed, 1)

        @block.scalar
        def _(act):
            act.wait_ge(mixed, 1)
            nc.scalar.activation(t["mix_qk"][:, :], ps_mix[:, :], ACT.Copy, scale=D ** -0.5).then_inc(copied, 1)
            act.wait_ge(mixed, 2)
            nc.scalar.activation(t["w_vm"][:, :, HD:VM], ps_mem[:, :, :], ACT.Copy).then_inc(copied, 1)
            act.wait_ge(copied, 2)

        @block.vector
        def _(dve):
            dve.wait_ge(loaded, 16 * len(loads))
            nc.vector.tensor_scalar(q_scale[:, :], q_scale[:, :], HD ** -0.5, None, ALU.mult).then_inc(scaled, 1)
            nc.vector.tensor_scalar(mem_scale[:, :], mem_scale[:, :], HD ** -0.5, None, ALU.mult).then_inc(scaled, 1)
            dve.wait_ge(scaled, 2)
            wq_part = t["w_qk"][:, :, 0:HD]
            nc.vector.tensor_tensor(wq_part, wq_part, spread(q_scale[:, :], HD), ALU.mult).then_inc(scaled, 1)
            nc.vector.tensor_tensor(mem_kT[:, :, :], mem_kT[:, :, :], spread(mem_scale[:, :], M), ALU.mult) \
                .then_inc(scaled, 1)
            dve.wait_ge(made, 1)
            for l in range(2):
                nc.vector.tensor_tensor(t["w_shared"][:, l, :], t["w_shared"][:, l, :], t["ident"][:, :],
                                        ALU.add).then_inc(scaled, 1)
            dve.wait_ge(scaled, 6)


def attention0(nc, a, t):
    with phase(nc) as (ctx, take):
        def sb(name, shape, dt=F32):
            return [ctx.enter_context(nc.sbuf_tensor(f"a_{name}{u}", shape, dt)) for u in range(2)]

        def ps(name, shape):
            return [ctx.enter_context(nc.psum_tensor(f"a_{name}{u}", shape, F32)) for u in range(2)]

        def sem(name):
            return [take(nc.alloc_semaphore(f"a_{name}{u}")) for u in range(2)]

        ids = sb("ids", [P, T], I32)
        gathered_rows = sb("gathered_rows", [P, T, D])
        not_pad = sb("not_pad", [P, T])
        h = sb("h", [P, T, D])
        stats, mean_var = sb("stats", [P, T, 6]), sb("mean_var", [P, T, 2])
        var_eps, rstd = sb("var_eps", [P, T]), sb("rstd", [P, T])
        xn, x2 = sb("xn", [P, T, D]), sb("x2", [P, T, D])
        xT, mixT = sb("xT", [D, S]), sb("mixT", [D, S])
        neg_max, weight_sum, inv_sum = sb("neg_max", [P, T]), sb("weight_sum", [P, T]), sb("inv_sum", [P, T])
        weights = [t["heads"][:, u * T * S:(u + 1) * T * S].rearrange("p (k q) -> p k q", k=T) for u in range(2)]
        values = sb("values", [P, T, D])
        ps_x = ps("ps_x", [D, S])
        ps_vo = ps("ps_vo", [P, S])
        ps_sc = [ps(f"ps_sc{u}_", [P, S]) for u in range(2)]

        ids_ready, gathered, rows_used = sem("ids_ready"), sem("gathered"), sem("rows_used")
        var1, rstd1, xn_ready = sem("var1"), sem("rstd1"), sem("xn_ready")
        xT_ps, xT_sb, mix_ps, mix_sb = sem("xT_ps"), sem("xT_sb"), sem("mix_ps"), sem("mix_sb")
        v_ps, score_ps, max_ready, exp_ready = sem("v_ps"), sem("score_ps"), sem("max_ready"), sem("exp_ready")
        v_ready, o_ps, h_added, h_saved = sem("v_ready"), sem("o_ps"), sem("h_added"), sem("h_saved")
        var2, rstd2, x2_ready, x2_saved = sem("var2"), sem("rstd2"), sem("x2_ready"), sem("x2_saved")
        x2T_ps, x2T_saved = sem("x2T_ps"), sem("x2T_saved")
        chain = take(nc.alloc_semaphore("a_chain"))
        gate = {e: take(nc.alloc_semaphore(f"a_gate_{e}")) for e in ("pool", "act", "dve", "pe")}
        block = ctx.enter_context(nc.Block())

        @block.gpsimd
        def _(pool):
            for u in range(2):
                pool.sem_inc(h_saved[u], 1)
                pool.sem_inc(x2_saved[u], 1)
            with pool.Fori(0, PAIRS) as i:
                for u in range(2):
                    pool.wait_ge(rows_used[u], i + 1)
                    pool.sem_inc(gate["pool"], 1)
                    nc.gpsimd.tensor_copy(ids[u][:, :], t["token_ids"][:, bass.ds(i * (2 * T) + u * T, T)]) \
                        .then_inc(ids_ready[u], 1)
                    pool.wait_ge(ids_ready[u], i + 1)
                    pool.sem_inc(gate["pool"], 1)
                    for j in range(T):
                        nc.gpsimd.indirect_dma_start(
                            out=gathered_rows[u][:, j, :], out_offset=None, in_=a["table"],
                            in_offset=bass.IndirectOffsetOnAxis(ap=ids[u][:, j:j + 1].bitcast(U32), axis=0),
                        ).then_inc(gathered[u], 16)
                for u in range(2):
                    pool.wait_ge(var1[u], i + 1)
                    nc.gpsimd.tensor_tensor(rstd[u][:, :], var_eps[u][:, :], t["minus_half"][:, :], ALU.pow) \
                        .then_inc(rstd1[u], 1)
                for u in range(2):
                    pool.wait_ge(h_added[u], i + 2)
                    pool.sem_inc(gate["pool"], 1)
                    nc.gpsimd.tensor_copy(t["hidden"][:, bass.ds(i * (2 * T) + u * T, T), :], h[u][:, :, :]) \
                        .then_inc(h_saved[u], 1)
                    pool.wait_ge(var2[u], i + 1)
                    nc.gpsimd.tensor_tensor(rstd[u][:, :], var_eps[u][:, :], t["minus_half"][:, :], ALU.pow) \
                        .then_inc(rstd2[u], 1)
                for u in range(2):
                    pool.wait_ge(x2_ready[u], i + 1)
                    pool.sem_inc(gate["pool"], 1)
                    nc.gpsimd.tensor_copy(t["normed"][:, bass.ds(i * (2 * T) + u * T, T), :], x2[u][:, :, :]) \
                        .then_inc(x2_saved[u], 1)

        @block.vector
        def _(dve):
            count = [0]

            def link(ins):
                count[0] += 1
                ins.then_inc(chain, 1)
                dve.wait_ge(chain, count[0])

            def variance(u):
                for j in range(T):
                    last = nc.vector.bn_stats(stats[u][:, j, :], h[u][:, j, :])
                link(last)
                for j in range(T):
                    last = nc.vector.bn_aggr(mean_var[u][:, j, :], stats[u][:, j, :])
                link(last)

            def normalise(dst, u):
                for j in range(T):
                    last = nc.vector.tensor_scalar(dst[u][:, j, :], h[u][:, j, :], mean_var[u][:, j, 0:1],
                                                   rstd[u][:, j:j + 1], ALU.subtract, ALU.mult)
                return last

            for u in range(2):
                dve.sem_inc(rows_used[u], 1)
                dve.sem_inc(h_added[u], 1)
            with dve.Fori(0, PAIRS) as i:
                count[0] = 0
                for u in range(2):
                    dve.wait_ge(gathered[u], i * (16 * T) + 16 * T)
                    dve.sem_inc(gate["dve"], 1)
                    link(nc.vector.tensor_scalar(not_pad[u][:, :], ids[u][:, :], 0.0, None, ALU.not_equal))
                    dve.wait_ge(h_saved[u], i + 1)
                    nc.vector.tensor_tensor(h[u][:, :, :], gathered_rows[u][:, :, :], spread(not_pad[u][:, :], D),
                                            ALU.mult).then_inc(rows_used[u], 1)
                    dve.wait_ge(rows_used[u], i + 2)
                    dve.sem_inc(gate["dve"], 1)
                    variance(u)
                    nc.vector.tensor_scalar(var_eps[u][:, :], mean_var[u][:, :, 1], EPS, None, ALU.add) \
                        .then_inc(var1[u], 1)
                for u in range(2):
                    dve.wait_ge(rstd1[u], i + 1)
                    normalise(xn, u).then_inc(xn_ready[u], 1)
                for k in range(T):
                    for u in range(2):
                        dve.wait_ge(score_ps[u], i * T + k + 1)
                        nc.vector.tensor_reduce(neg_max[u][:, k:k + 1], ps_sc[u][k % 2][:, :], AX.X, ALU.max,
                                                negate=True).then_inc(max_ready[u], 1)
                for u in range(2):
                    dve.wait_ge(exp_ready[u], i * T + T)
                    link(nc.vector.reciprocal(inv_sum[u][:, :], weight_sum[u][:, :]))
                    dve.wait_ge(v_ps[u], i + 1)
                    nc.vector.tensor_tensor(values[u][:, :, :],
                                            ps_vo[u][:, 0:T * D].rearrange("p (k d) -> p k d", k=T),
                                            spread(inv_sum[u][:, :], D), ALU.mult).then_inc(v_ready[u], 1)
                for u in range(2):
                    dve.wait_ge(o_ps[u], i + 1)
                    nc.vector.tensor_tensor(h[u][:, :, :], h[u][:, :, :],
                                            ps_vo[u][:, 0:T * D].rearrange("p (k d) -> p k d", k=T),
                                            ALU.add).then_inc(h_added[u], 1)
                    dve.wait_ge(h_added[u], i + 2)
                    dve.sem_inc(gate["dve"], 1)
                    variance(u)
                    nc.vector.tensor_scalar(var_eps[u][:, :], mean_var[u][:, :, 1], EPS, None, ALU.add) \
                        .then_inc(var2[u], 1)
                for u in range(2):
                    dve.wait_ge(rstd2[u], i + 1)
                    dve.sem_inc(gate["dve"], 1)
                    dve.wait_ge(x2_saved[u], i + 1)
                    normalise(x2, u).then_inc(x2_ready[u], 1)
                dve.sem_clear(chain)

        @block.tensor
        def _(pe):
            def to_features(u, x):
                for j in range(T):
                    last = nc.tensor.transpose(ps_x[u][:, j * P:(j + 1) * P], x[u][:, j, :], t["ident"][:, :])
                return last

            with pe.Fori(0, PAIRS) as i:
                for u in range(2):
                    pe.wait_ge(xn_ready[u], i + 1)
                    pe.wait_ge(x2T_saved[u], i + 1)
                    pe.sem_inc(gate["pe"], 1)
                    to_features(u, xn).then_inc(xT_ps[u], 1)
                for u in range(2):
                    pe.wait_ge(xT_sb[u], i + 1)
                    pe.sem_inc(gate["pe"], 1)
                    nc.tensor.matmul(ps_x[u][:, :], t["mix_qk"][:, :], xT[u][:, :], start=True, stop=True) \
                        .then_inc(mix_ps[u], 1)
                    pe.wait_ge(h_added[u], i + 1)
                    for k in range(T):
                        last = nc.tensor.matmul(ps_vo[u][:, k * D:(k + 1) * D], xT[u][:, k * P:(k + 1) * P],
                                                t["wv0T"][:, :], start=True, stop=True)
                    last.then_inc(v_ps[u], 1)
                for k in range(T):
                    for u in range(2):
                        if k == 0:
                            pe.wait_ge(mix_sb[u], i + 1)
                        if k >= 2:
                            pe.wait_ge(exp_ready[u], i * T + k - 1)
                        nc.tensor.matmul(ps_sc[u][k % 2][:, :], xT[u][:, k * P:(k + 1) * P], mixT[u][:, :],
                                         start=True, stop=True).then_inc(score_ps[u], 1)
                for u in range(2):
                    pe.wait_ge(v_ready[u], i + 1)
                    for j in range(T):
                        for k in range(T):
                            last = nc.tensor.matmul(ps_vo[u][:, j * D:(j + 1) * D],
                                                    weights[u][:, k, j * P:(j + 1) * P], values[u][:, k, :],
                                                    start=(k == 0), stop=(k == T - 1))
                    last.then_inc(o_ps[u], 1)
                for u in range(2):
                    pe.wait_ge(x2_ready[u], i + 1)
                    pe.sem_inc(gate["pe"], 1)
                    to_features(u, x2).then_inc(x2T_ps[u], 1)

        @block.scalar
        def _(act):
            for u in range(2):
                act.sem_inc(x2T_saved[u], 1)
            with act.Fori(0, PAIRS) as i:
                for u in range(2):
                    act.wait_ge(xT_ps[u], i + 1)
                    nc.scalar.activation(xT[u][:, :], ps_x[u][:, :], ACT.Copy).then_inc(xT_sb[u], 1)
                for u in range(2):
                    act.wait_ge(mix_ps[u], i + 1)
                    nc.scalar.activation(mixT[u][:, :], ps_x[u][:, :], ACT.Copy).then_inc(mix_sb[u], 1)
                for k in range(T):
                    for u in range(2):
                        act.wait_ge(max_ready[u], i * T + k + 1)
                        nc.scalar.activation(weights[u][:, k, :], ps_sc[u][k % 2][:, :], ACT.Exp,
                                             bias=neg_max[u][:, k:k + 1], accum_out=weight_sum[u][:, k:k + 1]) \
                            .then_inc(exp_ready[u], 1)
                for u in range(2):
                    act.wait_ge(x2T_ps[u], i + 1)
                    act.sem_inc(gate["act"], 1)
                    nc.scalar.activation(t["normedT"][:, bass.ds(i * (2 * S) + u * S, S)], ps_x[u][:, :], ACT.Copy,
                                         accum_out=t["token_sums"][:, bass.ds(i * 2 + u, 1)]) \
                        .then_inc(x2T_saved[u], 1)


def router(nc, t):
    with phase(nc) as (ctx, take):
        def sb(name, shape, dt=F32):
            return ctx.enter_context(nc.sbuf_tensor("r_" + name, shape, dt))

        means = sb("means", [D, B])
        load_rows = sb("load_rows", [B, B])
        top, neg_top, total, inv = sb("top", [B, 1]), sb("neg_top", [B, 1]), sb("total", [B, 1]), sb("inv", [B, 1])
        probs, shrink = sb("probs", [B, E0]), sb("shrink", [B, E0])
        best, best_at = sb("best", [B, 8]), sb("best_at", [B, 8], U32)
        pair = sb("pair", [B, 2])
        gate_row = sb("gate_row", [1, 2 * B])
        ps_logits = ctx.enter_context(nc.psum_tensor("r_logits", [B, E0], F32))
        ps_loads = ctx.enter_context(nc.psum_tensor("r_loads", [B, E0], F32))
        ps_gates = ctx.enter_context(nc.psum_tensor("r_gates", [P, 2 * B], F32))
        sem = lambda name: take(nc.alloc_semaphore("r_" + name))
        means_ready, logits_ps, steps, exps = sem("means_ready"), sem("logits_ps"), sem("steps"), sem("exps")
        probs_ready, loads_ps, pair_ready, rows_in = sem("probs_ready"), sem("loads_ps"), sem("pair_ready"), sem("rows_in")
        max_ready, gates_ps = sem("max_ready"), sem("gates_ps")
        block = ctx.enter_context(nc.Block())

        @block.tensor
        def _(pe):
            pe.wait_ge(means_ready, 1)
            nc.tensor.matmul(ps_logits[:, :], means[:, :], t["w_route"][:, :], start=True, stop=False)
            nc.tensor.matmul(ps_logits[:, :], t["ones_row"][:, 0:B], t["b_route"][:, :], start=False, stop=True) \
                .then_inc(logits_ps, 1)
            pe.wait_ge(probs_ready, 1)
            nc.tensor.matmul(ps_loads[:, :], load_rows[:, :], probs[:, :], start=True, stop=True).then_inc(loads_ps, 1)
            pe.wait_ge(rows_in, 32)
            nc.tensor.matmul(ps_gates[:, :], t["ones_row"][:, :], gate_row[:, :], start=True, stop=True) \
                .then_inc(gates_ps, 1)

        @block.scalar
        def _(act):
            act.wait_ge(max_ready, 1)
            nc.scalar.activation(probs[:, :], ps_logits[:, :], ACT.Exp, bias=neg_top[:, :], accum_out=total[:, :]) \
                .then_inc(exps, 1)
            act.wait_ge(max_ready, 2)
            nc.scalar.activation(probs[:, :], shrink[:, :], ACT.Exp, bias=neg_top[:, :], accum_out=total[:, :]) \
                .then_inc(exps, 1)
            act.wait_ge(max_ready, 3)
            nc.scalar.activation(pair[:, :], best[:, 0:2], ACT.Exp, bias=neg_top[:, :], accum_out=total[:, :]) \
                .then_inc(exps, 1)
            act.wait_ge(gates_ps, 1)
            nc.scalar.activation(t["gate_cols"][:, :], ps_gates[:, :], ACT.Copy).then_inc(exps, 1)
            act.wait_ge(exps, 4)

        @block.vector
        def _(dve):
            count = [0]

            def link(ins):
                count[0] += 1
                ins.then_inc(steps, 1)
                dve.wait_ge(steps, count[0])

            nc.vector.memset(load_rows[:, :], float(S))
            nc.vector.tensor_scalar(means[:, :], t["token_sums"][:, :], 1.0 / S, None, ALU.mult).then_inc(means_ready, 1)
            dve.wait_ge(logits_ps, 1)
            nc.vector.tensor_reduce(neg_top[:, :], ps_logits[:, :], AX.X, ALU.max, negate=True).then_inc(max_ready, 1)
            dve.wait_ge(exps, 1)
            link(nc.vector.reciprocal(inv[:, :], total[:, :]))
            nc.vector.tensor_scalar(probs[:, :], probs[:, :], inv[:, :], None, ALU.mult).then_inc(probs_ready, 1)
            dve.wait_ge(probs_ready, 1)
            dve.wait_ge(loads_ps, 1)
            link(nc.vector.reciprocal(shrink[:, :], ps_loads[:, :]))
            link(nc.vector.tensor_scalar(shrink[:, :], shrink[:, :], CAPACITY, 1.0, ALU.mult, ALU.min))
            link(nc.vector.tensor_tensor(shrink[:, :], shrink[:, :], probs[:, :], ALU.mult))
            nc.vector.tensor_reduce(neg_top[:, :], shrink[:, :], AX.X, ALU.max, negate=True).then_inc(max_ready, 1)
            dve.wait_ge(exps, 2)
            link(nc.vector.reciprocal(inv[:, :], total[:, :]))
            link(nc.vector.tensor_scalar(probs[:, :], probs[:, :], inv[:, :], None, ALU.mult))
            link(nc.vector.max(best[:, :], probs[:, :]))
            link(nc.vector.max_index(best_at[:, :], best[:, :], probs[:, :]))
            nc.vector.tensor_scalar(neg_top[:, :], best[:, 0:1], -1.0, None, ALU.mult).then_inc(max_ready, 1)
            dve.wait_ge(exps, 3)
            link(nc.vector.reciprocal(inv[:, :], total[:, :]))
            nc.vector.tensor_scalar(pair[:, :], pair[:, :], inv[:, :], None, ALU.mult).then_inc(pair_ready, 1)

        @block.sync
        def _(sp):
            sp.wait_ge(pair_ready, 1)
            sp.dma_start(gate_row[:, :].rearrange("a (b k) -> a b k", k=2), pair[:, :]).then_inc(rows_in, 16)
            sp.dma_start(t["expert_row"][:, :].rearrange("a (b k) -> a b k", k=2), best_at[:, 0:2]).then_inc(rows_in, 16)
            sp.wait_ge(rows_in, 32)


def experts(nc, a, t):
    with phase(nc) as (ctx, take):
        def sb(name, shape, dt=F32):
            return [ctx.enter_context(nc.sbuf_tensor(f"e_{name}{u}", shape, dt)) for u in range(2)]

        def ps(name, shape):
            return [ctx.enter_context(nc.psum_tensor(f"e_{name}{u}", shape, F32)) for u in range(2)]

        def sem(name):
            return [take(nc.alloc_semaphore(f"e_{name}{u}")) for u in range(2)]

        w1, w2, b2 = sb("w1", [D, 2, F0]), sb("w2", [F0, 2, D + 1]), sb("b2", [1, 2, D])
        w2g, b2g = sb("w2g", [F0, 2, D]), sb("b2g", [1, 2, D])
        act_h = sb("act_h", [F0, 2, S])
        r, y, h, x3 = sb("r", [P, T, D]), sb("y", [P, T, D]), sb("h", [P, T, D]), sb("x3", [P, T, D])
        stats, mean_var = sb("stats", [P, T, 6]), sb("mean_var", [P, T, 2])
        var_eps, rstd = sb("var_eps", [P, T]), sb("rstd", [P, T])
        ps_h = [ps(f"ps_h{u}_", [F0, S]) for u in range(2)]
        ps_y = ps("ps_y", [P, S])
        ps_x = ps("ps_x", [D, S])
        w_loaded, w2_gated, h_ps, gelu_ready = sem("w_loaded"), sem("w2_gated"), sem("h_ps"), sem("gelu_ready")
        y_ps, var1, rstd1, y_normed, y_step = sem("y_ps"), sem("var1"), sem("rstd1"), sem("y_normed"), sem("y_step")
        h_ready, var2, rstd2, x3_ready = sem("h_ready"), sem("var2"), sem("rstd2"), sem("x3_ready")
        x3T_ps, x3T_saved = sem("x3T_ps"), sem("x3T_saved")
        chain = take(nc.alloc_semaphore("e_chain"))
        gate = {e: take(nc.alloc_semaphore(f"e_gate_{e}")) for e in ("pool", "act", "dve", "pe")}
        block = ctx.enter_context(nc.Block())

        @block.sync
        def _(sp):
            with sp.Fori(0, PAIRS) as i:
                for u in range(2):
                    sp.wait_ge(y_ps[u], i + 1)
                    for k in range(2):
                        e = sp.value_load(t["expert_row"][0:1, bass.ds(i * 4 + 2 * u + k, 1)], min_val=0, max_val=E0 - 1)
                        sp.dma_start(w1[u][:, k, :], a["L0_ffn_W1"][bass.ds(e, 1), :, :].rearrange("e d f -> (e d) f")) \
                            .then_inc(w_loaded[u], 16)
                        sp.dma_start(w2[u][:, k, :], a["w2_b1"][bass.ds(e, 1), :, :].rearrange("e f d -> (e f) d")) \
                            .then_inc(w_loaded[u], 16)
                        sp.dma_start(b2[u][:, k, :], a["L0_ffn_b2"][bass.ds(e, 1), :]).then_inc(w_loaded[u], 16)

        @block.tensor
        def _(pe):
            for u in range(2):
                pe.sem_inc(y_ps[u], 1)
            with pe.Fori(0, PAIRS) as i:
                for u in range(2):
                    pe.wait_ge(w_loaded[u], i * 96 + 96)
                    pe.sem_inc(gate["pe"], 1)
                    for k in range(2):
                        nc.tensor.matmul(ps_h[u][k][:, :], w1[u][:, k, :], t["normedT"][:, bass.ds(i * (2 * S) + u * S, S)],
                                         start=True, stop=True).then_inc(h_ps[u], 1)
                for u in range(2):
                    pe.wait_ge(w2_gated[u], i + 1)
                    pe.wait_ge(gelu_ready[u], i * 2 + 2)
                    for j in range(T):
                        for k in range(2):
                            nc.tensor.matmul(ps_y[u][:, j * D:(j + 1) * D], act_h[u][:, k, j * P:(j + 1) * P],
                                             w2g[u][:, k, :], start=(k == 0), stop=False)
                        for k in range(2):
                            last = nc.tensor.matmul(ps_y[u][:, j * D:(j + 1) * D], t["ones_row"][:, :],
                                                    b2g[u][:, k, :], start=False, stop=(k == 1))
                    last.then_inc(y_ps[u], 1)
                for u in range(2):
                    pe.wait_ge(x3_ready[u], i + 1)
                    pe.wait_ge(x3T_saved[u], i + 1)
                    pe.sem_inc(gate["pe"], 1)
                    for j in range(T):
                        last = nc.tensor.transpose(ps_x[u][:, j * P:(j + 1) * P], x3[u][:, j, :], t["ident"][:, :])
                    last.then_inc(x3T_ps[u], 1)

        @block.scalar
        def _(act):
            for u in range(2):
                act.sem_inc(x3T_saved[u], 1)
            with act.Fori(0, PAIRS) as i:
                for u in range(2):
                    for k in range(2):
                        act.wait_ge(h_ps[u], i * 2 + k + 1)
                        nc.scalar.activation(act_h[u][:, k, :], ps_h[u][k][:, :], ACT.Gelu, bias=w2[u][:, k, D:D + 1]) \
                            .then_inc(gelu_ready[u], 1)
                for u in range(2):
                    act.wait_ge(x3T_ps[u], i + 1)
                    act.sem_inc(gate["act"], 1)
                    nc.scalar.activation(t["normedT"][:, bass.ds(i * (2 * S) + u * S, S)], ps_x[u][:, :], ACT.Copy) \
                        .then_inc(x3T_saved[u], 1)

        @block.vector
        def _(dve):
            count = [0]

            def link(ins):
                count[0] += 1
                ins.then_inc(chain, 1)
                dve.wait_ge(chain, count[0])

            def variance(u, x):
                for j in range(T):
                    last = nc.vector.bn_stats(stats[u][:, j, :], x[u][:, j, :])
                link(last)
                for j in range(T):
                    last = nc.vector.bn_aggr(mean_var[u][:, j, :], stats[u][:, j, :])
                link(last)
                return nc.vector.tensor_scalar(var_eps[u][:, :], mean_var[u][:, :, 1], EPS, None, ALU.add)

            def normalise(dst, x, u):
                for j in range(T):
                    last = nc.vector.tensor_scalar(dst[u][:, j, :], x[u][:, j, :], mean_var[u][:, j, 0:1],
                                                   rstd[u][:, j:j + 1], ALU.subtract, ALU.mult)
                return last

            with dve.Fori(0, PAIRS) as i:
                count[0] = 0
                for u in range(2):
                    gates = t["gate_cols"][:, bass.ds(i * 4 + 2 * u, 2)]
                    dve.wait_ge(w_loaded[u], i * 96 + 96)
                    dve.sem_inc(gate["dve"], 1)
                    nc.vector.tensor_tensor(w2g[u][:, :, :], w2[u][:, :, 0:D], spread(gates, D), ALU.mult)
                    nc.vector.tensor_tensor(b2g[u][:, :, :], b2[u][:, :, :],
                                            spread(t["gate_cols"][0:1, bass.ds(i * 4 + 2 * u, 2)], D),
                                            ALU.mult).then_inc(w2_gated[u], 1)
                for u in range(2):
                    dve.wait_ge(y_ps[u], i + 2)
                    dve.sem_inc(gate["dve"], 1)
                    link(nc.vector.tensor_tensor(r[u][:, :, :], ps_y[u][:, 0:T * D].rearrange("p (j d) -> p j d", j=T),
                                                 t["normed"][:, bass.ds(i * (2 * T) + u * T, T), :], ALU.add))
                    variance(u, r).then_inc(var1[u], 1)
                for u in range(2):
                    dve.wait_ge(rstd1[u], i + 1)
                    normalise(y, r, u).then_inc(y_normed[u], 1)
                for u in range(2):
                    dve.wait_ge(h_ready[u], i + 1)
                    variance(u, h).then_inc(var2[u], 1)
                for u in range(2):
                    dve.wait_ge(rstd2[u], i + 1)
                    normalise(x3, h, u).then_inc(x3_ready[u], 1)
                dve.sem_clear(chain)

        @block.gpsimd
        def _(pool):
            with pool.Fori(0, PAIRS) as i:
                for u in range(2):
                    pool.wait_ge(var1[u], i + 1)
                    nc.gpsimd.tensor_tensor(rstd[u][:, :], var_eps[u][:, :], t["minus_half"][:, :], ALU.pow) \
                        .then_inc(rstd1[u], 1)
                for u in range(2):
                    hidden = t["hidden"][:, bass.ds(i * (2 * T) + u * T, T), :]
                    pool.wait_ge(y_normed[u], i + 1)
                    for j in range(T):
                        last = nc.gpsimd.tensor_tensor(y[u][:, j, :], y[u][:, j, :], t["gamma"][:, :], ALU.mult)
                    last.then_inc(y_step[u], 1)
                    pool.wait_ge(y_step[u], i * 2 + 1)
                    for j in range(T):
                        last = nc.gpsimd.tensor_tensor(y[u][:, j, :], y[u][:, j, :], t["beta"][:, :], ALU.add)
                    last.then_inc(y_step[u], 1)
                    pool.wait_ge(y_step[u], i * 2 + 2)
                    pool.sem_inc(gate["pool"], 1)
                    nc.gpsimd.tensor_tensor(h[u][:, :, :], y[u][:, :, :], hidden, ALU.add).then_inc(h_ready[u], 1)
                for u in range(2):
                    pool.wait_ge(var2[u], i + 1)
                    nc.gpsimd.tensor_tensor(rstd[u][:, :], var_eps[u][:, :], t["minus_half"][:, :], ALU.pow) \
                        .then_inc(rstd2[u], 1)
                    pool.wait_ge(h_ready[u], i + 1)
                    pool.sem_inc(gate["pool"], 1)
                    nc.gpsimd.tensor_copy(t["hidden"][:, bass.ds(i * (2 * T) + u * T, T), :], h[u][:, :, :])


def attention1(nc, t):
    with phase(nc) as (ctx, take):
        def sb(name, shape, dt=F32):
            return ctx.enter_context(nc.sbuf_tensor("c_" + name, shape, dt))

        def sb2(name, shape, dt=F32):
            return [sb(f"{name}{u}", shape, dt) for u in range(2)]

        def ps(name, width):
            return ctx.enter_context(nc.psum_tensor("c_" + name, [P, width], F32))

        def sem(name):
            return take(nc.alloc_semaphore("c_" + name))

        w_qk = sb2("w_qk", [D + 1, 2 * HD])
        w_vm = sb("w_vm", [D + 1, 2, VM])
        x_in = sb2("x_in", [D + 1, S])
        qT, kT = sb2("qT", [P, S]), sb2("kT", [P, S])
        vals = sb2("vals", [P, T + 1, HV])
        scores = sb2("scores", [P, T, SK])
        left = sb2("left", [P, SK])
        largest = sb("largest", [P, T, TOPK])
        shift = sb("shift", [P, T, 2])
        factors = sb("factors", [P, 2])
        masked = sb2("masked", [P, SK])
        expT = sb2("expT", [P, T + 1, P])
        oT = sb("oT", [HV, S])
        ps_s = [ps(f"ps_s{k}", S) for k in range(2)]
        ps_t = [ps(f"ps_t{k}", 2 * S) for k in range(2)]
        ps_o = ps("ps_o", S)
        ps_v = ps("ps_v", S)

        def vm(u, lo, hi):
            return ps_v[:, OW:OW + T * 2 * VM].rearrange("p (j w) -> p j w", j=T)[:, :, u * VM + lo:u * VM + hi]

        cleared, made = sem("cleared"), sem("made")
        staged = [sem(f"staged{u}") for u in range(2)]
        mem_staged = [sem(f"mem_staged{u}") for u in range(2)]
        s_ps, s_copied, v_ps, v_copied = sem("s_ps"), sem("s_copied"), sem("v_ps"), sem("v_copied")
        s_ready, found, shifts, dropped = sem("s_ready"), sem("found"), sem("shifts"), sem("dropped")
        subtracted, exps, expT_ps, expT_copied = sem("subtracted"), sem("exps"), sem("expT_ps"), sem("expT_copied")
        pv_done, o_copied = sem("pv_done"), sem("o_copied")
        chain = sem("chain")
        gate = {e: sem(f"gate_{e}") for e in ("pool", "act", "dve", "pe")}
        in_loop = NH - 4
        block = ctx.enter_context(nc.Block())
        STAGED = (48, 32)
        RING = T + 1
        O_CREDIT, S_CREDIT = 2 * T, 2 * RING

        @block.sync
        def _(sp):
            sp.wait_ge(made, 1)
            with sp.Fori(0, B) as b:
                with sp.Fori(0, H // 2) as g:
                    for u in range(2):
                        sp.wait_ge(s_copied, (b * H + g * 2) * RING + (u + 1) * RING)
                        sp.dma_start(w_qk[u][:, :], t["w_qk"][:, bass.ds(g * 2 + u, 1), :].rearrange("p h c -> p (h c)")) \
                            .then_inc(staged[u], 16)
                        sp.dma_start(x_in[u][0:D, :], t["normedT"][:, bass.ds(b * S, S)]).then_inc(staged[u], 16)
                        if u == 0:
                            sp.dma_start(w_vm[:, :, :], t["w_vm"][:, bass.ds(g * 2, 2), :]).then_inc(staged[u], 16)
                        sp.wait_ge(pv_done, (b * H + g * 2) * T + (u + 1) * T)
                        sp.dma_start(vals[u][0:M, T, 0:HD],
                                     t["mem_v"][:, bass.ds(g * 2 + u, 1), :].rearrange("p h c -> p (h c)")) \
                            .then_inc(mem_staged[u], 16)

        @block.tensor
        def _(pe):
            def project(n, u, turns):
                pe.wait_ge(staged[u], turns * STAGED[u])
                pe.wait_ge(s_copied, n * RING - 1 + S_CREDIT)
                nc.tensor.matmul(ps_s[u][0:2 * HD, :], w_qk[u][:, :], x_in[u][:, :], start=True, stop=True) \
                    .then_inc(s_ps, 1)

            def project_values():
                for j in range(T):
                    last = nc.tensor.matmul(ps_v[:, OW + j * 2 * VM:OW + (j + 1) * 2 * VM], x_in[0][:, j * P:(j + 1) * P],
                                            w_vm[:, :, :].rearrange("p h c -> p (h c)"), start=True, stop=True)
                return last

            def score(n, u, j):
                pe.wait_ge(s_copied, n * RING + max(j, 1) + S_CREDIT)
                nc.tensor.matmul(ps_s[(u + j + 1) % 2][:, :], qT[u][:, j * P:(j + 1) * P], kT[u][:, :],
                                 start=True, stop=True).then_inc(s_ps, 1)

            def turn_over(n, j):
                pe.wait_ge(exps, n * T + j + 1)
                for c in range(T):
                    nc.tensor.transpose(ps_t[j % 2][:, c * P:(c + 1) * P], masked[j % 2][:, c * P:(c + 1) * P],
                                        t["ident"][:, :])
                nc.tensor.transpose(ps_t[j % 2][0:M, S:S + P], masked[j % 2][:, S:SK], t["ident"][:, :]) \
                    .then_inc(expT_ps, 1)

            def apply(n, u, j, turns=None):
                pe.wait_ge(expT_copied, n * T + j + 1)
                if j == 0:
                    pe.wait_ge(v_copied, n + 1)
                    pe.wait_ge(mem_staged[u], turns * 16)
                for c in range(T + 1):
                    last = nc.tensor.matmul(ps_o[0:HV, j * P:(j + 1) * P], vals[u][:, c, :], expT[j % 2][:, c, :],
                                            start=(c == 0), stop=(c == T))
                last.then_inc(pv_done, 1)

            def queries_first(n):
                pe.wait_ge(o_copied, n + 1)
                pe.sem_inc(gate["pe"], 1)
                for j in range(T):
                    last = nc.tensor.transpose(ps_v[:, j * HV:(j + 1) * HV], oT[:, j * P:(j + 1) * P],
                                               t["ident"][0:HV, 0:HV])
                return last

            def head(n, u, turns, turns_ahead=None, first=False, last=False):
                if not last:
                    score(n + 1, 1 - u, 0)
                if not first:
                    apply(n - 1, 1 - u, T - 1)
                if not last:
                    score(n + 1, 1 - u, 1)
                pe.wait_ge(v_copied, n + 1)
                if u == 1 and not last:
                    project_values()
                if not first:
                    queries_first(n - 1).then_inc(v_ps, 1)
                else:
                    pe.sem_inc(v_ps, 1)
                turn_over(n, 0)
                for j in range(1, T):
                    if not last and j + 1 < T:
                        score(n + 1, 1 - u, j + 1)
                    if turns_ahead is not None and j + 1 == T:
                        project(n + 2, u, turns_ahead)
                    apply(n, u, j - 1, turns)
                    turn_over(n, j)

            pe.wait_ge(made, 1)
            pe.sem_inc(pv_done, O_CREDIT)
            project(0, 0, 1)
            project_values().then_inc(v_ps, 1)
            for j in range(T):
                score(0, 0, j)
            project(1, 1, 1)
            head(0, 0, 1, 2, first=True)
            with pe.Fori(0, in_loop // 2) as i:
                head(i * 2 + 1, 1, i + 1, i + 2)
                head(i * 2 + 2, 0, i + 2, i + 3)
            head(NH - 3, 1, NH // 2 - 1, NH // 2)
            head(NH - 2, 0, NH // 2)
            head(NH - 1, 1, NH // 2, last=True)
            apply(NH - 1, 1, T - 1)
            queries_first(NH - 1).then_inc(v_ps, 1)

        @block.scalar
        def _(act):
            def copy_qk(n, u):
                act.wait_ge(s_ps, n * RING + 1)
                nc.scalar.activation(qT[u][0:HD, :], ps_s[u][0:HD, :], ACT.Copy)
                nc.scalar.activation(kT[u][0:HD, :], ps_s[u][HD:2 * HD, :], ACT.Copy).then_inc(s_copied, 1)

            def copy_outputs(n):
                act.wait_ge(pv_done, n * T + T + O_CREDIT)
                nc.scalar.activation(oT[:, :], ps_o[0:HV, :], ACT.Copy).then_inc(o_copied, 1)

            def copy_values(n, u, outputs=True, values=True):
                act.wait_ge(v_ps, n + 1)
                if outputs:
                    act.sem_inc(gate["act"], 1)
                    last = nc.scalar.activation(t["heads"][:, bass.ds(n * OW - 2 * OW, OW)], ps_v[:, 0:OW], ACT.Copy)
                if values:
                    nc.scalar.activation(vals[u][:, 0:T, 0:HD], vm(u, 0, HD), ACT.Copy)
                    last = nc.scalar.activation(scores[u][:, :, S:SK], vm(u, HD, VM), ACT.Copy)
                last.then_inc(v_copied, 1)

            def copy_scores(n, u, j):
                act.wait_ge(s_ps, n * RING + j + 2)
                nc.scalar.activation(scores[u][:, j, 0:S], ps_s[(u + j + 1) % 2][:, :], ACT.Copy).then_inc(s_copied, 1)

            def drop(n, u, j):
                act.wait_ge(shifts, n * T + j + 1)
                nc.scalar.activation(masked[j % 2][:, :], scores[u][:, j, :], ACT.Relu, scale=-STEEP,
                                     bias=shift[:, j, 1:2]).then_inc(dropped, 1)

            def exponent(n, j):
                act.wait_ge(subtracted, n * T + j + 1)
                nc.scalar.activation(masked[j % 2][:, :], masked[j % 2][:, :], ACT.Exp, bias=shift[:, j, 0:1]) \
                    .then_inc(exps, 1)

            def copy_expT(n, j):
                act.wait_ge(expT_ps, n * T + j + 1)
                nc.scalar.activation(expT[j % 2][:, :, :], ps_t[j % 2][:, 0:(T + 1) * P].rearrange("p (c q) -> p c q", c=T + 1),
                                     ACT.Copy).then_inc(expT_copied, 1)

            def head(n, u, first=False, ahead=True, last=False):
                if not first:
                    copy_expT(n - 1, T - 1)
                drop(n, u, 0)
                if not last:
                    copy_scores(n + 1, 1 - u, 0)
                if not first:
                    copy_outputs(n - 1)
                exponent(n, 0)
                copy_values(n + 1, 1 - u, outputs=not first, values=not last)
                for j in range(1, T):
                    copy_expT(n, j - 1)
                    drop(n, u, j)
                    if not last:
                        copy_scores(n + 1, 1 - u, j)
                    exponent(n, j)
                if ahead:
                    copy_qk(n + 2, u)

            act.wait_ge(made, 1)
            act.sem_inc(s_copied, S_CREDIT)
            copy_qk(0, 0)
            copy_values(0, 0, outputs=False)
            for j in range(T):
                copy_scores(0, 0, j)
            copy_qk(1, 1)
            head(0, 0, first=True)
            with act.Fori(0, in_loop // 2) as i:
                head(i * 2 + 1, 1)
                head(i * 2 + 2, 0)
            head(NH - 3, 1)
            head(NH - 2, 0, ahead=False)
            head(NH - 1, 1, ahead=False, last=True)
            copy_expT(NH - 1, T - 1)
            copy_outputs(NH - 1)
            copy_values(NH + 1, 1, values=False)
            act.wait_ge(v_copied, NH + 2)

        @block.gpsimd
        def _(pool):
            def exclude_self(n, u, j):
                own = scores[u][:, j, j * P:(j + 1) * P]
                if j == 0:
                    pool.wait_ge(v_copied, n + 1)
                    pool.sem_inc(gate["pool"], 1)
                pool.wait_ge(s_copied, n * RING + j + 2 + S_CREDIT)
                pool.sem_inc(gate["pool"], 1)
                nc.gpsimd.affine_select(out=own, in_=own, compare_op=ALU.not_equal, fill=FILL, base=0,
                                        pattern=[[-1, P]], channel_multiplier=1).then_inc(s_ready, 1)

            def head(n, u, last=False):
                for j in range(T):
                    pool.wait_ge(found, n * T + j + 1)
                    nc.gpsimd.tensor_tensor(shift[:, j, :], largest[:, j, 0:TOPK:TOPK - 1], factors[:, :], ALU.mult) \
                        .then_inc(shifts, 1)
                    pool.wait_ge(dropped, n * T + j + 1)
                    nc.gpsimd.tensor_tensor(masked[j % 2][:, :], scores[u][:, j, :], masked[j % 2][:, :], ALU.subtract) \
                        .then_inc(subtracted, 1)
                    if not last:
                        exclude_self(n + 1, 1 - u, j)

            nc.gpsimd.memset(factors[:, 0:1], -1.0)
            nc.gpsimd.memset(factors[:, 1:2], STEEP).then_inc(gate["pool"], 1)
            pool.wait_ge(gate["pool"], 1)
            for j in range(T):
                exclude_self(0, 0, j)
            head(0, 0)
            with pool.Fori(0, in_loop // 2) as i:
                head(i * 2 + 1, 1)
                head(i * 2 + 2, 0)
            head(NH - 3, 1)
            head(NH - 2, 0)
            head(NH - 1, 1, last=True)

        @block.vector
        def _(dve):
            count, done = [0], [0, 0]
            PASSES = 2 * (TOPK // 8) - 1

            def step(n, u, j, k):
                if k == 0:
                    dve.wait_ge(s_ready, n * T + j + 1)
                    dve.sem_inc(gate["dve"], 1)
                elif done[j % 2]:
                    dve.wait_ge(chain, done[j % 2])
                eight = largest[:, j, k // 2 * 8:k // 2 * 8 + 8]
                source = left[j % 2][:, :] if k >= 2 else scores[u][:, j, :]
                if k % 2:
                    done_pass = nc.vector.match_replace(left[j % 2][:, :], eight, source, REMOVED)
                else:
                    done_pass = nc.vector.max(eight, source)
                if k == PASSES - 1:
                    done_pass.then_inc(found, 1)
                else:
                    done_pass.then_inc(chain, 1)
                    count[0] += 1
                    done[j % 2] = count[0]

            def head(n, u, first=False):
                for k in range(T // 2 * PASSES):
                    step(n, u, k // PASSES * 2, k % PASSES)
                    behind = k - PASSES // 2
                    if behind >= 0:
                        step(n, u, behind // PASSES * 2 + 1, behind % PASSES)
                    elif not first:
                        step(None, 1 - u, T - 1, behind + PASSES)

            def restart():
                dve.wait_ge(chain, done[1])
                dve.sem_clear(chain)
                count[0], done[0], done[1] = 0, 0, 0

            for u in range(2):
                nc.vector.memset(x_in[u][D:D + 1, :], 1.0)
                nc.vector.memset(vals[u][:, :, :], 0.0)
                nc.vector.memset(qT[u][:, :], 0.0)
                nc.vector.memset(kT[u][:, :], 0.0)
                nc.vector.memset(ps_t[u][:, S:S + P], 0.0).then_inc(cleared, 1)
            dve.wait_ge(cleared, 2)
            for u in range(2):
                last = nc.vector.memset(vals[u][:, 0:T, HD:HV], 1.0)
                last = nc.vector.memset(vals[u][0:M, T, HD:HV], 1.0)
            last.then_inc(made, 1)
            dve.wait_ge(made, 1)
            head(0, 0, first=True)
            restart()
            with dve.Fori(0, in_loop // 2) as i:
                head(i * 2 + 1, 1)
                head(i * 2 + 2, 0)
                restart()
            head(NH - 3, 1)
            head(NH - 2, 0)
            head(NH - 1, 1)
            for k in range(PASSES - PASSES // 2, PASSES):
                step(None, 1, T - 1, k)


def routed_ffn(nc, a, t, out):
    with phase(nc) as (ctx, take):
        def sb(name, shape, dt=F32):
            return [ctx.enter_context(nc.sbuf_tensor(f"d_{name}{u}", shape, dt)) for u in range(2)]

        def ps(name, shape):
            return [ctx.enter_context(nc.psum_tensor(f"d_{name}{u}", shape, F32)) for u in range(2)]

        def sem(name):
            return [take(nc.alloc_semaphore(f"d_{name}{u}")) for u in range(2)]

        w_routed = sb("w_routed", [P, T, 2, HID + 1])
        bias = sb("bias", [P, T, 2])
        inv = sb("inv", [P, H, T])
        attended = sb("attended", [P, T, H * HD])
        attendedT = sb("attendedT", [P, 2, S])
        h, xn, result = sb("h", [P, T, D]), sb("xn", [P, T, D]), sb("result", [P, T, D])
        stats, mean_var = sb("stats", [P, T, 6]), sb("mean_var", [P, T, 2])
        var_eps, rstd = sb("var_eps", [P, T]), sb("rstd", [P, T])
        xT = sb("xT", [D, S])
        g = [sb(f"g{l}_", [HID, S]) for l in range(3)]
        ps_a = ps("ps_a", [P, 2 * S])
        ps_g, ps_y = ps("ps_g", [P, S]), ps("ps_y", [P, S])
        w_loaded, bias_ready, attended_ready, aT_ps, aT_sb = (sem("w_loaded"), sem("bias_ready"),
                                                              sem("attended_ready"), sem("aT_ps"), sem("aT_sb"))
        y_ps, var, rstd_ready, xn_ready, xT_ps, xT_sb = (sem("y_ps"), sem("var"), sem("rstd_ready"), sem("xn_ready"),
                                                         sem("xT_ps"), sem("xT_sb"))
        g_ps, g_sb, out_ps, result_ready, stored = sem("g_ps"), sem("g_sb"), sem("out_ps"), sem("result_ready"), sem("stored")
        chain = take(nc.alloc_semaphore("d_chain"))
        gate = {e: take(nc.alloc_semaphore(f"d_gate_{e}")) for e in ("dve", "pe")}
        block = ctx.enter_context(nc.Block())

        @block.sync
        def _(sp):
            for u in range(2):
                sp.sem_inc(stored[u], 16)
            with sp.Fori(0, PAIRS) as i:
                for u in range(2):
                    sp.wait_ge(out_ps[u], i + 1)
                    for j in range(T):
                        route = sp.value_load(t["route_row"][0:1, bass.ds(i * (2 * T) + u * T + j, 1)],
                                              min_val=0, max_val=R - 1)
                        sp.dma_start(w_routed[u][:, j, :, :].rearrange("p l c -> p (l c)"),
                                     a["w_routed"][bass.ds(route, 1), :, :].rearrange("r p c -> (r p) c")) \
                            .then_inc(w_loaded[u], 16)
                for u in range(2):
                    sp.wait_ge(result_ready[u], i + 2)
                    sp.dma_start(out[bass.ds(i * 2 + u, 1), :, :].rearrange("b (j p) d -> p (b j) d", p=P),
                                 result[u][:, :, :]).then_inc(stored[u], 16)
            for u in range(2):
                sp.wait_ge(stored[u], 16 * (PAIRS + 1))

        @block.gpsimd
        def _(pool):
            with pool.Fori(0, PAIRS) as i:
                for u in range(2):
                    pool.wait_ge(w_loaded[u], i * (16 * T) + 16 * T)
                    for j in range(T):
                        last = nc.gpsimd.tensor_tensor(bias[u][:, j, :], w_routed[u][:, j, :, HID], t["b_shared"][:, :],
                                                       ALU.add)
                    last.then_inc(bias_ready[u], 1)
                for u in range(2):
                    pool.wait_ge(var[u], i + 1)
                    nc.gpsimd.tensor_tensor(rstd[u][:, :], var_eps[u][:, :], t["minus_half"][:, :], ALU.pow) \
                        .then_inc(rstd_ready[u], 1)

        @block.vector
        def _(dve):
            count = [0]

            def link(ins):
                count[0] += 1
                ins.then_inc(chain, 1)
                dve.wait_ge(chain, count[0])

            for u in range(2):
                dve.sem_inc(result_ready[u], 1)
            with dve.Fori(0, PAIRS) as i:
                count[0] = 0
                for u in range(2):
                    ours = t["heads"][:, bass.ds(i * (2 * H * OW) + u * H * OW, H * OW)] \
                        .rearrange("p (h j c) -> p h j c", h=H, j=T)
                    link(nc.vector.reciprocal(inv[u][:, :, :], ours[:, :, :, HD]))
                    for j in range(T):
                        last = nc.vector.tensor_tensor(
                            attended[u][:, j, :].rearrange("p (h c) -> p h c", h=H), ours[:, :, j, 0:HD],
                            spread(inv[u][:, :, j], HD), ALU.mult)
                    last.then_inc(attended_ready[u], 1)
                for u in range(2):
                    dve.wait_ge(y_ps[u], i + 1)
                    dve.sem_inc(gate["dve"], 1)
                    link(nc.vector.tensor_tensor(h[u][:, :, :], ps_y[u][:, 0:T * D].rearrange("p (j d) -> p j d", j=T),
                                                 t["hidden"][:, bass.ds(i * (2 * T) + u * T, T), :], ALU.add))
                    for j in range(T):
                        last = nc.vector.bn_stats(stats[u][:, j, :], h[u][:, j, :])
                    link(last)
                    for j in range(T):
                        last = nc.vector.bn_aggr(mean_var[u][:, j, :], stats[u][:, j, :])
                    link(last)
                    nc.vector.tensor_scalar(var_eps[u][:, :], mean_var[u][:, :, 1], EPS, None, ALU.add).then_inc(var[u], 1)
                for u in range(2):
                    dve.wait_ge(rstd_ready[u], i + 1)
                    for j in range(T):
                        last = nc.vector.tensor_scalar(xn[u][:, j, :], h[u][:, j, :], mean_var[u][:, j, 0:1],
                                                       rstd[u][:, j:j + 1], ALU.subtract, ALU.mult)
                    last.then_inc(xn_ready[u], 1)
                for u in range(2):
                    dve.wait_ge(out_ps[u], i + 2)
                    dve.sem_inc(gate["dve"], 1)
                    dve.wait_ge(stored[u], i * 16 + 16)
                    nc.vector.tensor_tensor(result[u][:, :, :], h[u][:, :, :],
                                            ps_y[u][:, 0:T * D].rearrange("p (j d) -> p j d", j=T), ALU.add) \
                        .then_inc(result_ready[u], 1)
                dve.sem_clear(chain)

        @block.tensor
        def _(pe):
            def rows(u, lhs, rhs, b_row):
                for j in range(T):
                    for c, (l, r) in enumerate(zip(lhs, rhs)):
                        nc.tensor.matmul(ps_y[u][:, j * D:(j + 1) * D], l[:, j * P:(j + 1) * P], r, start=(c == 0),
                                         stop=False)
                    last = nc.tensor.matmul(ps_y[u][:, j * D:(j + 1) * D], t["ones_row"][:, :], b_row, start=False,
                                            stop=True)
                return last

            for u in range(2):
                pe.sem_inc(out_ps[u], 1)
            with pe.Fori(0, PAIRS) as i:
                for u in range(2):
                    pe.wait_ge(attended_ready[u], i + 1)
                    for c in range(2):
                        for j in range(T):
                            last = nc.tensor.transpose(ps_a[u][:, c * S + j * P:c * S + (j + 1) * P],
                                                       attended[u][:, j, c * P:(c + 1) * P], t["ident"][:, :])
                    last.then_inc(aT_ps[u], 1)
                for u in range(2):
                    pe.wait_ge(aT_sb[u], i + 1)
                    pe.wait_ge(result_ready[u], i + 1)
                    rows(u, [attendedT[u][:, c, :] for c in range(2)], [t["w_proj"][:, c, :] for c in range(2)],
                         t["b_proj"][:, :]).then_inc(y_ps[u], 1)
                for u in range(2):
                    pe.wait_ge(xn_ready[u], i + 1)
                    pe.sem_inc(gate["pe"], 1)
                    for j in range(T):
                        last = nc.tensor.transpose(ps_a[u][0:D, j * P:(j + 1) * P], xn[u][:, j, :], t["ident"][:, :])
                    last.then_inc(xT_ps[u], 1)
                for u in range(2):
                    pe.wait_ge(xT_sb[u], i + 1)
                    nc.tensor.matmul(ps_g[u][:, :], t["w_inT"][:, :], xT[u][:, :], start=True, stop=True) \
                        .then_inc(g_ps[u], 1)
                for l in range(2):
                    for u in range(2):
                        pe.wait_ge(g_sb[u], i * 3 + l + 1)
                        pe.wait_ge(w_loaded[u], i * (16 * T) + 16 * T)
                        nc.tensor.matmul(ps_g[u][:, :], t["w_shared"][:, l, :], g[l][u][:, :], start=True, stop=False)
                        for j in range(T):
                            last = nc.tensor.matmul(ps_g[u][:, j * P:(j + 1) * P], w_routed[u][:, j, l, 0:HID],
                                                    g[l][u][:, j * P:(j + 1) * P], start=False, stop=(j == T - 1))
                        last.then_inc(g_ps[u], 1)
                for u in range(2):
                    pe.wait_ge(g_sb[u], i * 3 + 3)
                    rows(u, [g[2][u][:, :]], [t["w_outT"][:, :]], t["b_out"][:, :]).then_inc(out_ps[u], 1)

        @block.scalar
        def _(act):
            with act.Fori(0, PAIRS) as i:
                for u in range(2):
                    act.wait_ge(aT_ps[u], i + 1)
                    nc.scalar.activation(attendedT[u][:, :, :], ps_a[u][:, :].rearrange("p (c q) -> p c q", c=2),
                                         ACT.Copy).then_inc(aT_sb[u], 1)
                for u in range(2):
                    act.wait_ge(xT_ps[u], i + 1)
                    nc.scalar.activation(xT[u][:, :], ps_a[u][0:D, 0:S], ACT.Copy).then_inc(xT_sb[u], 1)
                for u in range(2):
                    act.wait_ge(g_ps[u], i * 3 + 1)
                    nc.scalar.activation(g[0][u][:, :], ps_g[u][:, :], ACT.Relu, bias=t["b_in"][:, :]).then_inc(g_sb[u], 1)
                for l in range(2):
                    for u in range(2):
                        act.wait_ge(g_ps[u], i * 3 + l + 2)
                        act.wait_ge(bias_ready[u], i + 1)
                        for j in range(T):
                            last = nc.scalar.activation(g[l + 1][u][:, j * P:(j + 1) * P], ps_g[u][:, j * P:(j + 1) * P],
                                                        ACT.Relu, bias=bias[u][:, j, l:l + 1])
                        last.then_inc(g_sb[u], 1)


def kernel(**inputs):
    import numpy as np
    import concourse.bacc as bacc
    from concourse.bass_utils import run_bass_kernel_spmd as run

    v = {name: np.asarray(x) for name, x in inputs.items()}
    row = lambda x: x.reshape(1, -1)
    w_heads = np.concatenate([v["L1_attn_w_qkv"], row(v["L1_attn_b_qkv"])]).reshape(D + 1, 3, H, HD) \
        .transpose(0, 2, 1, 3).reshape(D + 1, H, 3 * HD)
    w_routed = np.concatenate([v["L1_ffn_Wr"].transpose(1, 3, 0, 2), v["L1_ffn_br"].transpose(1, 2, 0)[..., None]], axis=3)
    arrays = {
        "token_ids": v["x"].reshape(NT, P).T,
        "table": v["L0_tok_W"].T,
        "L0_attn_Wq": v["L0_attn_Wq"],
        "L0_attn_Wk": v["L0_attn_Wk"],
        "wv0T": v["L0_attn_Wv"].T,
        "L0_ffn_Wr": v["L0_ffn_Wr"],
        "L0_ffn_br": row(v["L0_ffn_br"]),
        "L0_ffn_W1": v["L0_ffn_W1"],
        "w2_b1": np.concatenate([v["L0_ffn_W2"], v["L0_ffn_b1"][..., None]], axis=2),
        "L0_ffn_b2": v["L0_ffn_b2"],
        "L0_ffn_gamma": v["L0_ffn_gamma"],
        "L0_ffn_beta": v["L0_ffn_beta"],
        "w_qk": w_heads[:, :, 0:2 * HD],
        "w_v": w_heads[:, :, 2 * HD:],
        "w_qT": w_heads[:, :, 0:HD].transpose(2, 1, 0),
        "L1_attn_scale": v["L1_attn_scale"].reshape(-1),
        "mem_kT": v["L1_attn_mem_k"].transpose(2, 0, 1),
        "mem_v": v["L1_attn_mem_v"].transpose(1, 0, 2),
        "w_proj": v["L1_attn_w_proj"].reshape(2, P, D).transpose(1, 0, 2),
        "L1_attn_b_proj": row(v["L1_attn_b_proj"]),
        "w_inT": v["L1_ffn_Wi"].T,
        "b_in": v["L1_ffn_bi"].reshape(-1, 1),
        "w_routed": w_routed.reshape(R, HID, 2 * (HID + 1)),
        "w_shared": v["L1_ffn_Ws"].reshape(2, HID, HID).transpose(2, 0, 1),
        "b_shared": v["L1_ffn_bs"].reshape(2, HID).T,
        "w_outT": v["L1_ffn_Wo"].T,
        "L1_ffn_bo": row(v["L1_ffn_bo"]),
        "L1_ffn_route_id": row(v["L1_ffn_route_id"]),
    }
    nc = bacc.Bacc("TRN2", target_bir_lowering=False, num_devices=1)
    feed, aps = {}, {}
    for name, x in arrays.items():
        feed["in_" + name] = np.ascontiguousarray(x)
        aps[name] = nc.dram_tensor("in_" + name, x.shape, mybir.dt.from_np(x.dtype), kind="ExternalInput").ap()
    out = nc.dram_tensor("out", (B, S, D), F32, kind="ExternalOutput").ap()
    tower(nc, aps, out)
    return run(nc, [feed], core_ids=[0]).results[0]["out"]
```

```python
from contextlib import ExitStack, contextmanager

import concourse.bass as bass
from concourse import mybir

F32 = mybir.dt.float32
I32 = mybir.dt.int32
U32 = mybir.dt.uint32
ALU = mybir.AluOpType
ACT = mybir.ActivationFunctionType
AX = mybir.AxisListType

P = 128
B, S, D = 16, 512, 64
T = S // P
NT = B * T
EPS = 1e-5
E0, F0 = 8, 128
CAPACITY = 1280.0
H, HD, M = 8, 32, 4
SK = S + M
TOPK = 32
R, HID = 16, 128
HV = HD + 1
VM = HD + M
OW = T * HV
NH = B * H
FILL = -(2.0 ** 64)
STEEP = 2.0 ** 62
REMOVED = -3.0e38
PAIRS = B // 2


def spread(ap, width):
    return ap.unsqueeze(2).to_broadcast([ap.shape[0], ap.shape[1], width])


def tower(nc, a, out):
    ctx = ExitStack()
    with ctx:
        def sb(name, shape, dt=F32):
            return ctx.enter_context(nc.sbuf_tensor(name, shape, dt))

        t = {}
        t["hidden"] = sb("hidden", [P, NT, D])
        t["normed"] = sb("normed", [P, NT, D])
        t["normedT"] = sb("normedT", [P, B * S])
        t["heads"] = sb("heads", [P, NH * OW])
        t["ident"] = sb("ident", [P, P])
        t["ones_row"] = sb("ones_row", [1, P])
        t["minus_half"] = sb("minus_half", [P, T])
        t["token_ids"] = sb("token_ids", [P, NT], I32)
        t["gathered_rows"] = sb("gathered_rows", [P, 2 * T, D])
        t["mix_qk"] = sb("mix_qk", [P, D])
        t["wv0T"] = sb("wv0T", [P, D])
        t["token_sums"] = sb("token_sums", [D, B])
        t["w_route"] = sb("w_route", [D, E0])
        t["b_route"] = sb("b_route", [1, E0])
        t["gate_cols"] = sb("gate_cols", [P, 2 * B])
        t["expert_row"] = sb("expert_row", [1, 2 * B], U32)
        t["gamma"] = sb("gamma", [P, 2 * T, D])
        t["beta"] = sb("beta", [P, 2 * T, D])
        t["w_qk"] = sb("w_qk", [D + 1, H, 2 * HD])
        t["w_vm"] = sb("w_vm", [D + 1, H, VM])
        t["mem_v"] = sb("mem_v", [M, H, HD])
        t["w_proj"] = sb("w_proj", [P, 2, D])
        t["b_proj"] = sb("b_proj", [D, 1])
        t["w_inT"] = sb("w_inT", [P, HID])
        t["b_in"] = sb("b_in", [HID, 1])
        t["w_shared"] = sb("w_shared", [HID, 2, HID + 1])
        t["w_outT"] = sb("w_outT", [HID, D])
        t["b_out"] = sb("b_out", [D, 1])
        t["route_row"] = sb("route_row", [1, B * T], I32)

        setup(nc, a, t)
        attention0(nc, a, t)
        router(nc, t)
        experts(nc, a, t)
        attention1(nc, t)
        routed_ffn(nc, a, t, out)


@contextmanager
def phase(nc):
    taken = []

    def take(semaphore):
        taken.append(semaphore)
        return semaphore

    with ExitStack() as ctx:
        yield ctx, take
    nc.clear_and_free_semaphores(taken)
    nc.all_engine_barrier()


def setup(nc, a, t):
    with phase(nc) as (ctx, take):
        wq = ctx.enter_context(nc.sbuf_tensor("wq", [D, D], F32))
        wk = ctx.enter_context(nc.sbuf_tensor("wk", [D, D], F32))
        q_scale = ctx.enter_context(nc.sbuf_tensor("q_scale", [D + 1, H], F32))
        mem_scale = ctx.enter_context(nc.sbuf_tensor("mem_scale", [HD, H], F32))
        mem_kT = ctx.enter_context(nc.sbuf_tensor("mem_kT", [HD, H, M], F32))
        w_qT = ctx.enter_context(nc.sbuf_tensor("w_qT", [HD, H, D + 1], F32))
        ps_mem = ctx.enter_context(nc.psum_tensor("ps_mem", [D + 1, H, M], F32))
        ps_mix = ctx.enter_context(nc.psum_tensor("ps_mix", [D, D], F32))
        sem = lambda name: take(nc.alloc_semaphore(name))
        loaded, cleared, made = sem("loaded"), sem("cleared"), sem("made")
        ids_loaded, gathered = sem("ids_loaded"), sem("gathered")
        mixed, scaled, copied = sem("mixed"), sem("scaled"), sem("copied")
        block = ctx.enter_context(nc.Block())
        loads = [
            (wq[:, :], a["L0_attn_Wq"]),
            (wk[:, :], a["L0_attn_Wk"]),
            (q_scale[:, :], a["L1_attn_scale"].partition_broadcast(D + 1)),
            (t["wv0T"][:, :], a["wv0T"]),
            (t["w_route"][:, :], a["L0_ffn_Wr"]),
            (t["b_route"][:, :], a["L0_ffn_br"]),
            (t["gamma"][:, :, :].rearrange("p j d -> p (j d)"), a["gammas"].partition_broadcast(P)),
            (t["beta"][:, :, :].rearrange("p j d -> p (j d)"), a["betas"].partition_broadcast(P)),
            (mem_scale[:, :], a["L1_attn_scale"].partition_broadcast(HD)),
            (t["w_qk"][:, :, :], a["w_qk"]),
            (t["w_vm"][:, :, 0:HD], a["w_v"]),
            (w_qT[:, :, :], a["w_qT"]),
            (mem_kT[:, :, :], a["mem_kT"]),
            (t["mem_v"][:, :, :], a["mem_v"]),
            (t["w_proj"][:, :, :], a["w_proj"]),
            (t["b_proj"][:, :], a["L1_attn_b_proj"]),
            (t["w_inT"][:, :], a["w_inT"]),
            (t["b_in"][:, :], a["b_in"]),
            (t["w_shared"][:, :, :], a["w_shared"]),
            (t["w_outT"][:, :], a["w_outT"]),
            (t["b_out"][:, :], a["L1_ffn_bo"]),
            (t["route_row"][:, :], a["L1_ffn_route_id"]),
        ]

        @block.sync
        def _(sp):
            sp.dma_start(t["token_ids"][:, :], a["token_ids"]).then_inc(ids_loaded, 16)
            for dst, src in loads[0::2]:
                sp.dma_start(dst, src).then_inc(loaded, 16)
            sp.wait_ge(loaded, 16 * len(loads))

        @block.gpsimd
        def _(pool):
            nc.gpsimd.memset(t["ident"][:, :], 0.0).then_inc(cleared, 1)
            nc.gpsimd.memset(t["ones_row"][:, :], 1.0)
            nc.gpsimd.memset(t["minus_half"][:, :], -0.5)
            pool.wait_ge(cleared, 1)
            nc.gpsimd.affine_select(out=t["ident"][:, :], in_=t["ident"][:, :], compare_op=ALU.not_equal,
                                    fill=1.0, base=0, pattern=[[-1, P]], channel_multiplier=1).then_inc(made, 1)
            pool.wait_ge(made, 1)
            pool.wait_ge(ids_loaded, 16)
            for tile in range(2 * T):
                nc.gpsimd.indirect_dma_start(
                    out=t["gathered_rows"][:, tile, :], out_offset=None, in_=a["table"],
                    in_offset=bass.IndirectOffsetOnAxis(ap=t["token_ids"][:, tile:tile + 1].bitcast(U32), axis=0),
                ).then_inc(gathered, 16)
            pool.wait_ge(gathered, 2 * T * 16)

        @block.tensor
        def _(pe):
            pe.wait_ge(loaded, 16 * len(loads))
            nc.tensor.matmul(ps_mix[:, :], wq[:, :], wk[:, :], start=True, stop=True).then_inc(mixed, 1)
            pe.wait_ge(scaled, 5)
            for head in range(H):
                last = nc.tensor.matmul(ps_mem[:, head, :], w_qT[:, head, :], mem_kT[:, head, :], start=True, stop=True)
            last.then_inc(mixed, 1)

        @block.scalar
        def _(act):
            for dst, src in loads[1::2]:
                nc.scalar.dma_start(dst, src).then_inc(loaded, 16)
            act.wait_ge(mixed, 1)
            nc.scalar.activation(t["mix_qk"][0:D, :], ps_mix[:, :], ACT.Copy, scale=D ** -0.5).then_inc(copied, 1)
            act.wait_ge(mixed, 2)
            nc.scalar.activation(t["w_vm"][:, :, HD:VM], ps_mem[:, :, :], ACT.Copy).then_inc(copied, 1)
            act.wait_ge(copied, 2)

        @block.vector
        def _(dve):
            nc.vector.memset(t["mix_qk"][D:P, :], 0.0)
            nc.vector.memset(t["normedT"][D:P, :], 0.0).then_inc(scaled, 1)
            dve.wait_ge(loaded, 16 * len(loads))
            nc.vector.tensor_scalar(q_scale[:, :], q_scale[:, :], HD ** -0.5, None, ALU.mult).then_inc(scaled, 1)
            nc.vector.tensor_scalar(mem_scale[:, :], mem_scale[:, :], HD ** -0.5, None, ALU.mult).then_inc(scaled, 1)
            dve.wait_ge(scaled, 3)
            wq_part = t["w_qk"][:, :, 0:HD]
            nc.vector.tensor_tensor(wq_part, wq_part, spread(q_scale[:, :], HD), ALU.mult).then_inc(scaled, 1)
            nc.vector.tensor_tensor(mem_kT[:, :, :], mem_kT[:, :, :], spread(mem_scale[:, :], M), ALU.mult) \
                .then_inc(scaled, 1)
            dve.wait_ge(made, 1)
            for l in range(2):
                nc.vector.tensor_tensor(t["w_shared"][:, l, 0:HID], t["w_shared"][:, l, 0:HID], t["ident"][:, :],
                                        ALU.add).then_inc(scaled, 1)
            dve.wait_ge(scaled, 7)


def attention0(nc, a, t):
    with phase(nc) as (ctx, take):
        def sb(name, shape, dt=F32):
            return [ctx.enter_context(nc.sbuf_tensor(f"a_{name}{u}", shape, dt)) for u in range(2)]

        def ps(name, shape):
            return [ctx.enter_context(nc.psum_tensor(f"a_{name}{u}", shape, F32)) for u in range(2)]

        def sem(name):
            return [take(nc.alloc_semaphore(f"a_{name}{u}")) for u in range(2)]

        ids = sb("ids", [P, T], I32)
        gathered_rows = [t["gathered_rows"][:, u * T:(u + 1) * T, :] for u in range(2)]
        not_pad = ctx.enter_context(nc.sbuf_tensor("a_not_pad", [P, NT], F32))
        embedded, h = sb("embedded", [P, T, D]), sb("h", [P, T, D])
        stats = [sb(f"stats{k}_", [P, T, 6]) for k in range(2)]
        mean_var = [sb(f"mean_var{k}_", [P, T, 2]) for k in range(2)]
        var_eps, rstd = [sb(f"var_eps{k}_", [P, T]) for k in range(2)], [sb(f"rstd{k}_", [P, T]) for k in range(2)]
        xn, x2 = sb("xn", [P, T, D]), sb("x2", [P, T, D])
        xT, mixT = sb("xT", [P, S]), sb("mixT", [P, S])
        neg_max, weight_sum, inv_sum = sb("neg_max", [P, T]), sb("weight_sum", [P, T]), sb("inv_sum", [P, T])
        weights = [t["heads"][:, u * T * S:(u + 1) * T * S].rearrange("p (k q) -> p k q", k=T) for u in range(2)]
        values, oT = sb("values", [P, T, D]), sb("oT", [D, S])
        ps_x = ps("ps_x", [D, S])
        ps_vo = ps("ps_vo", [P, S])
        ps_sc = [ps(f"ps_sc{u}_", [P, S]) for u in range(2)]

        cleared = take(nc.alloc_semaphore("a_cleared"))
        ids_ready, gathered, rows_used, embedded_saved = (sem("ids_ready"), sem("gathered"), sem("rows_used"),
                                                          sem("embedded_saved"))
        var1, rstd1, xn_ready = sem("var1"), sem("rstd1"), sem("xn_ready")
        xT_ps, xT_sb, mix_ps, mix_sb = sem("xT_ps"), sem("xT_sb"), sem("mix_ps"), sem("mix_sb")
        v_ps, score_ps, max_ready, exp_ready = sem("v_ps"), sem("score_ps"), sem("max_ready"), sem("exp_ready")
        v_ready, o_ps, h_added, h_saved = sem("v_ready"), sem("o_ps"), sem("h_added"), sem("h_saved")
        var2, rstd2, x2_ready, x2_saved = sem("var2"), sem("rstd2"), sem("x2_ready"), sem("x2_saved")
        x2T_ps, x2T_saved = sem("x2T_ps"), sem("x2T_saved")
        oT_ps, oT_sb = sem("oT_ps"), sem("oT_sb")
        chain = take(nc.alloc_semaphore("a_chain"))
        gate = {e: take(nc.alloc_semaphore(f"a_gate_{e}")) for e in ("pool", "act", "dve", "pe")}
        block = ctx.enter_context(nc.Block())

        @block.gpsimd
        def _(pool):
            def gather(i, u):
                pool.wait_ge(rows_used[u], i + 1)
                pool.sem_inc(gate["pool"], 1)
                nc.gpsimd.tensor_copy(ids[u][:, :], t["token_ids"][:, bass.ds(i * (2 * T) + u * T, T)]) \
                    .then_inc(ids_ready[u], 1)
                pool.wait_ge(ids_ready[u], i + 1)
                pool.sem_inc(gate["pool"], 1)
                for j in range(T):
                    nc.gpsimd.indirect_dma_start(
                        out=gathered_rows[u][:, j, :], out_offset=None, in_=a["table"],
                        in_offset=bass.IndirectOffsetOnAxis(ap=ids[u][:, j:j + 1].bitcast(U32), axis=0),
                    ).then_inc(gathered[u], 16)

            def reciprocal_root(k, u, ready, done, number):
                pool.wait_ge(ready[u], number)
                nc.gpsimd.tensor_tensor(rstd[k][u][:, :], var_eps[k][u][:, :], t["minus_half"][:, :], ALU.pow) \
                    .then_inc(done[u], 1)

            def turn(i, ahead, front):
                if front:
                    for u in range(2):
                        reciprocal_root(0, u, var1, rstd1, i + 2)
                for u in range(2):
                    reciprocal_root(1, u, var2, rstd2, i + 1)
                    pool.wait_ge(h_added[u], i + 2)
                    pool.sem_inc(gate["pool"], 1)
                    nc.gpsimd.tensor_copy(t["hidden"][:, bass.ds(i * (2 * T) + u * T, T), :], h[u][:, :, :]) \
                        .then_inc(h_saved[u], 1)
                for u in range(2):
                    pool.wait_ge(x2_ready[u], i + 1)
                    pool.sem_inc(gate["pool"], 1)
                    nc.gpsimd.tensor_copy(t["normed"][:, bass.ds(i * (2 * T) + u * T, T), :], x2[u][:, :, :]) \
                        .then_inc(x2_saved[u], 1)
                if ahead:
                    for u in range(2):
                        gather(i + 2, u)

            for u in range(2):
                pool.sem_inc(h_saved[u], 1)
                pool.sem_inc(x2_saved[u], 1)
                pool.sem_inc(ids_ready[u], 1)
            for u in range(2):
                reciprocal_root(0, u, var1, rstd1, 1)
            for u in range(2):
                gather(1, u)
            with pool.Fori(0, PAIRS - 2) as i:
                turn(i, True, True)
            turn(PAIRS - 2, False, True)
            turn(PAIRS - 1, False, False)

        @block.vector
        def _(dve):
            count = [0]

            def link(ins):
                count[0] += 1
                ins.then_inc(chain, 1)
                dve.wait_ge(chain, count[0])

            def variance(k, u, x):
                for j in range(T):
                    last = nc.vector.bn_stats(stats[k][u][:, j, :], x[u][:, j, :])
                link(last)
                for j in range(T):
                    last = nc.vector.bn_aggr(mean_var[k][u][:, j, :], stats[k][u][:, j, :])
                link(last)
                return nc.vector.tensor_scalar(var_eps[k][u][:, :], mean_var[k][u][:, :, 1], EPS, None, ALU.add)

            def normalise(k, dst, x, u):
                for j in range(T):
                    last = nc.vector.tensor_scalar(dst[u][:, j, :], x[u][:, j, :], mean_var[k][u][:, j, 0:1],
                                                   rstd[k][u][:, j:j + 1], ALU.subtract, ALU.mult)
                return last

            def front(i, u, first=False):
                if not first:
                    dve.wait_ge(gathered[u], i * (16 * T))
                    dve.sem_inc(gate["dve"], 1)
                dve.wait_ge(embedded_saved[u], i + 1)
                dve.sem_inc(gate["dve"], 1)
                nc.vector.tensor_tensor(embedded[u][:, :, :], gathered_rows[u][:, :, :],
                                        spread(not_pad[:, bass.ds(i * (2 * T) + u * T, T)], D), ALU.mult) \
                    .then_inc(rows_used[u], 1)
                dve.wait_ge(rows_used[u], i + 2)
                dve.sem_inc(gate["dve"], 1)
                variance(0, u, embedded).then_inc(var1[u], 1)

            def norm1(i, u):
                dve.wait_ge(rstd1[u], i + 1)
                normalise(0, xn, embedded, u).then_inc(xn_ready[u], 1)

            def turn(i, ahead):
                for k in range(T):
                    for u in range(2):
                        dve.wait_ge(score_ps[u], i * T + k + 1)
                        nc.vector.tensor_reduce(neg_max[u][:, k:k + 1], ps_sc[u][k % 2][:, :], AX.X, ALU.max,
                                                negate=True).then_inc(max_ready[u], 1)
                for u in range(2):
                    dve.wait_ge(exp_ready[u], i * T + T)
                    link(nc.vector.reciprocal(inv_sum[u][:, :], weight_sum[u][:, :]))
                    dve.wait_ge(v_ps[u], i + 1)
                    nc.vector.tensor_tensor(values[u][:, :, :],
                                            ps_vo[u][:, 0:T * D].rearrange("p (k d) -> p k d", k=T),
                                            spread(inv_sum[u][:, :], D), ALU.mult).then_inc(v_ready[u], 1)
                if ahead:
                    for u in range(2):
                        front(i + 1, u)
                    for u in range(2):
                        norm1(i + 1, u)
                for u in range(2):
                    dve.wait_ge(h_saved[u], i + 1)
                    dve.sem_inc(gate["dve"], 1)
                    dve.wait_ge(embedded_saved[u], i + 2)
                    dve.sem_inc(gate["dve"], 1)
                    dve.wait_ge(o_ps[u], i + 1)
                    dve.sem_inc(gate["dve"], 1)
                    nc.vector.tensor_tensor(h[u][:, :, :], ps_vo[u][:, 0:T * D].rearrange("p (k d) -> p k d", k=T),
                                            t["hidden"][:, bass.ds(i * (2 * T) + u * T, T), :], ALU.add).then_inc(h_added[u], 1)
                    dve.wait_ge(h_added[u], i + 2)
                    dve.sem_inc(gate["dve"], 1)
                    variance(1, u, h).then_inc(var2[u], 1)
                for u in range(2):
                    dve.wait_ge(rstd2[u], i + 1)
                    dve.sem_inc(gate["dve"], 1)
                    dve.wait_ge(x2_saved[u], i + 1)
                    normalise(1, x2, h, u).then_inc(x2_ready[u], 1)
                dve.sem_clear(chain)
                count[0] = 0

            for u in range(2):
                dve.sem_inc(h_added[u], 1)
                dve.sem_inc(rows_used[u], 1)
            link(nc.vector.tensor_scalar(not_pad[:, :], t["token_ids"][:, :], 0.0, None, ALU.not_equal))
            for u in range(2):
                front(0, u, first=True)
                nc.vector.memset(xT[u][D:P, :], 0.0)
                nc.vector.memset(mixT[u][D:P, :], 0.0).then_inc(cleared, 1)
            for u in range(2):
                norm1(0, u)
            dve.sem_clear(chain)
            count[0] = 0
            with dve.Fori(0, PAIRS - 1) as i:
                turn(i, True)
            turn(PAIRS - 1, False)

        @block.tensor
        def _(pe):
            def to_features(u, x):
                for j in range(T):
                    last = nc.tensor.transpose(ps_x[u][:, j * P:(j + 1) * P], x[u][:, j, :], t["ident"][:, :])
                return last

            def front(i):
                for u in range(2):
                    pe.wait_ge(xn_ready[u], i + 1)
                    pe.sem_inc(gate["pe"], 1)
                    to_features(u, xn).then_inc(xT_ps[u], 1)
                for u in range(2):
                    pe.wait_ge(xT_sb[u], i + 1)
                    pe.sem_inc(gate["pe"], 1)
                    nc.tensor.matmul(ps_x[u][:, :], t["mix_qk"][:, :], xT[u][:, :], start=True, stop=True) \
                        .then_inc(mix_ps[u], 1)
                    pe.wait_ge(h_added[u], i + 1)
                    for k in range(T):
                        last = nc.tensor.matmul(ps_vo[u][:, k * D:(k + 1) * D], xT[u][:, k * P:(k + 1) * P],
                                                t["wv0T"][:, :], start=True, stop=True)
                    last.then_inc(v_ps[u], 1)

            def attend(i):
                for k in range(T):
                    for u in range(2):
                        if k == 0:
                            pe.wait_ge(mix_sb[u], i + 1)
                        if k >= 2:
                            pe.wait_ge(exp_ready[u], i * T + k - 1)
                        nc.tensor.matmul(ps_sc[u][k % 2][:, :], xT[u][:, k * P:(k + 1) * P], mixT[u][:, :],
                                         start=True, stop=True).then_inc(score_ps[u], 1)
                for u in range(2):
                    pe.wait_ge(x2T_saved[u], i + 1)
                    pe.wait_ge(v_ready[u], i + 1)
                    pe.sem_inc(gate["pe"], 1)
                    for k in range(T):
                        last = nc.tensor.matmul(ps_x[u][:, :], values[u][:, k, :], weights[u][:, k, :],
                                                start=(k == 0), stop=(k == T - 1))
                    last.then_inc(oT_ps[u], 1)
                for u in range(2):
                    pe.wait_ge(oT_sb[u], i + 1)
                    pe.sem_inc(gate["pe"], 1)
                    for j in range(T):
                        last = nc.tensor.transpose(ps_vo[u][:, j * D:(j + 1) * D], oT[u][:, j * P:(j + 1) * P],
                                                   t["ident"][0:D, 0:D])
                    last.then_inc(o_ps[u], 1)

            def tail(i, last=False):
                for u in range(2):
                    pe.wait_ge(x2_ready[u], i + 1)
                    if not last:
                        pe.wait_ge(mix_sb[u], i + 2)
                    pe.sem_inc(gate["pe"], 1)
                    to_features(u, x2).then_inc(x2T_ps[u], 1)

            pe.wait_ge(cleared, 2)
            front(0)
            with pe.Fori(0, PAIRS - 1) as i:
                attend(i)
                front(i + 1)
                tail(i)
            attend(PAIRS - 1)
            tail(PAIRS - 1, last=True)

        @block.scalar
        def _(act):
            def front(i):
                for u in range(2):
                    act.wait_ge(xT_ps[u], i + 1)
                    nc.scalar.activation(xT[u][0:D, :], ps_x[u][:, :], ACT.Copy).then_inc(xT_sb[u], 1)
                for u in range(2):
                    act.wait_ge(mix_ps[u], i + 1)
                    nc.scalar.activation(mixT[u][0:D, :], ps_x[u][:, :], ACT.Copy).then_inc(mix_sb[u], 1)

            def save_embedded(i, u):
                act.wait_ge(var1[u], i + 1)
                act.sem_inc(gate["act"], 1)
                nc.scalar.activation(t["hidden"][:, bass.ds(i * (2 * T) + u * T, T), :], embedded[u][:, :, :], ACT.Copy) \
                    .then_inc(embedded_saved[u], 1)

            def weigh(i, ahead):
                for k in range(T):
                    for u in range(2):
                        act.wait_ge(max_ready[u], i * T + k + 1)
                        nc.scalar.activation(weights[u][:, k, :], ps_sc[u][k % 2][:, :], ACT.Exp,
                                             bias=neg_max[u][:, k:k + 1], accum_out=weight_sum[u][:, k:k + 1]) \
                            .then_inc(exp_ready[u], 1)
                for u in range(2):
                    act.wait_ge(oT_ps[u], i + 1)
                    nc.scalar.activation(oT[u][:, :], ps_x[u][:, :], ACT.Copy).then_inc(oT_sb[u], 1)
                if ahead:
                    for u in range(2):
                        save_embedded(i + 1, u)

            def tail(i):
                for u in range(2):
                    act.wait_ge(x2T_ps[u], i + 1)
                    act.sem_inc(gate["act"], 1)
                    nc.scalar.activation(t["normedT"][0:D, bass.ds(i * (2 * S) + u * S, S)], ps_x[u][:, :], ACT.Copy,
                                         accum_out=t["token_sums"][:, bass.ds(i * 2 + u, 1)]) \
                        .then_inc(x2T_saved[u], 1)

            for u in range(2):
                act.sem_inc(x2T_saved[u], 1)
                act.sem_inc(embedded_saved[u], 1)
            act.wait_ge(cleared, 2)
            for u in range(2):
                save_embedded(0, u)
            front(0)
            with act.Fori(0, PAIRS - 1) as i:
                weigh(i, True)
                front(i + 1)
                tail(i)
            weigh(PAIRS - 1, False)
            tail(PAIRS - 1)


def router(nc, t):
    with phase(nc) as (ctx, take):
        def sb(name, shape, dt=F32):
            return ctx.enter_context(nc.sbuf_tensor("r_" + name, shape, dt))

        means = sb("means", [D, B])
        load_rows = sb("load_rows", [B, B])
        top, neg_top, total, inv = sb("top", [B, 1]), sb("neg_top", [B, 1]), sb("total", [B, 1]), sb("inv", [B, 1])
        probs, shrink = sb("probs", [B, E0]), sb("shrink", [B, E0])
        best, best_at = sb("best", [B, 8]), sb("best_at", [B, 8], U32)
        pair = sb("pair", [B, 2])
        gate_row = sb("gate_row", [1, 2 * B])
        ps_logits = ctx.enter_context(nc.psum_tensor("r_logits", [B, E0], F32))
        ps_loads = ctx.enter_context(nc.psum_tensor("r_loads", [B, E0], F32))
        ps_gates = ctx.enter_context(nc.psum_tensor("r_gates", [P, 2 * B], F32))
        sem = lambda name: take(nc.alloc_semaphore("r_" + name))
        means_ready, logits_ps, steps, exps = sem("means_ready"), sem("logits_ps"), sem("steps"), sem("exps")
        probs_ready, loads_ps, pair_ready, rows_in = sem("probs_ready"), sem("loads_ps"), sem("pair_ready"), sem("rows_in")
        max_ready, gates_ps = sem("max_ready"), sem("gates_ps")
        block = ctx.enter_context(nc.Block())

        @block.tensor
        def _(pe):
            pe.wait_ge(means_ready, 1)
            nc.tensor.matmul(ps_logits[:, :], means[:, :], t["w_route"][:, :], start=True, stop=False)
            nc.tensor.matmul(ps_logits[:, :], t["ones_row"][:, 0:B], t["b_route"][:, :], start=False, stop=True) \
                .then_inc(logits_ps, 1)
            pe.wait_ge(probs_ready, 1)
            nc.tensor.matmul(ps_loads[:, :], load_rows[:, :], probs[:, :], start=True, stop=True).then_inc(loads_ps, 1)
            pe.wait_ge(rows_in, 32)
            nc.tensor.matmul(ps_gates[:, :], t["ones_row"][:, :], gate_row[:, :], start=True, stop=True) \
                .then_inc(gates_ps, 1)

        @block.scalar
        def _(act):
            act.wait_ge(max_ready, 1)
            nc.scalar.activation(probs[:, :], ps_logits[:, :], ACT.Exp, bias=neg_top[:, :], accum_out=total[:, :]) \
                .then_inc(exps, 1)
            act.wait_ge(max_ready, 2)
            nc.scalar.activation(probs[:, :], shrink[:, :], ACT.Exp, bias=neg_top[:, :], accum_out=total[:, :]) \
                .then_inc(exps, 1)
            act.wait_ge(max_ready, 3)
            nc.scalar.activation(pair[:, :], best[:, 0:2], ACT.Exp, bias=neg_top[:, :], accum_out=total[:, :]) \
                .then_inc(exps, 1)
            act.wait_ge(gates_ps, 1)
            nc.scalar.activation(t["gate_cols"][:, :], ps_gates[:, :], ACT.Copy).then_inc(exps, 1)
            act.wait_ge(exps, 4)

        @block.vector
        def _(dve):
            count = [0]

            def link(ins):
                count[0] += 1
                ins.then_inc(steps, 1)
                dve.wait_ge(steps, count[0])

            nc.vector.memset(load_rows[:, :], float(S))
            nc.vector.tensor_scalar(means[:, :], t["token_sums"][:, :], 1.0 / S, None, ALU.mult).then_inc(means_ready, 1)
            dve.wait_ge(logits_ps, 1)
            nc.vector.tensor_reduce(neg_top[:, :], ps_logits[:, :], AX.X, ALU.max, negate=True).then_inc(max_ready, 1)
            dve.wait_ge(exps, 1)
            link(nc.vector.reciprocal(inv[:, :], total[:, :]))
            nc.vector.tensor_scalar(probs[:, :], probs[:, :], inv[:, :], None, ALU.mult).then_inc(probs_ready, 1)
            dve.wait_ge(probs_ready, 1)
            dve.wait_ge(loads_ps, 1)
            link(nc.vector.reciprocal(shrink[:, :], ps_loads[:, :]))
            link(nc.vector.tensor_scalar(shrink[:, :], shrink[:, :], CAPACITY, 1.0, ALU.mult, ALU.min))
            link(nc.vector.tensor_tensor(shrink[:, :], shrink[:, :], probs[:, :], ALU.mult))
            nc.vector.tensor_reduce(neg_top[:, :], shrink[:, :], AX.X, ALU.max, negate=True).then_inc(max_ready, 1)
            dve.wait_ge(exps, 2)
            link(nc.vector.reciprocal(inv[:, :], total[:, :]))
            link(nc.vector.tensor_scalar(probs[:, :], probs[:, :], inv[:, :], None, ALU.mult))
            link(nc.vector.max(best[:, :], probs[:, :]))
            link(nc.vector.max_index(best_at[:, :], best[:, :], probs[:, :]))
            nc.vector.tensor_scalar(neg_top[:, :], best[:, 0:1], -1.0, None, ALU.mult).then_inc(max_ready, 1)
            dve.wait_ge(exps, 3)
            link(nc.vector.reciprocal(inv[:, :], total[:, :]))
            nc.vector.tensor_scalar(pair[:, :], pair[:, :], inv[:, :], None, ALU.mult).then_inc(pair_ready, 1)

        @block.sync
        def _(sp):
            sp.wait_ge(pair_ready, 1)
            sp.dma_start(gate_row[:, :].rearrange("a (b k) -> a b k", k=2), pair[:, :]).then_inc(rows_in, 16)
            sp.dma_start(t["expert_row"][:, :].rearrange("a (b k) -> a b k", k=2), best_at[:, 0:2]).then_inc(rows_in, 16)
            sp.wait_ge(rows_in, 32)


def experts(nc, a, t):
    with phase(nc) as (ctx, take):
        TILES = 2 * T

        def sb(name, shape):
            return ctx.enter_context(nc.sbuf_tensor("e_" + name, shape, F32))

        def ps(name, shape):
            return ctx.enter_context(nc.psum_tensor("e_" + name, shape, F32))

        def sem(name):
            return take(nc.alloc_semaphore("e_" + name))

        w1 = [sb(f"w1_{v}", [P, 4, F0]) for v in range(2)]
        w2 = [sb(f"w2_{v}", [F0, 4, D + 1]) for v in range(2)]
        b2 = [sb(f"b2_{v}", [D, 4]) for v in range(2)]
        w2g, b2g, bias = sb("w2g", [F0, 4, D]), sb("b2g", [D, 4]), sb("bias", [D, 2])
        yT = [sb(f"yT{u}", [D, S]) for u in range(2)]
        act_h = sb("act_h", [F0, 4, S])
        r, y, h, x3 = (sb(name, [P, TILES, D]) for name in ("r", "y", "h", "x3"))
        hidden_beta = sb("hidden_beta", [P, TILES, D])
        stats, mean_var = sb("stats", [P, TILES, 6]), sb("mean_var", [P, TILES, 2])
        var_eps, rstd = sb("var_eps", [P, TILES]), sb("rstd", [P, TILES])
        ps_h = [ps(f"ps_h{c}", [F0, S]) for c in range(4)]
        ps_y = ps("ps_y", [P, TILES, D])
        ps_x = [ps(f"ps_x{u}", [D, S]) for u in range(2)]
        cleared = sem("cleared")
        w_loaded = [sem(f"w_loaded{v}") for v in range(2)]
        w2_gated, h_ps, gelu_ready, y_ps, r_ready = (sem("w2_gated"), sem("h_ps"), sem("gelu_ready"), sem("y_ps"),
                                                     sem("r_ready"))
        beta_added, var_ready, rstd_ready, h_ready, h_saved = (sem("beta_added"), sem("var_ready"), sem("rstd_ready"),
                                                               sem("h_ready"), sem("h_saved"))
        yT_ps, yT_sb = sem("yT_ps"), sem("yT_sb")
        x3_ready, x3T_ps, x3T_saved = sem("x3_ready"), sem("x3T_ps"), sem("x3T_saved")
        chain = sem("chain")
        gate = {e: sem(f"gate_{e}") for e in ("pool", "act", "dve", "pe")}
        block = ctx.enter_context(nc.Block())
        LOADED = 12 * 16

        @block.sync
        def _(sp):
            with sp.Fori(0, PAIRS // 2) as i:
                for v in range(2):
                    sp.wait_ge(y_ps, i * 2 + v + 1)
                    for c in range(4):
                        e = sp.value_load(t["expert_row"][0:1, bass.ds(i * 8 + 4 * v + c, 1)], min_val=0, max_val=E0 - 1)
                        sp.dma_start(w1[v][0:D, c, :], a["L0_ffn_W1"][bass.ds(e, 1), :, :].rearrange("e d f -> (e d) f")) \
                            .then_inc(w_loaded[v], 16)
                        sp.dma_start(w2[v][:, c, :], a["w2_b1"][bass.ds(e, 1), :, :].rearrange("e f d -> (e f) d")) \
                            .then_inc(w_loaded[v], 16)
                        sp.dma_start(b2[v][:, c:c + 1], a["b2"][bass.ds(e, 1), :, :].rearrange("e d o -> (e d) o")).then_inc(w_loaded[v], 16)

        @block.tensor
        def _(pe):
            def front(n, v, times):
                pe.wait_ge(w_loaded[v], times * LOADED)
                pe.sem_inc(gate["pe"], 1)
                for c in range(4):
                    nc.tensor.matmul(ps_h[c][:, :], w1[v][:, c, :], t["normedT"][:, bass.ds(n * (2 * S) + c // 2 * S, S)],
                                     start=True, stop=True).then_inc(h_ps, 1)
                pe.wait_ge(w2_gated, n + 1)
                for u in range(2):
                    pe.wait_ge(gelu_ready, n * 2 + u + 1)
                    for k in range(2):
                        last = nc.tensor.matmul(ps_h[2 * u][0:D, :], w2g[:, 2 * u + k, :], act_h[:, 2 * u + k, :],
                                                start=(k == 0), stop=(k == 1))
                    last.then_inc(yT_ps, 1)
                pe.wait_ge(r_ready, n + 1)
                for u in range(2):
                    pe.wait_ge(yT_sb, n * 2 + u + 1)
                    pe.sem_inc(gate["pe"], 1)
                    for j in range(T):
                        last = nc.tensor.transpose(ps_y[:, u * T + j, :], yT[u][:, j * P:(j + 1) * P],
                                                   t["ident"][0:D, 0:D])
                last.then_inc(y_ps, 1)

            def tail(n):
                for u in range(2):
                    pe.wait_ge(x3_ready, n * 2 + u + 1)
                    pe.sem_inc(gate["pe"], 1)
                    pe.wait_ge(x3T_saved, n * 2 + u + 1)
                    pe.sem_inc(gate["pe"], 1)
                    for j in range(T):
                        last = nc.tensor.transpose(ps_x[u][:, j * P:(j + 1) * P], x3[:, u * T + j, :], t["ident"][:, :])
                    last.then_inc(x3T_ps, 1)

            pe.wait_ge(cleared, 2)
            pe.sem_inc(y_ps, 2)
            pe.sem_inc(x3T_ps, 1)
            front(0, 0, 1)
            with pe.Fori(0, PAIRS // 2 - 1) as i:
                front(i * 2 + 1, 1, i + 1)
                tail(i * 2)
                front(i * 2 + 2, 0, i + 2)
                tail(i * 2 + 1)
            front(PAIRS - 1, 1, PAIRS // 2)
            tail(PAIRS - 2)
            tail(PAIRS - 1)

        @block.scalar
        def _(act):
            def front(n, v):
                for u in range(2):
                    for k in range(2):
                        act.wait_ge(h_ps, n * 4 + 2 * u + k + 1)
                        last = nc.scalar.activation(act_h[:, 2 * u + k, :], ps_h[2 * u + k][:, :], ACT.Gelu,
                                                    bias=w2[v][:, 2 * u + k, D:D + 1])
                    last.then_inc(gelu_ready, 1)
                for u in range(2):
                    act.wait_ge(yT_ps, n * 2 + u + 1)
                    nc.scalar.activation(yT[u][:, :], ps_h[2 * u][0:D, :], ACT.Identity, bias=bias[:, u:u + 1]) \
                        .then_inc(yT_sb, 1)

            def tail(n):
                for u in range(2):
                    act.wait_ge(x3T_ps, n * 2 + u + 2)
                    act.sem_inc(gate["act"], 1)
                    nc.scalar.activation(t["normedT"][0:D, bass.ds(n * (2 * S) + u * S, S)], ps_x[u][:, :], ACT.Copy) \
                        .then_inc(x3T_saved, 1)

            act.sem_inc(x3T_saved, 2)
            front(0, 0)
            with act.Fori(0, PAIRS // 2 - 1) as i:
                front(i * 2 + 1, 1)
                tail(i * 2)
                front(i * 2 + 2, 0)
                tail(i * 2 + 1)
            front(PAIRS - 1, 1)
            tail(PAIRS - 2)
            tail(PAIRS - 1)

        @block.vector
        def _(dve):
            count = [0]

            def link(ins):
                count[0] += 1
                ins.then_inc(chain, 1)
                dve.wait_ge(chain, count[0])

            def variance(x):
                for u in range(2):
                    tiles = range(u * T, (u + 1) * T)
                    for j in tiles:
                        last = nc.vector.bn_stats(stats[:, j, :], x[:, j, :])
                    link(last)
                    for j in tiles:
                        last = nc.vector.bn_aggr(mean_var[:, j, :], stats[:, j, :])
                    link(last)
                    nc.vector.tensor_scalar(var_eps[:, u * T:(u + 1) * T], mean_var[:, u * T:(u + 1) * T, 1], EPS, None,
                                            ALU.add).then_inc(var_ready, 1)

            def normalise(dst, x, roots, done=None):
                for j in range(TILES):
                    if j % T == 0:
                        dve.wait_ge(rstd_ready, roots + j // T + 1)
                    last = nc.vector.tensor_scalar(dst[:, j, :], x[:, j, :], mean_var[:, j, 0:1], rstd[:, j:j + 1],
                                                   ALU.subtract, ALU.mult)
                    if done is not None and j % T == T - 1:
                        last.then_inc(done, 1)
                return last

            def gates(n, v, times):
                cols = bass.ds(n * 4, 4)
                dve.wait_ge(w_loaded[v], times * LOADED)
                dve.sem_inc(gate["dve"], 1)
                nc.vector.tensor_tensor(w2g[:, :, :], w2[v][:, :, 0:D], spread(t["gate_cols"][:, cols], D), ALU.mult)
                link(nc.vector.tensor_tensor(b2g[:, :], b2[v][:, :], t["gate_cols"][0:D, cols], ALU.mult))
                nc.vector.tensor_tensor(bias[:, :], b2g[:, 0:4:2], b2g[:, 1:4:2], ALU.add).then_inc(w2_gated, 1)

            def turn(n, v=None, times=None):
                dve.wait_ge(y_ps, n + 3)
                dve.sem_inc(gate["dve"], 1)
                nc.vector.tensor_tensor(r[:, :, :], ps_y[:, :, :], t["normed"][:, bass.ds(n * TILES, TILES), :], ALU.add) \
                    .then_inc(r_ready, 1)
                dve.wait_ge(r_ready, n + 2)
                dve.sem_inc(gate["dve"], 1)
                variance(r)
                if v is not None:
                    gates(n + 1, v, times)
                link(normalise(y, r, n * 4))
                link(nc.vector.tensor_tensor(y[:, :, :], y[:, :, :], t["gamma"][:, :, :], ALU.mult))
                dve.wait_ge(beta_added, n + 1)
                dve.sem_inc(gate["dve"], 1)
                dve.wait_ge(h_saved, n + 1)
                nc.vector.tensor_tensor(h[:, :, :], y[:, :, :], hidden_beta[:, :, :], ALU.add).then_inc(h_ready, 1)
                dve.wait_ge(h_ready, n + 1)
                dve.sem_inc(gate["dve"], 1)
                variance(h)
                dve.wait_ge(x3T_ps, n * 2 + 1)
                dve.sem_inc(gate["dve"], 1)
                normalise(x3, h, n * 4 + 2, x3_ready)
                dve.sem_clear(chain)
                count[0] = 0

            for v in range(2):
                nc.vector.memset(w1[v][D:P, :, :], 0.0).then_inc(cleared, 1)
            dve.sem_inc(r_ready, 1)
            gates(0, 0, 1)
            dve.sem_clear(chain)
            count[0] = 0
            with dve.Fori(0, PAIRS // 2 - 1) as i:
                turn(i * 2, 1, i + 1)
                turn(i * 2 + 1, 0, i + 2)
            turn(PAIRS - 2, 1, PAIRS // 2)
            turn(PAIRS - 1)

        @block.gpsimd
        def _(pool):
            def reciprocal_roots(before):
                for u in range(2):
                    tiles = slice(u * T, (u + 1) * T)
                    pool.wait_ge(var_ready, before + u + 1)
                    nc.gpsimd.tensor_tensor(rstd[:, tiles], var_eps[:, tiles], t["minus_half"][:, :], ALU.pow) \
                        .then_inc(rstd_ready, 1)

            pool.sem_inc(h_saved, 1)
            with pool.Fori(0, PAIRS) as n:
                hidden = t["hidden"][:, bass.ds(n * TILES, TILES), :]
                nc.gpsimd.tensor_tensor(hidden_beta[:, :, :], hidden, t["beta"][:, :, :], ALU.add).then_inc(beta_added, 1)
                reciprocal_roots(n * 4)
                reciprocal_roots(n * 4 + 2)
                pool.wait_ge(h_ready, n + 1)
                pool.sem_inc(gate["pool"], 1)
                nc.gpsimd.tensor_copy(hidden, h[:, :, :]).then_inc(h_saved, 1)


def attention1(nc, t):
    with phase(nc) as (ctx, take):
        def sb(name, shape, dt=F32):
            return ctx.enter_context(nc.sbuf_tensor("c_" + name, shape, dt))

        def sb2(name, shape, dt=F32):
            return [sb(f"{name}{u}", shape, dt) for u in range(2)]

        def ps(name, width):
            return ctx.enter_context(nc.psum_tensor("c_" + name, [P, width], F32))

        def sem(name):
            return take(nc.alloc_semaphore("c_" + name))

        w_qk = sb2("w_qk", [D + 1, 2 * HD])
        w_vm = sb("w_vm", [D + 1, 2, VM])
        x_in = sb2("x_in", [D + 1, S])
        qT, kT = sb2("qT", [P, S]), sb2("kT", [P, S])
        vals = sb2("vals", [P, T + 1, HV])
        scores = sb2("scores", [P, T, SK])
        left = sb2("left", [P, SK])
        largest = sb("largest", [P, T, TOPK])
        shift = sb("shift", [P, T, 2])
        factors = sb("factors", [P, 2])
        masked = sb2("masked", [P, SK])
        expT = sb2("expT", [P, T + 1, P])
        oT = sb("oT", [HV, S])
        ps_s = [ps(f"ps_s{k}", S) for k in range(2)]
        ps_t = [ps(f"ps_t{k}", 2 * S) for k in range(2)]
        ps_o = ps("ps_o", S)
        ps_v = ps("ps_v", S)

        def vm(u, lo, hi):
            return ps_v[:, OW:OW + T * 2 * VM].rearrange("p (j w) -> p j w", j=T)[:, :, u * VM + lo:u * VM + hi]

        cleared, made = sem("cleared"), sem("made")
        staged = [sem(f"staged{u}") for u in range(2)]
        mem_staged = [sem(f"mem_staged{u}") for u in range(2)]
        s_ps, s_copied, v_ps, v_copied = sem("s_ps"), sem("s_copied"), sem("v_ps"), sem("v_copied")
        values_ps, memory_copied = sem("values_ps"), sem("memory_copied")
        s_ready, found, shifts, dropped = sem("s_ready"), sem("found"), sem("shifts"), sem("dropped")
        subtracted, exps, expT_ps, expT_copied = sem("subtracted"), sem("exps"), sem("expT_ps"), sem("expT_copied")
        pv_done, o_copied = sem("pv_done"), sem("o_copied")
        chain = sem("chain")
        gate = {e: sem(f"gate_{e}") for e in ("pool", "act", "dve", "pe")}
        in_loop = NH - 4
        block = ctx.enter_context(nc.Block())
        STAGED = (48, 32)
        RING = T + 1
        O_CREDIT, S_CREDIT = 2 * T, 2 * RING

        @block.sync
        def _(sp):
            with sp.Fori(0, B) as b:
                with sp.Fori(0, H // 2) as g:
                    for u in range(2):
                        sp.wait_ge(s_copied, (b * H + g * 2) * RING + (u + 1) * RING)
                        sp.dma_start(w_qk[u][:, :], t["w_qk"][:, bass.ds(g * 2 + u, 1), :].rearrange("p h c -> p (h c)")) \
                            .then_inc(staged[u], 16)
                        sp.dma_start(x_in[u][0:D, :], t["normedT"][0:D, bass.ds(b * S, S)]).then_inc(staged[u], 16)
                        if u == 0:
                            sp.dma_start(w_vm[:, :, :], t["w_vm"][:, bass.ds(g * 2, 2), :]).then_inc(staged[u], 16)
                        sp.wait_ge(pv_done, (b * H + g * 2) * T + (u + 1) * T)
                        sp.dma_start(vals[u][0:M, T, 0:HD],
                                     t["mem_v"][:, bass.ds(g * 2 + u, 1), :].rearrange("p h c -> p (h c)")) \
                            .then_inc(mem_staged[u], 16)

        @block.tensor
        def _(pe):
            def project(n, u, turns):
                pe.wait_ge(staged[u], turns * STAGED[u])
                pe.wait_ge(s_copied, n * RING - 1 + S_CREDIT)
                nc.tensor.matmul(ps_s[u][0:2 * HD, :], w_qk[u][:, :], x_in[u][:, :], start=True, stop=True) \
                    .then_inc(s_ps, 1)

            def project_values():
                for j in range(T):
                    last = nc.tensor.matmul(ps_v[:, OW + j * 2 * VM:OW + (j + 1) * 2 * VM], x_in[0][:, j * P:(j + 1) * P],
                                            w_vm[:, :, :].rearrange("p h c -> p (h c)"), start=True, stop=True)
                last.then_inc(values_ps, 1)

            def score(n, u, j):
                pe.wait_ge(s_copied, n * RING + max(j, 1) + S_CREDIT)
                nc.tensor.matmul(ps_s[(u + j + 1) % 2][:, :], qT[u][:, j * P:(j + 1) * P], kT[u][:, :],
                                 start=True, stop=True).then_inc(s_ps, 1)

            def turn_over(n, j):
                pe.wait_ge(exps, n * T + j + 1)
                for c in range(T):
                    nc.tensor.transpose(ps_t[j % 2][:, c * P:(c + 1) * P], masked[j % 2][:, c * P:(c + 1) * P],
                                        t["ident"][:, :])
                nc.tensor.transpose(ps_t[j % 2][0:M, S:S + P], masked[j % 2][:, S:SK], t["ident"][:, :]) \
                    .then_inc(expT_ps, 1)

            def apply(n, u, j, turns=None):
                pe.wait_ge(expT_copied, n * T + j + 1)
                if j == 0:
                    pe.wait_ge(v_copied, n + 1)
                    pe.wait_ge(mem_staged[u], turns * 16)
                for c in range(T + 1):
                    last = nc.tensor.matmul(ps_o[0:HV, j * P:(j + 1) * P], vals[u][:, c, :], expT[j % 2][:, c, :],
                                            start=(c == 0), stop=(c == T))
                last.then_inc(pv_done, 1)

            def queries_first(n):
                pe.wait_ge(o_copied, n + 1)
                pe.sem_inc(gate["pe"], 1)
                for j in range(T):
                    last = nc.tensor.transpose(ps_v[:, j * HV:(j + 1) * HV], oT[:, j * P:(j + 1) * P],
                                               t["ident"][0:HV, 0:HV])
                return last

            def head(n, u, turns, turns_ahead=None, first=False, last=False):
                if not last:
                    score(n + 1, 1 - u, 0)
                if not first:
                    apply(n - 1, 1 - u, T - 1)
                if not last:
                    score(n + 1, 1 - u, 1)
                pe.wait_ge(v_copied, n + 1)
                if not last:
                    pe.wait_ge(memory_copied, n + 2)
                if not first:
                    queries_first(n - 1).then_inc(v_ps, 1)
                else:
                    pe.sem_inc(v_ps, 1)
                turn_over(n, 0)
                for j in range(1, T):
                    if not last and j + 1 < T:
                        score(n + 1, 1 - u, j + 1)
                    if turns_ahead is not None and j + 1 == T:
                        project(n + 2, u, turns_ahead)
                        if u == 0:
                            pe.wait_ge(v_copied, n + 2)
                            project_values()
                    apply(n, u, j - 1, turns)
                    turn_over(n, j)

            pe.wait_ge(made, 1)
            pe.sem_inc(pv_done, O_CREDIT)
            project(0, 0, 1)
            project_values()
            pe.sem_inc(v_ps, 1)
            for j in range(T):
                score(0, 0, j)
            project(1, 1, 1)
            head(0, 0, 1, 2, first=True)
            with pe.Fori(0, in_loop // 2) as i:
                head(i * 2 + 1, 1, i + 1, i + 2)
                head(i * 2 + 2, 0, i + 2, i + 3)
            head(NH - 3, 1, NH // 2 - 1, NH // 2)
            head(NH - 2, 0, NH // 2)
            head(NH - 1, 1, NH // 2, last=True)
            apply(NH - 1, 1, T - 1)
            queries_first(NH - 1).then_inc(v_ps, 1)

        @block.scalar
        def _(act):
            def copy_qk(n, u):
                act.wait_ge(s_ps, n * RING + 1)
                nc.scalar.activation(qT[u][0:HD, :], ps_s[u][0:HD, :], ACT.Copy)
                nc.scalar.activation(kT[u][0:HD, :], ps_s[u][HD:2 * HD, :], ACT.Copy).then_inc(s_copied, 1)

            def copy_outputs(n):
                act.wait_ge(pv_done, n * T + T + O_CREDIT)
                nc.scalar.activation(oT[:, :], ps_o[0:HV, :], ACT.Copy).then_inc(o_copied, 1)

            def copy_values(n, u, outputs=True, values=True):
                act.wait_ge(v_ps, n + 1)
                if outputs:
                    act.sem_inc(gate["act"], 1)
                    last = nc.scalar.activation(t["heads"][:, bass.ds(n * OW - 2 * OW, OW)], ps_v[:, 0:OW], ACT.Copy)
                if values:
                    last = nc.scalar.activation(vals[u][:, 0:T, 0:HD], vm(u, 0, HD), ACT.Copy)
                last.then_inc(v_copied, 1)

            def copy_memory(u, pairs):
                act.wait_ge(values_ps, pairs)
                nc.scalar.activation(scores[u][:, :, S:SK], vm(u, HD, VM), ACT.Copy).then_inc(memory_copied, 1)

            def copy_scores(n, u, j):
                act.wait_ge(s_ps, n * RING + j + 2)
                nc.scalar.activation(scores[u][:, j, 0:S], ps_s[(u + j + 1) % 2][:, :], ACT.Copy).then_inc(s_copied, 1)

            def drop(n, u, j):
                act.wait_ge(shifts, n * T + j + 1)
                nc.scalar.activation(masked[j % 2][:, :], scores[u][:, j, :], ACT.Relu, scale=-STEEP,
                                     bias=shift[:, j, 1:2]).then_inc(dropped, 1)

            def exponent(n, j):
                act.wait_ge(subtracted, n * T + j + 1)
                nc.scalar.activation(masked[j % 2][:, :], masked[j % 2][:, :], ACT.Exp, bias=shift[:, j, 0:1]) \
                    .then_inc(exps, 1)

            def copy_expT(n, j):
                act.wait_ge(expT_ps, n * T + j + 1)
                nc.scalar.activation(expT[j % 2][:, :, :], ps_t[j % 2][:, 0:(T + 1) * P].rearrange("p (c q) -> p c q", c=T + 1),
                                     ACT.Copy).then_inc(expT_copied, 1)

            def head(n, u, pairs=None, first=False, ahead=True, last=False):
                if not first:
                    copy_expT(n - 1, T - 1)
                if not last:
                    copy_memory(1 - u, pairs)
                drop(n, u, 0)
                if not last:
                    copy_scores(n + 1, 1 - u, 0)
                if not first:
                    copy_outputs(n - 1)
                exponent(n, 0)
                copy_values(n + 1, 1 - u, outputs=not first, values=not last)
                for j in range(1, T):
                    copy_expT(n, j - 1)
                    drop(n, u, j)
                    if not last:
                        copy_scores(n + 1, 1 - u, j)
                    exponent(n, j)
                if ahead:
                    copy_qk(n + 2, u)

            act.wait_ge(made, 1)
            act.sem_inc(s_copied, S_CREDIT)
            copy_qk(0, 0)
            copy_memory(0, 1)
            copy_values(0, 0, outputs=False)
            for j in range(T):
                copy_scores(0, 0, j)
            copy_qk(1, 1)
            head(0, 0, 1, first=True)
            with act.Fori(0, in_loop // 2) as i:
                head(i * 2 + 1, 1, i + 2)
                head(i * 2 + 2, 0, i + 2)
            head(NH - 3, 1, NH // 2)
            head(NH - 2, 0, NH // 2, ahead=False)
            head(NH - 1, 1, ahead=False, last=True)
            copy_expT(NH - 1, T - 1)
            copy_outputs(NH - 1)
            copy_values(NH + 1, 1, values=False)
            act.wait_ge(v_copied, NH + 2)

        @block.gpsimd
        def _(pool):
            def exclude_self(n, u, j):
                own = scores[u][:, j, j * P:(j + 1) * P]
                pool.wait_ge(s_copied, n * RING + j + 2 + S_CREDIT)
                pool.sem_inc(gate["pool"], 1)
                nc.gpsimd.affine_select(out=own, in_=own, compare_op=ALU.not_equal, fill=FILL, base=0,
                                        pattern=[[-1, P]], channel_multiplier=1).then_inc(s_ready, 1)

            def head(n, u, last=False):
                for j in range(T):
                    pool.wait_ge(found, n * T + j + 1)
                    nc.gpsimd.tensor_tensor(shift[:, j, :], largest[:, j, 0:TOPK:TOPK - 1], factors[:, :], ALU.mult) \
                        .then_inc(shifts, 1)
                    pool.wait_ge(dropped, n * T + j + 1)
                    nc.gpsimd.tensor_tensor(masked[j % 2][:, :], scores[u][:, j, :], masked[j % 2][:, :], ALU.subtract) \
                        .then_inc(subtracted, 1)
                    if not last:
                        exclude_self(n + 1, 1 - u, j)

            nc.gpsimd.memset(factors[:, 0:1], -1.0)
            nc.gpsimd.memset(factors[:, 1:2], STEEP).then_inc(gate["pool"], 1)
            pool.wait_ge(gate["pool"], 1)
            for j in range(T):
                exclude_self(0, 0, j)
            head(0, 0)
            with pool.Fori(0, in_loop // 2) as i:
                head(i * 2 + 1, 1)
                head(i * 2 + 2, 0)
            head(NH - 3, 1)
            head(NH - 2, 0)
            head(NH - 1, 1, last=True)

        @block.vector
        def _(dve):
            count, done = [0], [0, 0]
            PASSES = 2 * (TOPK // 8) - 1

            def step(n, u, j, k):
                if k == 0:
                    if j == 0:
                        dve.wait_ge(memory_copied, n + 1)
                        dve.sem_inc(gate["dve"], 1)
                    dve.wait_ge(s_ready, n * T + j + 1)
                    dve.sem_inc(gate["dve"], 1)
                elif done[j % 2]:
                    dve.wait_ge(chain, done[j % 2])
                eight = largest[:, j, k // 2 * 8:k // 2 * 8 + 8]
                source = left[j % 2][:, :] if k >= 2 else scores[u][:, j, :]
                if k % 2:
                    done_pass = nc.vector.match_replace(left[j % 2][:, :], eight, source, REMOVED)
                else:
                    done_pass = nc.vector.max(eight, source)
                if k == PASSES - 1:
                    done_pass.then_inc(found, 1)
                else:
                    done_pass.then_inc(chain, 1)
                    count[0] += 1
                    done[j % 2] = count[0]

            def head(n, u, first=False):
                for k in range(T // 2 * PASSES):
                    step(n, u, k // PASSES * 2, k % PASSES)
                    behind = k - PASSES // 2
                    if behind >= 0:
                        step(n, u, behind // PASSES * 2 + 1, behind % PASSES)
                    elif not first:
                        step(None, 1 - u, T - 1, behind + PASSES)

            def restart():
                dve.wait_ge(chain, done[1])
                dve.sem_clear(chain)
                count[0], done[0], done[1] = 0, 0, 0

            for u in range(2):
                nc.vector.memset(x_in[u][D:D + 1, :], 1.0)
                nc.vector.memset(vals[u][:, :, :], 0.0)
                nc.vector.memset(qT[u][:, :], 0.0)
                nc.vector.memset(kT[u][:, :], 0.0)
                nc.vector.memset(ps_t[u][:, S:S + P], 0.0).then_inc(cleared, 1)
            dve.wait_ge(cleared, 2)
            for u in range(2):
                last = nc.vector.memset(vals[u][:, 0:T, HD:HV], 1.0)
                last = nc.vector.memset(vals[u][0:M, T, HD:HV], 1.0)
            last.then_inc(made, 1)
            dve.wait_ge(made, 1)
            head(0, 0, first=True)
            restart()
            with dve.Fori(0, in_loop // 4) as i:
                for n in range(1, 5):
                    head(i * 4 + n, n % 2)
                restart()
            head(NH - 3, 1)
            head(NH - 2, 0)
            head(NH - 1, 1)
            for k in range(PASSES - PASSES // 2, PASSES):
                step(None, 1, T - 1, k)


def routed_ffn(nc, a, t, out):
    with phase(nc) as (ctx, take):
        TILES = 2 * T

        def sb(name, shape):
            return ctx.enter_context(nc.sbuf_tensor("d_" + name, shape, F32))

        def ps(name, shape):
            return ctx.enter_context(nc.psum_tensor("d_" + name, shape, F32))

        def sem(name):
            return take(nc.alloc_semaphore("d_" + name))

        w_routed = [sb(f"w_routed{v}", [P, TILES, 2, HID + 1]) for v in range(2)]
        inv = sb("inv", [P, 2 * H, T])
        attended = sb("attended", [P, TILES, H * HD])
        attendedT = [sb(f"attendedT{u}", [P, 2, S]) for u in range(2)]
        h, xn, result = (sb(name, [P, TILES, D]) for name in ("h", "xn", "result"))
        stats, mean_var = sb("stats", [P, TILES, 6]), sb("mean_var", [P, TILES, 2])
        var_eps, rstd = sb("var_eps", [P, TILES]), sb("rstd", [P, TILES])
        xT = [sb(f"xT{u}", [P, S]) for u in range(2)]
        yT, outT = ([sb(f"{name}{u}", [D, S]) for u in range(2)] for name in ("yT", "outT"))
        g = [[sb(f"g{l}_{u}", [HID, S]) for u in range(2)] for l in range(3)]
        ps_a = [ps(f"ps_a{u}", [P, 2 * S]) for u in range(2)]
        ps_g = [ps(f"ps_g{u}", [P, S]) for u in range(2)]
        ps_y, ps_out = ps("ps_y", [P, TILES, D]), ps("ps_out", [P, TILES, D])
        w_loaded = [sem(f"w_loaded{v}") for v in range(2)]
        w_ready, attended_ready, aT_ps, aT_sb = sem("w_ready"), sem("attended_ready"), sem("aT_ps"), sem("aT_sb")
        y_ps, h_added, h_saved = sem("y_ps"), sem("h_added"), sem("h_saved")
        var_ready, rstd_ready, xn_ready, xT_ps, xT_sb = (sem("var_ready"), sem("rstd_ready"), sem("xn_ready"),
                                                         sem("xT_ps"), sem("xT_sb"))
        g_ps, g_sb, out_ps, result_ready, stored = sem("g_ps"), sem("g_sb"), sem("out_ps"), sem("result_ready"), sem("stored")
        yT_ps, yT_sb, outT_ps, outT_sb = sem("yT_ps"), sem("yT_sb"), sem("outT_ps"), sem("outT_sb")
        cleared, chain = sem("cleared"), sem("chain")
        gate = {e: sem(f"gate_{e}") for e in ("pool", "act", "dve", "pe")}
        block = ctx.enter_context(nc.Block())
        LOADED = TILES * 16

        @block.sync
        def _(sp):
            def load(n, v):
                for j in range(TILES):
                    route = sp.value_load(t["route_row"][0:1, bass.ds(n * TILES + j, 1)], min_val=0, max_val=R - 1)
                    sp.dma_start(w_routed[v][:, j, :, :].rearrange("p l c -> p (l c)"),
                                 a["w_routed"][bass.ds(route, 1), :, :].rearrange("r p c -> (r p) c")) \
                        .then_inc(w_loaded[v], 16)

            def store(n):
                sp.wait_ge(result_ready, n + 2)
                sp.dma_start(out[bass.ds(n * 2, 2), :, :].rearrange("b (j p) d -> p (b j) d", p=P),
                             result[:, :, :]).then_inc(stored, 16)

            load(0, 0)
            load(1, 1)
            sp.sem_inc(stored, 16)
            with sp.Fori(0, PAIRS // 2 - 1) as i:
                for v in range(2):
                    store(i * 2 + v)
                    load(i * 2 + v + 2, v)
            store(PAIRS - 2)
            store(PAIRS - 1)
            sp.wait_ge(stored, 16 * (PAIRS + 1))

        @block.gpsimd
        def _(pool):
            def add_shared(v, times):
                pool.wait_ge(w_loaded[v], times * LOADED)
                for j in range(TILES):
                    last = nc.gpsimd.tensor_tensor(w_routed[v][:, j, :, :], w_routed[v][:, j, :, :],
                                                   t["w_shared"][:, :, :], ALU.add)
                last.then_inc(w_ready, 1)

            def front(n):
                for u in range(2):
                    tiles = slice(u * T, (u + 1) * T)
                    pool.wait_ge(var_ready, n * 2 + u + 1)
                    nc.gpsimd.tensor_tensor(rstd[:, tiles], var_eps[:, tiles], t["minus_half"][:, :], ALU.pow) \
                        .then_inc(rstd_ready, 1)
                pool.wait_ge(h_added, n + 1)
                pool.sem_inc(gate["pool"], 1)
                nc.gpsimd.tensor_copy(t["hidden"][:, bass.ds(n * TILES, TILES), :], h[:, :, :]).then_inc(h_saved, 1)

            pool.sem_inc(h_saved, 1)
            front(0)
            add_shared(0, 1)
            with pool.Fori(0, PAIRS // 2 - 1) as i:
                front(i * 2 + 1)
                add_shared(1, i + 1)
                front(i * 2 + 2)
                add_shared(0, i + 2)
            front(PAIRS - 1)
            add_shared(1, PAIRS // 2)

        @block.vector
        def _(dve):
            count = [0]

            def link(ins):
                count[0] += 1
                ins.then_inc(chain, 1)
                dve.wait_ge(chain, count[0])

            def attend(n):
                ours = t["heads"][:, bass.ds(n * (2 * H * OW), 2 * H * OW)].rearrange("p (h j c) -> p h j c", h=2 * H, j=T)
                link(nc.vector.reciprocal(inv[:, :, :], ours[:, :, :, HD]))
                for u in range(2):
                    heads = slice(u * H, (u + 1) * H)
                    for j in range(T):
                        last = nc.vector.tensor_tensor(attended[:, u * T + j, :].rearrange("p (h c) -> p h c", h=H),
                                                       ours[:, heads, j, 0:HD], spread(inv[:, heads, j], HD), ALU.mult)
                    last.then_inc(attended_ready, 1)

            def norm(n):
                dve.wait_ge(h_saved, n + 1)
                dve.sem_inc(gate["dve"], 1)
                dve.wait_ge(y_ps, n + 1)
                dve.sem_inc(gate["dve"], 1)
                nc.vector.tensor_tensor(h[:, :, :], ps_y[:, :, :], t["hidden"][:, bass.ds(n * TILES, TILES), :], ALU.add) \
                    .then_inc(h_added, 1)
                dve.wait_ge(h_added, n + 1)
                dve.sem_inc(gate["dve"], 1)
                for u in range(2):
                    tiles = range(u * T, (u + 1) * T)
                    for j in tiles:
                        last = nc.vector.bn_stats(stats[:, j, :], h[:, j, :])
                    link(last)
                    for j in tiles:
                        last = nc.vector.bn_aggr(mean_var[:, j, :], stats[:, j, :])
                    link(last)
                    nc.vector.tensor_scalar(var_eps[:, u * T:(u + 1) * T], mean_var[:, u * T:(u + 1) * T, 1], EPS, None,
                                            ALU.add).then_inc(var_ready, 1)

            def normalise(n):
                for j in range(TILES):
                    if j % T == 0:
                        dve.wait_ge(rstd_ready, n * 2 + j // T + 1)
                    last = nc.vector.tensor_scalar(xn[:, j, :], h[:, j, :], mean_var[:, j, 0:1], rstd[:, j:j + 1],
                                                   ALU.subtract, ALU.mult)
                    if j % T == T - 1:
                        last.then_inc(xn_ready, 1)

            def finish(n):
                dve.wait_ge(stored, n * 16 + 16)
                dve.sem_inc(gate["dve"], 1)
                dve.wait_ge(h_saved, n + 2)
                dve.sem_inc(gate["dve"], 1)
                dve.wait_ge(out_ps, n + 1)
                dve.sem_inc(gate["dve"], 1)
                nc.vector.tensor_tensor(result[:, :, :], ps_out[:, :, :], t["hidden"][:, bass.ds(n * TILES, TILES), :],
                                        ALU.add).then_inc(result_ready, 1)
                dve.sem_clear(chain)
                count[0] = 0

            for u in range(2):
                nc.vector.memset(xT[u][D:P, :], 0.0).then_inc(cleared, 1)
            dve.sem_inc(result_ready, 1)
            attend(0)
            norm(0)
            normalise(0)
            dve.sem_clear(chain)
            count[0] = 0
            with dve.Fori(0, PAIRS - 1) as n:
                attend(n + 1)
                norm(n + 1)
                normalise(n + 1)
                finish(n)
            finish(PAIRS - 1)

        @block.tensor
        def _(pe):
            def tokens_first(dst, u, x):
                for j in range(T):
                    last = nc.tensor.transpose(dst[:, u * T + j, :], x[:, j * P:(j + 1) * P], t["ident"][0:D, 0:D])
                return last

            def turn_over(n):
                for u in range(2):
                    pe.wait_ge(attended_ready, n * 2 + u + 1)
                    for c in range(2):
                        for j in range(T):
                            last = nc.tensor.transpose(ps_a[u][:, c * S + j * P:c * S + (j + 1) * P],
                                                       attended[:, u * T + j, c * P:(c + 1) * P], t["ident"][:, :])
                    last.then_inc(aT_ps, 1)

            def project(n):
                for u in range(2):
                    pe.wait_ge(aT_sb, n * 2 + u + 1)
                    for c in range(2):
                        last = nc.tensor.matmul(ps_a[u][0:D, 0:S], t["w_proj"][:, c, :], attendedT[u][:, c, :],
                                                start=(c == 0), stop=(c == 1))
                    last.then_inc(yT_ps, 1)

            def projected(n):
                for u in range(2):
                    pe.wait_ge(yT_sb, n * 2 + u + 1)
                    pe.sem_inc(gate["pe"], 1)
                    last = tokens_first(ps_y, u, yT[u])
                last.then_inc(y_ps, 1)

            def to_features(n):
                for u in range(2):
                    pe.wait_ge(xn_ready, n * 2 + u + 1)
                    pe.sem_inc(gate["pe"], 1)
                    for j in range(T):
                        last = nc.tensor.transpose(ps_a[u][0:D, j * P:(j + 1) * P], xn[:, u * T + j, :], t["ident"][:, :])
                    last.then_inc(xT_ps, 1)

            def first(n):
                for u in range(2):
                    pe.wait_ge(xT_sb, n * 2 + u + 1)
                    nc.tensor.matmul(ps_g[u][:, :], t["w_inT"][:, :], xT[u][:, :], start=True, stop=True) \
                        .then_inc(g_ps, 1)

            def layer(n, l, v):
                if l == 0:
                    pe.wait_ge(w_ready, n + 1)
                    pe.sem_inc(gate["pe"], 1)
                for u in range(2):
                    pe.wait_ge(g_sb, n * 6 + 2 * l + u + 1)
                    for j in range(T):
                        last = nc.tensor.matmul(ps_g[u][:, j * P:(j + 1) * P], w_routed[v][:, u * T + j, l, 0:HID],
                                                g[l][u][:, j * P:(j + 1) * P], start=True, stop=True)
                    last.then_inc(g_ps, 1)

            def finish(n):
                for u in range(2):
                    pe.wait_ge(g_sb, n * 6 + 4 + u + 1)
                    nc.tensor.matmul(ps_g[u][0:D, :], t["w_outT"][:, :], g[2][u][:, :], start=True, stop=True) \
                        .then_inc(outT_ps, 1)
                pe.wait_ge(result_ready, n + 1)
                for u in range(2):
                    pe.wait_ge(outT_sb, n * 2 + u + 1)
                    pe.sem_inc(gate["pe"], 1)
                    last = tokens_first(ps_out, u, outT[u])
                last.then_inc(out_ps, 1)

            def turn(n, v, ahead=True):
                first(n)
                if ahead:
                    turn_over(n + 1)
                    project(n + 1)
                layer(n, 0, v)
                if ahead:
                    projected(n + 1)
                layer(n, 1, v)
                finish(n)
                if ahead:
                    to_features(n + 1)

            pe.wait_ge(cleared, 2)
            turn_over(0)
            project(0)
            projected(0)
            to_features(0)
            with pe.Fori(0, PAIRS // 2 - 1) as i:
                turn(i * 2, 0)
                turn(i * 2 + 1, 1)
            turn(PAIRS - 2, 0)
            turn(PAIRS - 1, 1, ahead=False)

        @block.scalar
        def _(act):
            def copy_attendedT(n):
                for u in range(2):
                    act.wait_ge(aT_ps, n * 2 + u + 1)
                    nc.scalar.activation(attendedT[u][:, :, :], ps_a[u][:, :].rearrange("p (c q) -> p c q", c=2),
                                         ACT.Copy).then_inc(aT_sb, 1)

            def copy_yT(n):
                for u in range(2):
                    act.wait_ge(yT_ps, n * 2 + u + 1)
                    nc.scalar.activation(yT[u][:, :], ps_a[u][0:D, 0:S], ACT.Identity, bias=t["b_proj"][:, :]) \
                        .then_inc(yT_sb, 1)

            def copy_outT(n):
                for u in range(2):
                    act.wait_ge(outT_ps, n * 2 + u + 1)
                    nc.scalar.activation(outT[u][:, :], ps_g[u][0:D, :], ACT.Identity, bias=t["b_out"][:, :]) \
                        .then_inc(outT_sb, 1)

            def copy_xT(n):
                for u in range(2):
                    act.wait_ge(xT_ps, n * 2 + u + 1)
                    nc.scalar.activation(xT[u][0:D, :], ps_a[u][0:D, 0:S], ACT.Copy).then_inc(xT_sb, 1)

            def first(n):
                for u in range(2):
                    act.wait_ge(g_ps, n * 6 + u + 1)
                    nc.scalar.activation(g[0][u][:, :], ps_g[u][:, :], ACT.Relu, bias=t["b_in"][:, :]).then_inc(g_sb, 1)

            def layer(n, l, v):
                for u in range(2):
                    act.wait_ge(g_ps, n * 6 + 2 * l + u + 3)
                    for j in range(T):
                        last = nc.scalar.activation(g[l + 1][u][:, j * P:(j + 1) * P], ps_g[u][:, j * P:(j + 1) * P],
                                                    ACT.Relu, bias=w_routed[v][:, u * T + j, l, HID:HID + 1])
                    last.then_inc(g_sb, 1)

            def turn(n, v, ahead=True):
                first(n)
                if ahead:
                    copy_attendedT(n + 1)
                    copy_yT(n + 1)
                layer(n, 0, v)
                layer(n, 1, v)
                copy_outT(n)
                if ahead:
                    copy_xT(n + 1)

            copy_attendedT(0)
            copy_yT(0)
            copy_xT(0)
            with act.Fori(0, PAIRS // 2 - 1) as i:
                turn(i * 2, 0)
                turn(i * 2 + 1, 1)
            turn(PAIRS - 2, 0)
            turn(PAIRS - 1, 1, ahead=False)


def kernel(**inputs):
    import numpy as np
    import concourse.bacc as bacc
    from concourse.bass_utils import run_bass_kernel_spmd as run

    v = {name: np.asarray(x) for name, x in inputs.items()}
    row = lambda x: x.reshape(1, -1)
    zeros_below = lambda x: np.pad(x, ((0, P - D), (0, 0)))
    w_heads = np.concatenate([v["L1_attn_w_qkv"], row(v["L1_attn_b_qkv"])]).reshape(D + 1, 3, H, HD) \
        .transpose(0, 2, 1, 3).reshape(D + 1, H, 3 * HD)
    w_routed = np.concatenate([v["L1_ffn_Wr"].transpose(1, 3, 0, 2), v["L1_ffn_br"].transpose(1, 2, 0)[..., None]], axis=3)
    arrays = {
        "token_ids": v["x"].reshape(NT, P).T,
        "table": v["L0_tok_W"].T,
        "L0_attn_Wq": v["L0_attn_Wq"],
        "L0_attn_Wk": v["L0_attn_Wk"],
        "wv0T": zeros_below(v["L0_attn_Wv"].T),
        "L0_ffn_Wr": v["L0_ffn_Wr"],
        "L0_ffn_br": row(v["L0_ffn_br"]),
        "L0_ffn_W1": v["L0_ffn_W1"],
        "w2_b1": np.concatenate([v["L0_ffn_W2"], v["L0_ffn_b1"][..., None]], axis=2),
        "b2": v["L0_ffn_b2"][..., None],
        "gammas": np.tile(v["L0_ffn_gamma"], 2 * T),
        "betas": np.tile(v["L0_ffn_beta"], 2 * T),
        "w_qk": w_heads[:, :, 0:2 * HD],
        "w_v": w_heads[:, :, 2 * HD:],
        "w_qT": w_heads[:, :, 0:HD].transpose(2, 1, 0),
        "L1_attn_scale": v["L1_attn_scale"].reshape(-1),
        "mem_kT": v["L1_attn_mem_k"].transpose(2, 0, 1),
        "mem_v": v["L1_attn_mem_v"].transpose(1, 0, 2),
        "w_proj": v["L1_attn_w_proj"].reshape(2, P, D).transpose(1, 0, 2),
        "L1_attn_b_proj": v["L1_attn_b_proj"].reshape(-1, 1),
        "w_inT": zeros_below(v["L1_ffn_Wi"].T),
        "b_in": v["L1_ffn_bi"].reshape(-1, 1),
        "w_routed": w_routed.reshape(R, HID, 2 * (HID + 1)),
        "w_shared": np.concatenate([v["L1_ffn_Ws"].reshape(2, HID, HID).transpose(2, 0, 1),
                                    v["L1_ffn_bs"].reshape(2, HID).T[..., None]], axis=2),
        "w_outT": v["L1_ffn_Wo"].T,
        "L1_ffn_bo": v["L1_ffn_bo"].reshape(-1, 1),
        "L1_ffn_route_id": row(v["L1_ffn_route_id"]),
    }
    nc = bacc.Bacc("TRN2", target_bir_lowering=False, num_devices=1)
    feed, aps = {}, {}
    for name, x in arrays.items():
        feed["in_" + name] = np.ascontiguousarray(x)
        aps[name] = nc.dram_tensor("in_" + name, x.shape, mybir.dt.from_np(x.dtype), kind="ExternalInput").ap()
    out = nc.dram_tensor("out", (B, S, D), F32, kind="ExternalOutput").ap()
    tower(nc, aps, out)
    return run(nc, [feed], core_ids=[0]).results[0]["out"]
```
